# Optimizing a Trainium2 kernel written in Bass

```python
import numpy as np
import jax
import jax.numpy as jnp

def _softmax(x, axis=-1):
    return jax.nn.softmax(x, axis=axis)

def _gelu(x):
    return jax.nn.gelu(x, approximate=True)

def _silu(x):
    return jax.nn.silu(x)

def _sigmoid(x):
    return jax.nn.sigmoid(x)

def _layernorm(x, axis=-1, eps=1e-05):
    m = jnp.mean(x, axis=axis, keepdims=True)
    v = jnp.var(x, axis=axis, keepdims=True)
    return (x - m) / jnp.sqrt(v + eps)

def _scatter_add(tgt, idx, src, axis=0):
    return tgt.at[idx].add(src)

def _segment_sum(src, seg, n):
    return jax.ops.segment_sum(src, seg, n)
kernel_name = 'mk_cond_seq_d4_seqx_r8_cfd7d5'

def setup_inputs(seed: int=0):
    np.random.seed(seed)
    _w = jnp.asarray

    def _rec_inputs():
        import jax
        import jax.numpy as jnp
        _rk = jax.random.key(seed)
        x = 0.4999 + 0.2886 * jax.random.normal(jax.random.fold_in(_rk, 1), (16, 128, 128), jnp.float32)
        _lenS = 128 - jax.random.randint(jax.random.fold_in(_rk, 7), (16,), 0, max(1, 128 // 4) + 1, jnp.int32)
        _lenS2 = 128 - jax.random.randint(jax.random.fold_in(_rk, 8), (16,), 0, max(1, 128 // 4) + 1, jnp.int32)
        condB_dt = jax.random.uniform(jax.random.fold_in(_rk, 11), (16,), jnp.float32, 0.0, 0.981965)
        itok_B_34_63 = jax.random.randint(jax.random.fold_in(_rk, 13), (16,), 34, 64, jnp.int32)
        fside_Bx16xSxS_0 = -1.47943e-05 + 1.00017 * jax.random.normal(jax.random.fold_in(_rk, 14), (16, 16, 128, 128), jnp.float32)
        condB_gatescore = jax.random.uniform(jax.random.fold_in(_rk, 15), (16,), jnp.float32, 0.0, 0.581427)
        condB_safetyscore = -0.927215 + 0.920279 * jax.random.normal(jax.random.fold_in(_rk, 16), (16,), jnp.float32)
        _validS = jnp.arange(128)[None, :] < _lenS[:, None]
        _validS2 = jnp.arange(128)[None, :] < _lenS2[:, None]
        _causal = jnp.tril(jnp.ones((128, 128), dtype=bool))
        mask_Bx1xSxS_bk0 = jnp.logical_not(jnp.broadcast_to(_validS[:, None, None, :], (16, 1, 128, 128)))
        return (x, condB_dt, itok_B_34_63, fside_Bx16xSxS_0, condB_gatescore, condB_safetyscore, mask_Bx1xSxS_bk0)
    x, condB_dt, itok_B_34_63, fside_Bx16xSxS_0, condB_gatescore, condB_safetyscore, mask_Bx1xSxS_bk0 = _rec_inputs()

    def _L0_cond_setup():
        import jax, jax.numpy as jnp
        import numpy as np
        B, NX, NY = (16, 128, 128)

        def _grad(f, axis):
            fm = jnp.moveaxis(f, axis, -1)
            g = (jnp.roll(fm, -1, -1) - jnp.roll(fm, 1, -1)) * 0.5
            g0 = (-3.0 * fm[..., 0] + 4.0 * fm[..., 1] - fm[..., 2]) * 0.5
            gN = (3.0 * fm[..., -1] - 4.0 * fm[..., -2] + fm[..., -3]) * 0.5
            g = g.at[..., 0].set(g0).at[..., -1].set(gN)
            return jnp.moveaxis(g, -1, axis)

        def _grad2(f, axis):
            fm = jnp.moveaxis(f, axis, -1)
            g = jnp.roll(fm, -1, -1) - 2.0 * fm + jnp.roll(fm, 1, -1)
            g0 = 2.0 * fm[..., 0] - 5.0 * fm[..., 1] + 4.0 * fm[..., 2] - fm[..., 3]
            gN = 2.0 * fm[..., -1] - 5.0 * fm[..., -2] + 4.0 * fm[..., -3] - fm[..., -4]
            g = g.at[..., 0].set(g0).at[..., -1].set(gN)
            return jnp.moveaxis(g, -1, axis)
        key = jax.random.key(seed)
        k1, k2, k3, k4 = jax.random.split(key, 4)
        f = jax.random.uniform(k1, (B, NX, NY), dtype=jnp.float32)
        A_grid = jax.random.normal(k2, (2, NX, NY), dtype=jnp.float32)
        B_grid = jax.random.uniform(k3, (3, NX, NY), dtype=jnp.float32)
        dt = jax.random.uniform(k4, (B,), dtype=jnp.float32)
        return {'f': f, 'A_grid': A_grid, 'B_grid': B_grid, 'dt': dt}
    _L0_cond_all = _L0_cond_setup()
    _L0_cond_in = {k: v for k, v in _L0_cond_all.items() if k in ('A_grid', 'B_grid')}
    del _L0_cond_all

    def _L1_cond_setup():
        import jax, jax.numpy as jnp
        import numpy as np
        import math
        D_MODEL = 128
        N_HEAD = 16
        HEAD_DIM = D_MODEL // N_HEAD
        D_FF = 512
        NUM_STEPS = 100.0
        RESCALE = 4000.0
        EPS = 1e-05

        def _sin_emb(t):
            half = D_MODEL // 2
            x = t.astype(jnp.float32) / NUM_STEPS * RESCALE
            freqs = jnp.exp(jnp.arange(half, dtype=jnp.float32) * (-math.log(10000.0) / (half - 1)))
            e = x[:, None] * freqs[None, :]
            return jnp.concatenate([jnp.sin(e), jnp.cos(e)], axis=-1)

        def _ln(x):
            m = jnp.mean(x, axis=-1, keepdims=True)
            v = jnp.var(x, axis=-1, keepdims=True)
            return (x - m) / jnp.sqrt(v + EPS)

        def _gelu2(x):
            return x * jax.nn.sigmoid(1.702 * x)
        key = jax.random.key(seed)
        ks = jax.random.split(key, 24)
        B, S, D, F = (4, 64, D_MODEL, D_FF)
        std = 0.02
        inp = {'src': jax.random.normal(ks[0], (B, S, D), dtype=jnp.float32), 'src_mask': jax.random.randint(ks[1], (B, 1, S, S), 0, 2).astype(bool), 'timestep': jax.random.randint(ks[2], (B,), 0, 100, dtype=jnp.int32), 'attention_bias': jax.random.normal(ks[3], (B, N_HEAD, S, S), dtype=jnp.float32), 'W_ada': jax.random.normal(ks[4], (D, 2 * D), dtype=jnp.float32) * std, 'b_ada': jnp.zeros((2 * D,), dtype=jnp.float32), 'Wq': jax.random.normal(ks[5], (D, D), dtype=jnp.float32) * std, 'bq': jnp.zeros((D,), dtype=jnp.float32), 'Wk': jax.random.normal(ks[6], (D, D), dtype=jnp.float32) * std, 'bk': jnp.zeros((D,), dtype=jnp.float32), 'Wv': jax.random.normal(ks[7], (D, D), dtype=jnp.float32) * std, 'bv': jnp.zeros((D,), dtype=jnp.float32), 'Wo': jax.random.normal(ks[8], (D, D), dtype=jnp.float32) * std, 'bo': jnp.zeros((D,), dtype=jnp.float32), 'W1': jax.random.normal(ks[9], (D, F), dtype=jnp.float32) * std, 'b1': jnp.zeros((F,), dtype=jnp.float32), 'W2': jax.random.normal(ks[10], (F, D), dtype=jnp.float32) * std, 'b2': jnp.zeros((D,), dtype=jnp.float32), 'g2': jnp.ones((D,), dtype=jnp.float32), 'beta2': jnp.zeros((D,), dtype=jnp.float32)}
        return inp
    _L1_cond_all = _L1_cond_setup()
    _L1_cond_in = {k: v for k, v in _L1_cond_all.items() if k in ('W_ada', 'b_ada', 'Wq', 'bq', 'Wk', 'bk', 'Wv', 'bv', 'Wo', 'bo', 'W1', 'b1', 'W2', 'b2', 'g2', 'beta2')}
    del _L1_cond_all

    def _L2_cond_setup():
        import jax, jax.numpy as jnp
        import numpy as np
        D_MODEL = 128
        N_HEADS = 16
        D_HEAD = D_MODEL // N_HEADS
        D_FF = 512
        EPS = 1e-05

        def layernorm(x, gamma, beta):
            mu = jnp.mean(x, axis=-1, keepdims=True)
            var = jnp.var(x, axis=-1, keepdims=True)
            return (x - mu) * jax.lax.rsqrt(var + EPS) * gamma + beta
        key = jax.random.key(seed)
        ks = jax.random.split(key, 16)
        B, T = (4, 256)
        s = 1.0 / np.sqrt(D_MODEL)
        sf = 1.0 / np.sqrt(D_FF)
        return {'x': jax.random.normal(ks[0], (B, T, D_MODEL), jnp.float32), 'gate_score': jax.random.uniform(ks[1], (B,), jnp.float32), 'Wq': jax.random.normal(ks[2], (D_MODEL, D_MODEL), jnp.float32) * s, 'bq': jnp.zeros((D_MODEL,), jnp.float32), 'Wk': jax.random.normal(ks[3], (D_MODEL, D_MODEL), jnp.float32) * s, 'bk': jnp.zeros((D_MODEL,), jnp.float32), 'Wv': jax.random.normal(ks[4], (D_MODEL, D_MODEL), jnp.float32) * s, 'bv': jnp.zeros((D_MODEL,), jnp.float32), 'Wo': jax.random.normal(ks[5], (D_MODEL, D_MODEL), jnp.float32) * s, 'bo': jnp.zeros((D_MODEL,), jnp.float32), 'W1': jax.random.normal(ks[6], (D_MODEL, D_FF), jnp.float32) * s, 'b1': jnp.zeros((D_FF,), jnp.float32), 'W2': jax.random.normal(ks[7], (D_FF, D_MODEL), jnp.float32) * sf, 'b2': jnp.zeros((D_MODEL,), jnp.float32), 'gamma1': jnp.ones((D_MODEL,), jnp.float32), 'beta1': jnp.zeros((D_MODEL,), jnp.float32), 'gamma2': jnp.ones((D_MODEL,), jnp.float32), 'beta2': jnp.zeros((D_MODEL,), jnp.float32)}
    _L2_cond_all = _L2_cond_setup()
    _L2_cond_in = {k: v for k, v in _L2_cond_all.items() if k in ('Wq', 'bq', 'Wk', 'bk', 'Wv', 'bv', 'Wo', 'bo', 'W1', 'b1', 'W2', 'b2', 'gamma1', 'beta1', 'gamma2', 'beta2')}
    del _L2_cond_all

    def _L3_cond_setup():
        import jax, jax.numpy as jnp
        import numpy as np
        TEMPERATURE = 1.0
        ACT_THRESHOLD = 0.1
        MAX_ACT = 1.0
        SAFETY_KNOB = 1.0
        EPS = 1e-08

        def gram_schmidt(X):
            r = X.shape[1]
            Q = X
            for i in range(r):
                q = Q[:, i]
                q = q / (jnp.linalg.norm(q) + EPS)
                Q = Q.at[:, i].set(q)
                coeffs = q @ Q[:, i + 1:]
                Q = Q.at[:, i + 1:].add(-jnp.outer(q, coeffs))
            return Q
        key = jax.random.key(seed)
        ks = jax.random.split(key, 8)
        B, S, D, R = (8, 512, 128, 32)
        init_std = 0.02
        return {'hidden_states': jax.random.normal(ks[0], (B, S, D), jnp.float32), 'safety_score': jax.random.normal(ks[1], (B,), jnp.float32), 'U': jax.random.normal(ks[2], (D, R), jnp.float32) * init_std, 'V': jax.random.normal(ks[3], (D, R), jnp.float32) * init_std, 'safety_bias': jnp.zeros((D,), jnp.float32), 'gate_w1': jax.random.normal(ks[4], (D // 4, D), jnp.float32) * (1.0 / np.sqrt(D)), 'gate_b1': jnp.zeros((D // 4,), jnp.float32), 'gate_w2': jax.random.normal(ks[5], (1, D // 4), jnp.float32) * (1.0 / np.sqrt(D // 4)), 'gate_b2': jnp.zeros((1,), jnp.float32), 'resp_w': jax.random.normal(ks[6], (D, R), jnp.float32) * (1.0 / np.sqrt(R)), 'resp_b': jnp.zeros((D,), jnp.float32)}
    _L3_cond_all = _L3_cond_setup()
    _L3_cond_in = {k: v for k, v in _L3_cond_all.items() if k in ('U', 'V', 'safety_bias', 'gate_w1', 'gate_b1', 'gate_w2', 'gate_b2', 'resp_w', 'resp_b')}
    del _L3_cond_all
    return {'x': x, 'condB_dt': condB_dt, 'itok_B_34_63': itok_B_34_63, 'fside_Bx16xSxS_0': fside_Bx16xSxS_0, 'condB_gatescore': condB_gatescore, 'condB_safetyscore': condB_safetyscore, 'mask_Bx1xSxS_bk0': mask_Bx1xSxS_bk0, 'L0_cond_A_grid': _L0_cond_in['A_grid'], 'L0_cond_B_grid': _L0_cond_in['B_grid'], 'L1_cond_W_ada': _L1_cond_in['W_ada'], 'L1_cond_b_ada': _L1_cond_in['b_ada'], 'L1_cond_Wq': _L1_cond_in['Wq'], 'L1_cond_bq': _L1_cond_in['bq'], 'L1_cond_Wk': _L1_cond_in['Wk'], 'L1_cond_bk': _L1_cond_in['bk'], 'L1_cond_Wv': _L1_cond_in['Wv'], 'L1_cond_bv': _L1_cond_in['bv'], 'L1_cond_Wo': _L1_cond_in['Wo'], 'L1_cond_bo': _L1_cond_in['bo'], 'L1_cond_W1': _L1_cond_in['W1'], 'L1_cond_b1': _L1_cond_in['b1'], 'L1_cond_W2': _L1_cond_in['W2'], 'L1_cond_b2': _L1_cond_in['b2'], 'L1_cond_g2': _L1_cond_in['g2'], 'L1_cond_beta2': _L1_cond_in['beta2'], 'L2_cond_Wq': _L2_cond_in['Wq'], 'L2_cond_bq': _L2_cond_in['bq'], 'L2_cond_Wk': _L2_cond_in['Wk'], 'L2_cond_bk': _L2_cond_in['bk'], 'L2_cond_Wv': _L2_cond_in['Wv'], 'L2_cond_bv': _L2_cond_in['bv'], 'L2_cond_Wo': _L2_cond_in['Wo'], 'L2_cond_bo': _L2_cond_in['bo'], 'L2_cond_W1': _L2_cond_in['W1'], 'L2_cond_b1': _L2_cond_in['b1'], 'L2_cond_W2': _L2_cond_in['W2'], 'L2_cond_b2': _L2_cond_in['b2'], 'L2_cond_gamma1': _L2_cond_in['gamma1'], 'L2_cond_beta1': _L2_cond_in['beta1'], 'L2_cond_gamma2': _L2_cond_in['gamma2'], 'L2_cond_beta2': _L2_cond_in['beta2'], 'L3_cond_U': _L3_cond_in['U'], 'L3_cond_V': _L3_cond_in['V'], 'L3_cond_safety_bias': _L3_cond_in['safety_bias'], 'L3_cond_gate_w1': _L3_cond_in['gate_w1'], 'L3_cond_gate_b1': _L3_cond_in['gate_b1'], 'L3_cond_gate_w2': _L3_cond_in['gate_w2'], 'L3_cond_gate_b2': _L3_cond_in['gate_b2'], 'L3_cond_resp_w': _L3_cond_in['resp_w'], 'L3_cond_resp_b': _L3_cond_in['resp_b']}

def reference(x, condB_dt, itok_B_34_63, fside_Bx16xSxS_0, condB_gatescore, condB_safetyscore, mask_Bx1xSxS_bk0, L0_cond_A_grid, L0_cond_B_grid, L1_cond_W_ada, L1_cond_b_ada, L1_cond_Wq, L1_cond_bq, L1_cond_Wk, L1_cond_bk, L1_cond_Wv, L1_cond_bv, L1_cond_Wo, L1_cond_bo, L1_cond_W1, L1_cond_b1, L1_cond_W2, L1_cond_b2, L1_cond_g2, L1_cond_beta2, L2_cond_Wq, L2_cond_bq, L2_cond_Wk, L2_cond_bk, L2_cond_Wv, L2_cond_bv, L2_cond_Wo, L2_cond_bo, L2_cond_W1, L2_cond_b1, L2_cond_W2, L2_cond_b2, L2_cond_gamma1, L2_cond_beta1, L2_cond_gamma2, L2_cond_beta2, L3_cond_U, L3_cond_V, L3_cond_safety_bias, L3_cond_gate_w1, L3_cond_gate_b1, L3_cond_gate_w2, L3_cond_gate_b2, L3_cond_resp_w, L3_cond_resp_b):
    import jax
    import jax.numpy as jnp

    def _L0_cond_ref(f, A_grid, B_grid, dt):
        import jax, jax.numpy as jnp
        import numpy as np
        B, NX, NY = (16, 128, 128)

        def _grad(f, axis):
            fm = jnp.moveaxis(f, axis, -1)
            g = (jnp.roll(fm, -1, -1) - jnp.roll(fm, 1, -1)) * 0.5
            g0 = (-3.0 * fm[..., 0] + 4.0 * fm[..., 1] - fm[..., 2]) * 0.5
            gN = (3.0 * fm[..., -1] - 4.0 * fm[..., -2] + fm[..., -3]) * 0.5
            g = g.at[..., 0].set(g0).at[..., -1].set(gN)
            return jnp.moveaxis(g, -1, axis)

        def _grad2(f, axis):
            fm = jnp.moveaxis(f, axis, -1)
            g = jnp.roll(fm, -1, -1) - 2.0 * fm + jnp.roll(fm, 1, -1)
            g0 = 2.0 * fm[..., 0] - 5.0 * fm[..., 1] + 4.0 * fm[..., 2] - fm[..., 3]
            gN = 2.0 * fm[..., -1] - 5.0 * fm[..., -2] + 4.0 * fm[..., -3] - fm[..., -4]
            g = g.at[..., 0].set(g0).at[..., -1].set(gN)
            return jnp.moveaxis(g, -1, axis)
        Af = A_grid[None] * f[:, None]
        Bf = B_grid[None] * f[:, None]
        gradv_Af = _grad(Af[:, 0], 1) + _grad(Af[:, 1], 2)
        gradvv_Bf = _grad2(Bf[:, 0], 1) + _grad2(Bf[:, 1], 2) + _grad(_grad(Bf[:, 2], 2), 1) + _grad(_grad(Bf[:, 2], 1), 2)
        df = -gradv_Af + gradvv_Bf * 0.5
        f_new = f + df * dt[:, None, None]
        return jnp.maximum(f_new, 0.0)

    def _L1_cond_ref(src, src_mask, timestep, attention_bias, W_ada, b_ada, Wq, bq, Wk, bk, Wv, bv, Wo, bo, W1, b1, W2, b2, g2, beta2):
        import jax, jax.numpy as jnp
        import numpy as np
        import math
        D_MODEL = 128
        N_HEAD = 16
        HEAD_DIM = D_MODEL // N_HEAD
        D_FF = 512
        NUM_STEPS = 100.0
        RESCALE = 4000.0
        EPS = 1e-05

        def _sin_emb(t):
            half = D_MODEL // 2
            x = t.astype(jnp.float32) / NUM_STEPS * RESCALE
            freqs = jnp.exp(jnp.arange(half, dtype=jnp.float32) * (-math.log(10000.0) / (half - 1)))
            e = x[:, None] * freqs[None, :]
            return jnp.concatenate([jnp.sin(e), jnp.cos(e)], axis=-1)

        def _ln(x):
            m = jnp.mean(x, axis=-1, keepdims=True)
            v = jnp.var(x, axis=-1, keepdims=True)
            return (x - m) / jnp.sqrt(v + EPS)

        def _gelu2(x):
            return x * jax.nn.sigmoid(1.702 * x)
        B, S, D = src.shape
        emb = jax.nn.silu(_sin_emb(timestep)) @ W_ada + b_ada
        scale, shift = jnp.split(emb[:, None, :], 2, axis=-1)
        x = _ln(src) * (1.0 + scale) + shift
        q = (x @ Wq + bq).reshape(B, S, N_HEAD, HEAD_DIM).transpose(0, 2, 1, 3)
        k = (x @ Wk + bk).reshape(B, S, N_HEAD, HEAD_DIM).transpose(0, 2, 1, 3)
        v = (x @ Wv + bv).reshape(B, S, N_HEAD, HEAD_DIM).transpose(0, 2, 1, 3)
        scores = jnp.einsum('bhqd,bhkd->bhqk', q / math.sqrt(HEAD_DIM), k)
        scores = scores + attention_bias
        scores = jnp.where(src_mask, -jnp.inf, scores.astype(jnp.float32))
        probs = jax.nn.softmax(scores, axis=-1).astype(v.dtype)
        ctx = jnp.einsum('bhqk,bhkd->bhqd', probs, v)
        ctx = ctx.transpose(0, 2, 1, 3).reshape(B, S, D)
        x = x + (ctx @ Wo + bo)
        h = _ln(x) * g2 + beta2
        ff = _gelu2(h @ W1 + b1) @ W2 + b2
        return x + ff

    def _L2_cond_ref(x, gate_score, Wq, bq, Wk, bk, Wv, bv, Wo, bo, W1, b1, W2, b2, gamma1, beta1, gamma2, beta2):
        import jax, jax.numpy as jnp
        import numpy as np
        D_MODEL = 128
        N_HEADS = 16
        D_HEAD = D_MODEL // N_HEADS
        D_FF = 512
        EPS = 1e-05

        def layernorm(x, gamma, beta):
            mu = jnp.mean(x, axis=-1, keepdims=True)
            var = jnp.var(x, axis=-1, keepdims=True)
            return (x - mu) * jax.lax.rsqrt(var + EPS) * gamma + beta
        B, T, C = x.shape
        h = layernorm(x, gamma1, beta1)
        Q = (h @ Wq + bq).reshape(B, T, N_HEADS, D_HEAD).transpose(0, 2, 1, 3)
        K = (h @ Wk + bk).reshape(B, T, N_HEADS, D_HEAD).transpose(0, 2, 1, 3)
        V = (h @ Wv + bv).reshape(B, T, N_HEADS, D_HEAD).transpose(0, 2, 1, 3)
        scores = jnp.einsum('bhqd,bhkd->bhqk', Q, K) / np.sqrt(D_HEAD)
        causal = jnp.tril(jnp.ones((T, T), dtype=bool))
        scores = jnp.where(causal, scores, -jnp.inf)
        attn = jax.nn.softmax(scores, axis=-1)
        ctx = jnp.einsum('bhqk,bhkd->bhqd', attn, V)
        ctx = ctx.transpose(0, 2, 1, 3).reshape(B, T, C)
        attn_out = ctx @ Wo + bo
        x1 = x + attn_out
        h2 = layernorm(x1, gamma2, beta2)
        ff = jax.nn.gelu(h2 @ W1 + b1, approximate=False) @ W2 + b2
        x2 = x1 + ff
        g = gate_score[:, None, None]
        return x + g * (x2 - x)

    def _L3_cond_ref(hidden_states, safety_score, U, V, safety_bias, gate_w1, gate_b1, gate_w2, gate_b2, resp_w, resp_b):
        import jax, jax.numpy as jnp
        import numpy as np
        TEMPERATURE = 1.0
        ACT_THRESHOLD = 0.1
        MAX_ACT = 1.0
        SAFETY_KNOB = 1.0
        EPS = 1e-08

        def gram_schmidt(X):
            r = X.shape[1]
            Q = X
            for i in range(r):
                q = Q[:, i]
                q = q / (jnp.linalg.norm(q) + EPS)
                Q = Q.at[:, i].set(q)
                coeffs = q @ Q[:, i + 1:]
                Q = Q.at[:, i + 1:].add(-jnp.outer(q, coeffs))
            return Q
        R = resp_w.shape[1]
        U_o = gram_schmidt(U)
        V_o = gram_schmidt(V)
        basis = U_o @ V_o.T
        pooled = hidden_states.mean(axis=1)
        h1 = jax.nn.relu(pooled @ gate_w1.T + gate_b1)
        base_act = jax.nn.sigmoid(h1 @ gate_w2.T + gate_b2)
        mod = jax.nn.sigmoid(safety_score[:, None] / TEMPERATURE)
        knob = jnp.clip(jnp.asarray(SAFETY_KNOB, hidden_states.dtype), ACT_THRESHOLD, MAX_ACT)
        strength = (base_act * mod * knob)[:, None, :]
        proj = hidden_states @ basis
        feats = proj @ basis.T[:, :R]
        response = feats @ resp_w.T + resp_b + safety_bias
        return hidden_states + strength * response
    x = _L0_cond_ref(x, L0_cond_A_grid, L0_cond_B_grid, condB_dt)
    x = _L1_cond_ref(x, mask_Bx1xSxS_bk0, itok_B_34_63, fside_Bx16xSxS_0, L1_cond_W_ada, L1_cond_b_ada, L1_cond_Wq, L1_cond_bq, L1_cond_Wk, L1_cond_bk, L1_cond_Wv, L1_cond_bv, L1_cond_Wo, L1_cond_bo, L1_cond_W1, L1_cond_b1, L1_cond_W2, L1_cond_b2, L1_cond_g2, L1_cond_beta2)
    x = _L2_cond_ref(x, condB_gatescore, L2_cond_Wq, L2_cond_bq, L2_cond_Wk, L2_cond_bk, L2_cond_Wv, L2_cond_bv, L2_cond_Wo, L2_cond_bo, L2_cond_W1, L2_cond_b1, L2_cond_W2, L2_cond_b2, L2_cond_gamma1, L2_cond_beta1, L2_cond_gamma2, L2_cond_beta2)
    x = _L3_cond_ref(x, condB_safetyscore, L3_cond_U, L3_cond_V, L3_cond_safety_bias, L3_cond_gate_w1, L3_cond_gate_b1, L3_cond_gate_w2, L3_cond_gate_b2, L3_cond_resp_w, L3_cond_resp_b)
    return x

_drawn_inputs = setup_inputs


def setup_inputs(seed=0):
    import zlib

    import numpy as np

    out = dict(_drawn_inputs(seed))
    spreads = {'L1_cond_b_ada': (0.0, 0.1),
     'L1_cond_bq': (0.0, 0.8),
     'L1_cond_bk': (0.0, 2.0),
     'L1_cond_bv': (0.0, 0.331),
     'L1_cond_bo': (0.0, 0.1),
     'L1_cond_b1': (0.0, 0.356),
     'L1_cond_b2': (0.0, 0.1),
     'L1_cond_g2': (1.0, 0.6),
     'L1_cond_beta2': (0.0, 0.8),
     'L2_cond_bq': (0.0, 0.8),
     'L2_cond_bk': (0.0, 2.0),
     'L2_cond_bv': (0.0, 0.1),
     'L2_cond_bo': (0.0, 0.1),
     'L2_cond_b1': (0.0, 0.371),
     'L2_cond_b2': (0.0, 0.267),
     'L2_cond_gamma1': (1.0, 0.2),
     'L2_cond_beta1': (0.0, 0.1),
     'L2_cond_gamma2': (1.0, 0.2),
     'L2_cond_beta2': (0.0, 0.355),
     'L3_cond_safety_bias': (0.0, 0.483),
     'L3_cond_gate_b1': (0.0, 2.0),
     'L3_cond_resp_b': (0.0, 0.535)}
    factors = {'fside_Bx16xSxS_0': 8.0,
     'L1_cond_Wq': 8.0,
     'L1_cond_Wk': 8.0,
     'L1_cond_Wv': 5.596,
     'L3_cond_V': 64.0,
     'L3_cond_gate_w1': 5.979,
     'L3_cond_gate_w2': 8.0}
    for name, (base, spread) in spreads.items():
        noise = np.random.default_rng([zlib.crc32(name.encode()), seed]).standard_normal(out[name].shape)
        drawn = base * np.exp(spread * noise) if base else spread * noise
        out[name] = jnp.asarray(drawn.astype(out[name].dtype))
    for name, factor in factors.items():
        out[name] = (out[name] * factor).astype(out[name].dtype)
    return out
```

```python
from contextlib import ExitStack

import numpy as np
import concourse.bass as bass
from concourse import mybir

F32 = mybir.dt.float32
BF16 = mybir.dt.bfloat16
I32 = mybir.dt.int32
U32 = mybir.dt.uint32
U8 = mybir.dt.uint8
ALU = mybir.AluOpType
ACT = mybir.ActivationFunctionType
AX = mybir.AxisListType
ds = bass.ds

B, S, D, H, DH, FF = 16, 128, 128, 16, 8, 512
GB = 4
NG = B // GB
GW = GB * D
PR = H // 2
HU = H // 2
UW = HU * S
NU = 2 * B
R = 32
NF = FF // 128
SLOTS = 8
HROWS = SLOTS * DH
TOK = B * S
LN_EPS = 1e-5
GS_EPS = 1e-8
NEG = -1e30
ISQ = float(DH) ** -0.5
MAGIC = 0x5F3759DF

C_ID, C_PD1, C_ND1, C_HD2, C_CAUS, C_FREQ, C_PHASE, C_QUART, C_GSM = 0, 128, 256, 384, 512, 640, 641, 642, 643
C_ALL = C_GSM + 2 * R

V_BADA, V_G2, V_BETA2, V_B1, V_GA1, V_BE1, V_GA2, V_BE2, V_B1B = 0, 2, 3, 4, 8, 9, 10, 11, 12
V_ALL = 16


def constants():
    c = np.zeros((128, C_ALL), np.float32)
    n = S
    d1 = np.zeros((n, n), np.float32)
    d2 = np.zeros((n, n), np.float32)
    for i in range(1, n - 1):
        d1[i, i - 1], d1[i, i + 1] = -0.5, 0.5
        d2[i, i - 1], d2[i, i], d2[i, i + 1] = 1.0, -2.0, 1.0
    d1[0, :3] = [-1.5, 2.0, -0.5]
    d1[-1, -3:] = [0.5, -2.0, 1.5]
    d2[0, :4] = [2.0, -5.0, 4.0, -1.0]
    d2[-1, -4:] = [-1.0, 4.0, -5.0, 2.0]
    c[:, C_ID:C_ID + 128] = np.eye(128)
    c[:, C_PD1:C_PD1 + 128] = d1.T
    c[:, C_ND1:C_ND1 + 128] = -d1.T
    c[:, C_HD2:C_HD2 + 128] = 0.5 * d2.T
    c[:, C_CAUS:C_CAUS + 128] = np.where(np.tril(np.ones((n, n), bool)), 0.0, NEG)
    half = D // 2
    freq = np.exp(np.arange(half, dtype=np.float32) * np.float32(-np.log(10000.0) / (half - 1)))
    c[:, C_FREQ] = np.concatenate([freq, freq])
    c[half:, C_PHASE] = np.pi / 2
    c[half:, C_QUART] = 0.25
    c[:, C_GSM:C_GSM + R] = 1.0
    return c


def build(nc, a, out):
    ctx = ExitStack()
    with ctx:
        def sb(name, shape, dt=F32):
            return ctx.enter_context(nc.sbuf_tensor(name, shape, dt))

        def sem(name):
            return ctx.enter_context(nc.semaphore(name))

        X = sb("X", [128, B, D])
        V = sb("V", [128, B, D])
        CTX = sb("CTX", [128, B, D])
        QS = sb("QS", [128, PR, TOK], BF16)
        KS = sb("KS", [128, PR, 2, TOK], BF16)
        FS = sb("FS", [128, 2, H, S])
        VP = sb("VP", [128, 2, H, 32])
        MSK = sb("MSK", [128, B, S], BF16)
        CST = sb("CST", [128, C_ALL])
        IDB = sb("IDB", [128, 128], BF16)
        CAUS = sb("CAUS", [128, 128], BF16)
        WQK = sb("WQK", [128, 2, 2, D])
        WV = sb("WV", [128, 2, D])
        WO = sb("WO", [128, 2, D])
        W1 = sb("W1", [128, 2, FF])
        W2 = sb("W2", [128, 2, NF, D])
        VR = sb("VR", [32, 128])
        VRP = sb("VRP", [4, 128])
        VRT = sb("VRT", [4, 128])
        COL = sb("COL", [128, V_ALL])
        BQK = sb("BQK", [128, 4])
        BVB = sb("BVB", [128, 2, D])
        BOB = sb("BOB", [128, 2, D])
        B2B = sb("B2B", [128, 2, D])
        CB = sb("CB", [128, 2, D])
        DTB = sb("DTB", [128, B])
        GATE = sb("GATE", [128, B])
        SAFE = sb("SAFE", [128, B])
        MOD = sb("MOD", [128, B])
        GB2 = sb("GB2", [128, 1])
        ADA = sb("ADA", [128, 2, B])
        MV = sb("MV", [128, B, 2])
        ST6 = sb("ST6", [128, B, 6])
        RS = sb("RS", [128, B])
        NMR = sb("NMR", [128, B])
        NT = sb("NT", [128, B])
        NI = sb("NI", [128, B], I32)
        NY = sb("NY", [128, B])
        MX = sb("MX", [128, 2, HU])
        RSUM = sb("RSUM", [128, H])
        RM = sb("RM", [128, D])
        W1T = sb("W1T", [128, R])
        W2G = sb("W2G", [R, 1])
        GB1 = sb("GB1", [R, 1])
        DUM = sb("DUM", [128, 8])
        SM = sb("SM", [128, 64])
        WORK = sb("WORK", [128, 8320])

        P = ctx.enter_context(nc.psum_tensor("P", [128, 8, 512], F32))
        QD = nc.dram_tensor("q_parts", (2, SLOTS, 64, TOK), BF16, kind="Internal").ap()
        KD = nc.dram_tensor("k_parts", (2, 3, 64, TOK), BF16, kind="Internal").ap()
        QD2 = nc.dram_tensor("q_parts2", (2, SLOTS, 64, TOK), BF16, kind="Internal").ap()
        KD2 = nc.dram_tensor("k_parts2", (2, 3, 64, TOK), BF16, kind="Internal").ap()

        ident = CST[:, C_ID:C_ID + 128]
        pD1T = CST[:, C_PD1:C_PD1 + 128]
        nD1T = CST[:, C_ND1:C_ND1 + 128]
        hD2T = CST[:, C_HD2:C_HD2 + 128]

        def work(at, *shape, dt=F32):
            n = int(np.prod(shape))
            if dt == BF16:
                n //= 2
            v = WORK[:, at:at + n]
            if dt != F32:
                v = v.bitcast(dt)
            names = " ".join(f"d{i}" for i in range(len(shape)))
            if len(shape) == 1:
                return v
            return v.rearrange(f"p ({names}) -> p {names}", **{f"d{i}": s for i, s in enumerate(shape)})

        def early(at, *shape):
            v = FS[:, :, :, :].rearrange("p a h k -> p (a h k)")[:, at:at + int(np.prod(shape))]
            if len(shape) == 1:
                return v
            names = " ".join(f"d{i}" for i in range(len(shape)))
            return v.rearrange(f"p ({names}) -> p {names}", **{f"d{i}": n for i, n in enumerate(shape)})

        GRID = early(0, 5, D)
        GRT = early(640, 3, D)
        gsb = early(1024, 2, 2, R)
        gcm = early(1152, 2, R)
        gws = early(1216, 16)
        EMB = early(1232, 8, B)
        TI = early(1360, B).bitcast(I32)
        LR = early(1376, R)
        BBm = early(1408, R)
        WADA = early(1440, 2 * D)
        LW = early(1696, D)
        UT = early(1824, 2, D)
        BST = early(2080, D)
        WQ0 = early(2208, 2, 2, D)
        MU8 = early(2720, B * S // 4).bitcast(U8).rearrange("q (b k) -> q b k", b=B)
        BBTt = sb("BBTt", [R, D])
        RWT = sb("RWT", [R, D])
        fS = work(0, 2, GW)
        fT = work(1024, 2, 3, GW)
        AF = work(4096, 2, GW)
        BFv = work(5120, 2, GW)
        STG = work(6144, 2, GW)
        xn = work(0, 2, GB, D)
        xT = work(1024, 2, GW)
        qf = work(2048, 2, 2, GW)
        qr = work(4096, 2, GW)
        qp = work(5120, 2, 2, 3, GW, dt=BF16)
        Sc = work(0, 2, HU, S)
        E = work(2048, 2, HU, S)
        pT = work(4096, 2, HU, S)
        cs = work(6144, 2, 2 * S)
        cS = work(0, 2, GB, D)
        cT = work(1024, 2, GW)
        gT = work(2048, 2, NF, GW)
        yS = work(6144, 2, GB, D)
        zS = work(7168, 2, GB, D)
        pl = work(8192, 2, 16)

        ld_const, ld_vec, ld_w, ld_gs, ld_mask, ld_row = (sem(f"ld_{n}") for n in ("const", "vec", "w", "gs", "mask", "row"))
        f_landed = [sem("f_landed0"), sem("f_landed1")]
        fs_landed = [sem("fs_landed0"), sem("fs_landed1")]
        gs_dot, gs_norm, gs_step, gs_chain = sem("gs_dot"), sem("gs_norm"), sem("gs_step"), sem("gs_chain")
        su_pe, su_dve, su_act = sem("setup_pe"), sem("setup_dve"), sem("setup_act")
        zeros_set, mask_set, vrp_turned = sem("zeros_set"), sem("mask_set"), sem("biases_turned")
        s_prod, s_fT, s_fTp, s_H, s_U, s_df, s_stage, s_x0 = (sem(n) for n in (
            "stencil_products", "f_transposed", "fT_products", "H_ready", "U_ready", "df_ready", "stage_ready", "x_ready"))
        stats_st, stats_done, newton = sem("stats_st"), sem("stats_done"), sem("newton")
        p_norm, p_T, p_xT, p_back, p_nat, p_q, p_qf, p_r, p_q2, p_q3, p_v = (sem(n) for n in (
            "normed", "transposed", "xT_ready", "x_back", "x_natural", "qkv_ready", "qk_evacuated", "qk_rest", "qk_second",
            "qk_third", "v_ready"))
        parts_out, stacks_in = [sem("parts_out0"), sem("parts_out1")], sem("stacks_in")
        a_qk, a_add, a_max, a_sub, a_exp, a_T, a_pT, a_pv, a_cs, a_ct, a_rs, a_ctx, a_vp = (sem(n) for n in (
            "scores_ready", "biased", "max_ready", "shifted", "exp_done", "probs_transposed", "probsT_ready", "pv_done",
            "ctxT_copied", "ctx_back", "rowsum_inv", "ctx_ready", "v_padded"))
        o_cp, o_T, o_cT, o_wo, o_res, o_bo = (sem(n) for n in (
            "ctx_staged", "ctx_T", "ctxT_ready", "wo_done", "x1_ready", "x1_bias"))
        m_n, m_T, m_hT, m_f, m_g, m_y, m_t, m_u, m_d, m_x = (sem(n) for n in (
            "ff_normed", "ff_T", "ff_hT", "ff_up", "ff_gelu", "ff_down", "ff_biased", "ff_sum", "ff_diff", "ff_x"))
        r_cp, r_T, r_hT, r_pl, r_m, r_g1, r_h1, r_g2, r_ba, r_st, r_t, r_o, r_out = (sem(n) for n in (
            "l3_staged", "l3_T", "l3_hT", "l3_pooled", "l3_resp", "l3_gate1", "l3_h1", "l3_gate2", "l3_base", "l3_strength",
            "l3_biased", "l3_out", "out_written"))

        N_VEC = 18 * 16
        N_W = 14 * 16
        N_ROW = 11 * 16
        block = ctx.enter_context(nc.Block())

        @block.sync
        def _(sp):
            sp.dma_start(CST[:, :], a["consts"]).then_inc(ld_const, 16)
            sp.dma_start(gsb[:, 0, 0, :], a["L3_cond_U"]).then_inc(ld_gs, 16)
            sp.dma_start(gsb[:, 0, 1, :], a["L3_cond_V"]).then_inc(ld_gs, 16)
            sp.dma_start(GRID[:, 0:2, :], a["L0_cond_A_grid"].rearrange("c x y -> x c y")).then_inc(ld_const, 16)
            sp.dma_start(GRID[:, 2:5, :], a["L0_cond_B_grid"].rearrange("c x y -> x c y")).then_inc(ld_const, 16)
            sp.dma_start(DTB[:, :], a["condB_dt"][None, :].to_broadcast([128, B])).then_inc(ld_const, 16)
            for g in range(2):
                sp.dma_start(fS[:, g, :].rearrange("p (b y) -> p b y", b=GB),
                             a["x"][GB * g:GB * g + GB].rearrange("b x y -> x b y")).then_inc(f_landed[g], 16)
            vecs = [("L1_cond_b_ada", V_BADA, 2), ("L1_cond_g2", V_G2, 1), ("L1_cond_beta2", V_BETA2, 1), ("L1_cond_b1", V_B1, 4),
                    ("L2_cond_gamma1", V_GA1, 1), ("L2_cond_beta1", V_BE1, 1), ("L2_cond_gamma2", V_GA2, 1),
                    ("L2_cond_beta2", V_BE2, 1), ("L2_cond_b1", V_B1B, 4)]
            for name, at, n in vecs:
                sp.dma_start(VR[at:at + n, :], a[name].rearrange("(n d) -> n d", n=n)).then_inc(ld_vec, 16)
            sp.dma_start(GB1[:, :], a["L3_cond_gate_b1"][:, None], allow_slow_non_contiguous=True).then_inc(ld_vec, 16)
            for i, name in enumerate(("L1_cond_bq", "L1_cond_bk", "L2_cond_bq", "L2_cond_bk")):
                sp.dma_start(VRP[i:i + 1, :], a[name][None, :]).then_inc(ld_vec, 16)
            sp.dma_start(TI, a["itok_B_34_63"][None, :].to_broadcast([128, B])).then_inc(ld_vec, 16)
            sp.dma_start(WADA, a["L1_cond_W_ada"]).then_inc(ld_vec, 16)
            sp.dma_start(LR, a["L3_cond_resp_w"]).then_inc(ld_vec, 16)
            sp.dma_start(LW[0:R, :], a["L3_cond_gate_w1"]).then_inc(ld_vec, 16)
            for l in range(2):
                n = f"L{l + 1}_cond_"
                sp.dma_start(WQ0[:, l, 0, :], a[n + "Wq"]).then_inc(ld_w, 16)
                sp.dma_start(WQ0[:, l, 1, :], a[n + "Wk"]).then_inc(ld_w, 16)
                sp.dma_start(WV[:, l, :], a[n + "Wv"]).then_inc(ld_w, 16)
                sp.dma_start(WO[:, l, :], a[n + "Wo"]).then_inc(ld_w, 16)
                sp.dma_start(W1[:, l, :], a[n + "W1"]).then_inc(ld_w, 16)
                sp.dma_start(W2[:, l, :, :], a[n + "W2"].rearrange("(c f) d -> f c d", c=NF)).then_inc(ld_w, 16)
            sp.dma_start(W2G[:, :], a["L3_cond_gate_w2"].rearrange("a b -> b a"), allow_slow_non_contiguous=True).then_inc(ld_w, 16)
            sp.dma_start(GB2[:, :], a["L3_cond_gate_b2"][None, :].to_broadcast([128, 1])).then_inc(ld_w, 16)
            for l in range(2):
                n = f"L{l + 1}_cond_"
                sp.dma_start(BVB[:, l, :], a[n + "bv"][None, :].to_broadcast([128, D])).then_inc(ld_row, 16)
                sp.dma_start(BOB[:, l, :], a[n + "bo"][None, :].to_broadcast([128, D])).then_inc(ld_row, 16)
                sp.dma_start(B2B[:, l, :], a[n + "b2"][None, :].to_broadcast([128, D])).then_inc(ld_row, 16)
            sp.dma_start(CB[:, 0, :], a["L3_cond_resp_b"][None, :].to_broadcast([128, D])).then_inc(ld_row, 16)
            sp.dma_start(CB[:, 1, :], a["L3_cond_safety_bias"][None, :].to_broadcast([128, D])).then_inc(ld_row, 16)
            sp.dma_start(GATE[:, :], a["condB_gatescore"][None, :].to_broadcast([128, B])).then_inc(ld_row, 16)
            sp.dma_start(SAFE[:, :], a["condB_safetyscore"][None, :].to_broadcast([128, B])).then_inc(ld_row, 16)
            sp.dma_start(MU8.bitcast(I32), a["mask_Bx1xSxS_bk0"].rearrange("b o q k -> q b (o k)")).then_inc(ld_row, 16)
            for g in range(2, NG):
                sp.wait_ge(s_stage, g - 1)
                sp.dma_start(fS[:, g - 2, :].rearrange("p (b y) -> p b y", b=GB),
                             a["x"][GB * g:GB * g + GB].rearrange("b x y -> x b y")).then_inc(f_landed[g - 2], 16)
            sp.wait_ge(s_stage, NG)
            sp.wait_ge(su_act, 8)
            sp.wait_ge(mask_set, 3)
            for b in range(2):
                for rows in (slice(0, 64), slice(64, 128)):
                    sp.dma_start(FS[rows, b, :, :], a["fside_Bx16xSxS_0"][b, :, rows, :].rearrange("h q k -> q h k")).then_inc(fs_landed[b], 16)

            def stacks(l):
                qd, kd = (QD, KD) if l == 0 else (QD2, KD2)
                for g in range(NG):
                    par, cols = g % 2, slice(g * GW, (g + 1) * GW)
                    sp.wait_ge(p_q3, 2 * (NG * l + g + 1))
                    for h2 in range(2):
                        rows = slice(64 * h2, 64 * h2 + 64)
                        for p, (s0, n) in enumerate(((0, 3), (3, 3), (6, 2))):
                            sp.dma_start(qd[h2, s0:s0 + n, :, cols].rearrange("s r t -> r s t"),
                                         qp[rows, par, 0, p:p + 1, :].to_broadcast([64, n, GW])).then_inc(parts_out[par], 16)
                        sp.dma_start(kd[h2, :, :, cols].rearrange("s r t -> r s t"),
                                     qp[rows, par, 1, :, :]).then_inc(parts_out[par], 16)
                    if l == 0:
                        sp.wait_ge(zeros_set, 3)
                    else:
                        sp.wait_ge(a_qk, NU)
                    sp.wait_ge(parts_out[par], 128 * ((NG // 2) * l + g // 2 + 1))
                    sp.dma_start(QS[:, :, cols], qd[:, :, :, cols].rearrange("h s (d r) t -> (h s d) r t", r=PR)).then_inc(stacks_in, 16)
                    for h2 in range(2):
                        for s0, n in ((0, 3), (3, 3), (6, 2)):
                            sp.dma_start(KS[64 * h2 + 8 * s0:64 * h2 + 8 * (s0 + n), :, h2, cols],
                                         kd[h2, 0:n, :, cols].rearrange("s (d r) t -> (s d) r t", r=PR)).then_inc(stacks_in, 16)

            stacks(0)
            with sp.Fori(1, B // 2) as i:
                for par in range(2):
                    sp.wait_ge(a_add, 4 * i + 2 * par - 2)
                    for rows in (slice(0, 64), slice(64, 128)):
                        sp.dma_start(FS[rows, par, :, :], a["fside_Bx16xSxS_0"][ds(2 * i + par, 1), :, rows, :].rearrange("b h q k -> q (b h) k"))\
                          .then_inc(fs_landed[par], 16)
            stacks(1)
            with sp.Fori(0, NG // 2) as i:
                for par in range(2):
                    sp.wait_ge(r_o, 2 * i + par + 1)
                    sp.dma_start(out[ds((2 * i + par) * GB, GB)].rearrange("b s d -> s b d"), zS[:, par, :, :]).then_inc(r_out, 16)
            sp.wait_ge(r_out, 16 * NG)

        @block.gpsimd
        def _(pool):
            pool.memset(VP[:, :, :, :], 0.0).then_inc(zeros_set, 1)
            pool.wait_ge(zeros_set, 1)
            pool.memset(KS[0:64, :, 1, :].bitcast(U32), 0).then_inc(zeros_set, 1)
            pool.wait_ge(zeros_set, 2)
            pool.memset(KS[64:128, :, 0, :].bitcast(U32), 0).then_inc(zeros_set, 1)
            pool.wait_ge(zeros_set, 3)
            vp5 = VP[:, :, :, :].rearrange("k p (r h2) (w e) -> k (p r) h2 w e", h2=2, w=2)
            for h2 in range(2):
                pool.memset(vp5[:, :, h2, h2, DH:DH + 1], 1.0).then_inc(mask_set, 1)
                pool.wait_ge(mask_set, h2 + 1)
            pool.wait_ge(ld_const, 64)
            pool.tensor_scalar(CAUS[:, :], CST[:, C_CAUS:C_CAUS + 128], 1.0, 0.0, ALU.mult, ALU.add).then_inc(zeros_set, 1)
            pool.wait_ge(zeros_set, 4)
            pool.wait_ge(ld_row, N_ROW)
            pool.tensor_scalar(MSK[:, :, :], MU8,
                               NEG, 0.0, ALU.mult, ALU.add).then_inc(mask_set, 1)

            def pad_v(l, b, par):
                u = NU * l
                pool.wait_ge(a_pv, u + 2 * b - 2)
                src = V[:, ds(b, 1), :].rearrange("k o (r e) -> k (o r) e", r=PR)
                for h2 in range(2):
                    pool.tensor_copy(vp5[:, PR * par:PR * par + PR, h2, h2, 0:DH], src[:, :, DH * h2:DH * h2 + DH]).then_inc(a_vp, 1)

            def pad_first(l, b):
                src = V[:, b, :].rearrange("k (r e) -> k r e", r=PR)
                for h2 in range(2):
                    pool.tensor_copy(vp5[:, PR * b:PR * b + PR, h2, h2, 0:DH], src[:, :, DH * h2:DH * h2 + DH]).then_inc(a_vp, 1)

            def shift(u, c):
                pool.wait_ge(a_max, u + 1)
                pool.tensor_tensor(Sc[:, c % 2, :, :], Sc[:, c % 2, :, :],
                                   MX[:, c % 2, :, None].to_broadcast([128, HU, S]), ALU.subtract).then_inc(a_sub, 1)

            pool.wait_ge(p_v, NG)
            for c in range(4):
                if c % 2 == 0:
                    pad_first(0, c // 2)
                shift(c, c)
            with pool.Fori(1, B // 2) as i:
                for c in range(4):
                    if c % 2 == 0:
                        pad_v(0, 2 * i + c // 2, c // 2)
                    shift(4 * i + c, c)
            pool.wait_ge(a_pv, NU)
            pool.wait_ge(p_v, 2 * NG)
            for b in range(2):
                pad_first(1, b)
            with pool.Fori(1, B // 2) as i:
                for par in range(2):
                    pad_v(1, 2 * i + par, par)

        @block.tensor
        def _(pe):
            mm, tr = nc.tensor.matmul, nc.tensor.transpose

            pe.wait_ge(ld_const, 64)
            pe.wait_ge(ld_gs, 32)
            with pe.Fori(0, R // 2) as i:
                for c in range(2):
                    pe.wait_ge(gs_step, 4 * i + 2 * c)
                    for m in range(2):
                        ins = mm(P[:, 6, R * m:R * m + R], gsb[:, c, m, 0:1].to_broadcast([128, 128]), gsb[:, c, m, :],
                                 start=True, stop=True)
                    ins.then_inc(gs_dot, 1)
            pe.wait_ge(gs_step, 2 * R)
            pe.wait_ge(ld_vec, N_VEC)
            for m in range(2):
                tr(P[0:R, 6, 128 * m:128 * m + 128], gsb[:, 0, m, :], ident)
            tr(P[0:R, 6, 256:384], LR, ident).then_inc(su_pe, 1)
            tr(P[:, 7, 0:R], LW[0:R, :], ident[0:R, 0:R])
            tr(P[:, 7, 64:64 + V_ALL], VR[0:V_ALL, :], ident[0:V_ALL, 0:V_ALL])
            pe.wait_ge(vrp_turned, 1)
            tr(P[:, 7, 128:132], VRT[0:4, :], ident[0:4, 0:4]).then_inc(su_pe, 1)
            for m in range(3):
                ins = tr(P[:, 5, 128 * m:128 * m + 128], GRID[:, (1, 3, 4)[m], :], ident)
            ins.then_inc(su_pe, 1)
            pe.wait_ge(su_dve, 1)
            mm(P[:, 4, 0:128], UT[0:R, 1, :], UT[0:R, 0, :], start=True, stop=True).then_inc(su_pe, 1)
            pe.wait_ge(su_dve, 2)
            mm(P[:, 4, 128:128 + R], BST, BST[:, 0:R], start=True, stop=True).then_inc(su_pe, 1)
            pe.wait_ge(su_dve, 3)
            tr(P[0:R, 4, 256:384], BBm, ident).then_inc(su_pe, 1)
            pe.wait_ge(su_dve, 4)
            mm(P[:, 4, 384:512], BBTt[:, :], RWT[:, :], start=True, stop=True).then_inc(su_pe, 1)
            pe.wait_ge(su_dve, 7)
            for m in range(2):
                ins = mm(P[:, 7, 256 + B * m:256 + B * m + B], WADA[:, 128 * m:128 * m + 128], EMB[:, 7, :], start=True, stop=True)
            ins.then_inc(su_pe, 1)

            with pe.Fori(0, NG // 2) as i:
                for par in range(2):
                    n = 2 * i + par + 1
                    pe.wait_ge(f_landed[par], 16 * (i + 1))
                    for j in range(GB):
                        ins = tr(P[:, par, D * j:D * j + D], fS[:, par, D * j:D * j + D], ident)
                    ins.then_inc(s_fT, 1)
                    pe.wait_ge(s_fTp, 3 * n)
                    for j in range(GB):
                        ins = mm(P[:, 2 + par, D * j:D * j + D], fT[:, par, 2, D * j:D * j + D], pD1T, start=True, stop=True)
                    ins.then_inc(s_H, 1)
                    pe.wait_ge(s_prod, 2 * n)
                    mm(P[:, 4 + par, :], hD2T, BFv[:, par, :], start=True, stop=False, skip_group_check=True)
                    for j in range(GB):
                        mm(P[:, 4 + par, D * j:D * j + D], fT[:, par, 0, D * j:D * j + D], nD1T, start=False, stop=False, skip_group_check=True)
                        mm(P[:, 4 + par, D * j:D * j + D], fT[:, par, 1, D * j:D * j + D], hD2T, start=False, stop=False, skip_group_check=True)
                    pe.wait_ge(s_U, n)
                    mm(P[:, 4 + par, :], nD1T, AF[:, par, :], start=False, stop=True, skip_group_check=True).then_inc(s_df, 1)

            def project(l):
                pe.wait_ge(ld_w, N_W)
                pe.wait_ge(su_act, 8)
                with pe.Fori(0, NG // 2) as i:
                    for par in range(2):
                        n = NG * l + 2 * i + par + 1
                        pe.wait_ge(p_norm, GB * n)
                        for j in range(GB):
                            ins = tr(P[:, 0, D * j:D * j + D], xn[:, par, j, :], ident)
                        ins.then_inc(p_T, 1)
                        pe.wait_ge(p_xT, GB * n if l == 0 else GB * NG + n - NG)
                        if l == 0:
                            for j in range(GB):
                                ins = tr(P[:, 1, D * j:D * j + D], xT[:, par, D * j:D * j + D], ident)
                            ins.then_inc(p_back, 1)
                        for m in range(2):
                            mm(P[:, 2 + 2 * par + m, :], WQK[:, l, m, :], xT[:, par, :], start=True, stop=True).then_inc(p_q, 1)
                        for j in range(GB):
                            ins = mm(P[:, 6 + par, D * j:D * j + D], xT[:, par, D * j:D * j + D], WV[:, l, :], start=True, stop=True)
                        ins.then_inc(p_q, 1)

            def attention(l):
                def scores(u, c, b):
                    if u is not None:
                        pe.wait_ge(a_add, u - 1)
                    par = c % 2
                    for k in range(2):
                        bank = P[:, 2 * par + k, :]
                        mask = CAUS[:, None, :] if l else MSK[:, ds(b, 1), :]
                        mm(bank, IDB[:, :], mask.to_broadcast([128, 4, S]), start=True, stop=False, skip_group_check=True)
                        for r in range(2):
                            pr = 4 * par + 2 * k + r
                            ins = mm(bank[:, 256 * r:256 * r + 256], QS[:, pr, ds(b * S, S)], KS[:, pr, :, ds(b * S, S)],
                                     start=False, stop=(r == 1), skip_group_check=True)
                    ins.then_inc(a_qk, 1)

                def transposes(u, c):
                    pe.wait_ge(a_exp, u + 1)
                    pe.wait_ge(a_pT, u)
                    for hh in range(HU):
                        ins = tr(P[:, 4 + hh // 4, S * (hh % 4):S * (hh % 4) + S], E[:, c % 2, hh, :], ident)
                    ins.then_inc(a_T, 1)

                def pv(u, c, b):
                    pe.wait_ge(a_pT, u + 1)
                    if c % 2 == 0:
                        pe.wait_ge(a_vp, 2 * (B * l + b + 1))
                        pe.wait_ge(a_cs, B * l + b)
                    for h2 in range(2):
                        for r in range(4):
                            hh = 2 * r + h2
                            ins = mm(P[32 * r:32 * r + 32, 6, S * (c % 2):S * (c % 2) + S],
                                     VP[:, (c // 2) % 2, HU * (c % 2) + hh, :], pT[:, c % 2, hh, :],
                                     start=(h2 == 0), stop=(h2 == 1), skip_group_check=True)
                    ins.then_inc(a_pv, 1)

                def back(b, par):
                    pe.wait_ge(a_cs, B * l + b + 1)
                    pe.wait_ge(a_ctx, B * l + b)
                    for m in range(2):
                        ins = tr(P[:, 7, S * m:S * m + S], cs[:, par, S * m:S * m + S], ident)
                    ins.then_inc(a_ct, 1)

                base = NU * l
                for c in range(4):
                    scores(base + c if c >= 2 or l else None, c, c // 2)
                    if c >= 2:
                        transposes(base + c - 2, c - 2)
                    if c >= 3:
                        pv(base + c - 3, c - 3, 0)
                with pe.Fori(1, B // 2) as i:
                    for c in range(4):
                        u = base + 4 * i + c
                        scores(u, c, 2 * i + c // 2)
                        transposes(u - 2, (c - 2) % 4)
                        pv(u - 3, (c - 3) % 4, 2 * i + (c - 3) // 2)
                        if c % 2:
                            back(2 * i + (c - 5) // 2, (c // 2) % 2)
                transposes(base + NU - 2, 2)
                pv(base + NU - 3, 1, B - 2)
                transposes(base + NU - 1, 3)
                pv(base + NU - 2, 2, B - 1)
                back(B - 2, 0)
                pv(base + NU - 1, 3, B - 1)
                back(B - 1, 1)

            def out_projection(l):
                with pe.Fori(0, NG // 2) as i:
                    for par in range(2):
                        n = NG * l + 2 * i + par + 1
                        pe.wait_ge(o_cp, n)
                        for j in range(GB):
                            ins = tr(P[:, par, D * j:D * j + D], cS[:, par, j, :], ident)
                        ins.then_inc(o_T, 1)
                        pe.wait_ge(o_cT, n)
                        for j in range(GB):
                            ins = mm(P[:, 2 + par, D * j:D * j + D], cT[:, par, D * j:D * j + D], WO[:, l, :], start=True, stop=True)
                        ins.then_inc(o_wo, 1)

            def feed_forward(l):
                with pe.Fori(0, NG // 2) as i:
                    for par in range(2):
                        n = NG * l + 2 * i + par + 1
                        pe.wait_ge(m_n, GB * n)
                        for j in range(GB):
                            ins = tr(P[:, par, D * j:D * j + D], cS[:, par, j, :], ident)
                        ins.then_inc(m_T, 1)
                        pe.wait_ge(m_hT, n)
                        for f in range(NF):
                            pe.wait_ge(m_g, NF * (n - 1) + f)
                            mm(P[:, 2 + f, :], W1[:, l, 128 * f:128 * f + 128], cT[:, par, :], start=True, stop=True).then_inc(m_f, 1)
                        pe.wait_ge(m_g, NF * n)
                        for j in range(GB):
                            for f in range(NF):
                                ins = mm(P[:, 6 + par, D * j:D * j + D], gT[:, par, f, D * j:D * j + D], W2[:, l, f, :],
                                         start=(f == 0), stop=(f == NF - 1))
                        ins.then_inc(m_y, 1)

            for l in range(2):
                if l == 1:
                    pe.wait_ge(m_x, NG)
                project(l)
                pe.wait_ge(stacks_in, 7 * 16 * NG * (l + 1))
                if l == 0:
                    pe.wait_ge(mask_set, 3)
                    pe.wait_ge(zeros_set, 4)
                pe.wait_ge(p_v, NG * (l + 1))
                pe.wait_ge(p_qf, 4 * NG * (l + 1))
                attention(l)
                pe.wait_ge(a_ctx, B * (l + 1))
                out_projection(l)
                pe.wait_ge(o_res, NG * (l + 1))
                feed_forward(l)

            pe.wait_ge(m_x, 2 * NG)
            with pe.Fori(0, NG // 2) as i:
                for par in range(2):
                    n = 2 * i + par + 1
                    pe.wait_ge(r_cp, n)
                    for j in range(GB):
                        ins = tr(P[:, par, D * j:D * j + D], cS[:, par, j, :], ident)
                    ins.then_inc(r_T, 1)
                    pe.wait_ge(r_pl, n)
                    mm(P[0:R, 4 + par, 0:GB], W1T[:, :], pl[:, par, 0:GB], start=True, stop=True).then_inc(r_g1, 1)
                    pe.wait_ge(r_hT, n)
                    for j in range(GB):
                        ins = mm(P[:, 2 + par, D * j:D * j + D], cT[:, par, D * j:D * j + D], RM[:, :], start=True, stop=True)
                    ins.then_inc(r_m, 1)
                    pe.wait_ge(r_h1, n)
                    mm(P[:, 6 + par, 0:GB], W2G[:, :].to_broadcast([R, 128]), pl[0:R, par, 4:4 + GB], start=True, stop=True).then_inc(r_g2, 1)

        @block.scalar
        def _(act):
            af = nc.scalar.activation
            act.wait_ge(ld_const, 64)
            nc.scalar.activation(IDB[:, :], ident, ACT.Copy).then_inc(su_act, 1)
            af(DUM[:, 0:1], ident[:, 0:1], ACT.Sqrt)
            with act.Fori(0, R) as i:
                act.wait_ge(gs_dot, i + 1)
                af(gws[:, 0:2], P[:, 6, 0:2 * R].rearrange("p (m c) -> p m c", m=2)[:, :, 0], ACT.Sqrt).then_inc(gs_norm, 1)
            act.wait_ge(ld_vec, N_VEC)
            af(VRT[:, :].rearrange("n (h d r) -> n h d r", h=2, d=DH),
               VRP[:, :].rearrange("n (r h d) -> n h d r", h=2, d=DH), ACT.Copy).then_inc(vrp_turned, 1)
            act.wait_ge(ld_w, N_W)
            for l in range(2):
                for m in range(2):
                    af(WQK[:, l, m, :].rearrange("k (h d r) -> k h d r", h=2, d=DH),
                       WQ0[:, l, m, :].rearrange("k (r h d) -> k h d r", h=2, d=DH), ACT.Copy).then_inc(su_act, 1)
            act.wait_ge(su_dve, 6)
            af(EMB[:, 6, :], EMB[:, 5, :], ACT.Sin).then_inc(su_act, 1)
            act.wait_ge(su_act, 6)
            af(EMB[:, 7, :], EMB[:, 6, :], ACT.Silu).then_inc(su_dve, 1)
            act.wait_ge(su_pe, 8)
            act.wait_ge(su_dve, 7)
            for m in range(2):
                af(ADA[:, m, :], P[:, 7, 256 + B * m:256 + B * m + B], ACT.Identity, bias=COL[:, V_BADA + m:V_BADA + m + 1]).then_inc(su_act, 1)
            with act.Fori(0, NG // 2) as i:
                for par in range(2):
                    act.wait_ge(s_stage, 2 * i + par + 1)
                    af(X[:, ds((2 * i + par) * GB, GB), :], STG[:, par, :].rearrange("p (b y) -> p b y", b=GB), ACT.Relu).then_inc(s_x0, 1)

            def project(l):
                with act.Fori(0, NG // 2) as i:
                    for par in range(2):
                        g = 2 * i + par
                        n = NG * l + g + 1
                        act.wait_ge(p_T, n)
                        if l == 0:
                            for j in range(GB):
                                b = GB * g + j
                                af(xT[:, par, D * j:D * j + D], P[:, 0, D * j:D * j + D], ACT.Identity,
                                   bias=ADA[:, 1, ds(b, 1)], scale=ADA[:, 0, ds(b, 1)]).then_inc(p_xT, 1)
                        else:
                            af(xT[:, par, :], P[:, 0, :], ACT.Identity, bias=COL[:, V_BE1:V_BE1 + 1],
                               scale=COL[:, V_GA1:V_GA1 + 1]).then_inc(p_xT, 1)
                        for m in range(2):
                            act.wait_ge(p_q, 3 * (n - 1) + m + 1)
                            if m == 0:
                                act.wait_ge(p_q3, 2 * (n - 1))
                                if l == 0:
                                    act.wait_ge(parts_out[par], 128 * i)
                                else:
                                    act.wait_ge(parts_out[par], 128 * (NG // 2 + i))
                            for dst in (qf[:, par, m, :], qp[:, par, m, 0, :]):
                                af(dst, P[:, 2 + 2 * par + m, :], ACT.Identity, bias=BQK[:, 2 * l + m:2 * l + m + 1],
                                   scale=ISQ if m == 0 else 1.0).then_inc(p_qf, 1)
                        for m in range(2):
                            act.wait_ge(p_r, 2 * (n - 1) + m + 1)
                            af(qp[:, par, m, 1, :], qr[:, m, :], ACT.Copy).then_inc(p_q2, 1)

            def attention(l):
                def exps(u, c):
                    act.wait_ge(a_add if l else a_sub, u + 1)
                    af(E[:, c % 2, :, :], Sc[:, c % 2, :, :], ACT.Exp).then_inc(a_exp, 1)

                def evac(u, c):
                    act.wait_ge(a_T, u + 1)
                    af(pT[:, c % 2, :, :].rearrange("p h k -> p (h k)"), P[:, 4:6, :].rearrange("p a k -> p (a k)"), ACT.Copy).then_inc(a_pT, 1)

                def context(b, par):
                    act.wait_ge(a_pv, NU * l + 2 * b + 2)
                    af(cs[:, par, :], P[:, 6, 0:2 * S], ACT.Copy).then_inc(a_cs, 1)

                base = NU * l
                for c in range(4):
                    if c >= 2 or l:
                        act.wait_ge(a_T, base + c - 1)
                    exps(base + c, c)
                    if c >= 2 or l:
                        act.wait_ge(a_pv, base + c - 1)
                    evac(base + c, c)
                    if c == 2:
                        context(0, 0)
                with act.Fori(1, B // 2) as i:
                    for c in range(4):
                        u = base + 4 * i + c
                        act.wait_ge(a_T, u - 1)
                        exps(u, c)
                        act.wait_ge(a_pv, u - 1)
                        evac(u, c)
                        if c == 0:
                            act.wait_ge(a_ct, B * l + 2 * i - 2)
                            context(2 * i - 1, 1)
                        if c == 2:
                            act.wait_ge(a_ct, B * l + 2 * i - 1)
                            context(2 * i, 0)
                act.wait_ge(a_ct, B * (l + 1) - 2)
                context(B - 1, 1)

            def out_projection(l):
                with act.Fori(0, NG // 2) as i:
                    for par in range(2):
                        act.wait_ge(o_T, NG * l + 2 * i + par + 1)
                        af(cT[:, par, :], P[:, par, :], ACT.Copy).then_inc(o_cT, 1)

            def feed_forward(l):
                sc, bi, b1 = ((V_G2, V_BETA2, V_B1), (V_GA2, V_BE2, V_B1B))[l]
                with act.Fori(0, NG // 2) as i:
                    for par in range(2):
                        n = NG * l + 2 * i + par + 1
                        act.wait_ge(m_T, n)
                        af(cT[:, par, :], P[:, par, :], ACT.Identity, bias=COL[:, bi:bi + 1], scale=COL[:, sc:sc + 1]).then_inc(m_hT, 1)
                        for f in range(NF):
                            act.wait_ge(m_f, NF * (n - 1) + f + 1)
                            af(gT[:, par, f, :], P[:, 2 + f, :], ACT.Gelu if l else ACT.Gelu_apprx_sigmoid,
                               bias=COL[:, b1 + f:b1 + f + 1]).then_inc(m_g, 1)

            for l in range(2):
                project(l)
                attention(l)
                act.wait_ge(a_ctx, B * (l + 1))
                out_projection(l)
                act.wait_ge(o_res, NG * (l + 1))
                feed_forward(l)
            af(MOD[:, :], SAFE[:, :], ACT.Sigmoid).then_inc(su_act, 1)
            with act.Fori(0, NG // 2) as i:
                for par in range(2):
                    n = 2 * i + par + 1
                    act.wait_ge(r_T, n)
                    af(cT[:, par, :], P[:, par, :], ACT.Copy).then_inc(r_hT, 1)
                    act.wait_ge(r_g1, n)
                    af(pl[0:R, par, 4:4 + GB], P[0:R, 4 + par, 0:GB], ACT.Relu, bias=GB1[:, 0:1], scale=1.0 / S).then_inc(r_h1, 1)
                    act.wait_ge(r_g2, n)
                    af(pl[:, par, 8:8 + GB], P[:, 6 + par, 0:GB], ACT.Sigmoid, bias=GB2[:, 0:1]).then_inc(r_ba, 1)

        @block.vector
        def _(dve):
            v = nc.vector
            chain = [0]

            def link(ins, s=gs_chain):
                chain[0] += 1
                ins.then_inc(s, 1)
                dve.wait_ge(s, chain[0])

            dve.wait_ge(ld_const, 64)
            dve.wait_ge(ld_gs, 32)
            NS = 6
            with dve.Fori(0, R // 2) as i:
                for c in range(2):
                    at = 2 * NS * i + NS * c
                    src, dst = gsb[:, c, :, :], gsb[:, 1 - c, :, :]
                    dve.wait_ge(gs_norm, 2 * i + c + 1)
                    v.tensor_tensor(gcm[:, :, 0:R - 1], P[:, 6, 0:2 * R].rearrange("p (m c) -> p m c", m=2)[:, :, 1:R],
                                    CST[:, None, ds(C_GSM + 1 + 2 * i + c, R - 1)].to_broadcast([128, 2, R - 1]), ALU.mult).then_inc(gs_chain, 1)
                    v.tensor_scalar(gws[:, 2:4], gws[:, 0:2], GS_EPS, None, ALU.add).then_inc(gs_chain, 1)
                    dve.wait_ge(gs_chain, at + 2)
                    v.reciprocal(gws[:, 4:6], gws[:, 2:4]).then_inc(gs_chain, 1)
                    dve.wait_ge(gs_chain, at + 3)
                    v.tensor_tensor(dst[:, :, R - 1], src[:, :, 0], gws[:, 4:6], ALU.mult).then_inc(gs_chain, 1)
                    dve.wait_ge(gs_chain, at + 4)
                    v.tensor_tensor(gws[:, 6:8], dst[:, :, R - 1], gws[:, 4:6], ALU.mult).then_inc(gs_chain, 1)
                    dve.wait_ge(gs_chain, at + 5)
                    v.tensor_scalar(gws[:, 8:10], gws[:, 6:8], -1.0, None, ALU.mult).then_inc(gs_chain, 1)
                    dve.wait_ge(gs_chain, at + 6)
                    for m in range(2):
                        v.scalar_tensor_tensor(dst[:, m, 0:R - 1], gcm[:, m, 0:R - 1], gws[:, 8 + m:9 + m], src[:, m, 1:R],
                                               ALU.mult, ALU.add).then_inc(gs_step, 1)
            chain[0] = NS * R
            dve.wait_ge(su_pe, 1)
            v.tensor_copy(RWT[:, :], P[0:R, 6, 256:384]).then_inc(gs_norm, 1)
            v.tensor_copy(UT[0:R, :, :], P[0:R, 6, 0:256].rearrange("p (m d) -> p m d", m=2)).then_inc(su_dve, 1)
            dve.wait_ge(su_pe, 3)
            v.tensor_copy(W1T[:, :], P[:, 7, 0:R]).then_inc(gs_norm, 1)
            v.tensor_copy(COL[:, :], P[:, 7, 64:64 + V_ALL]).then_inc(gs_norm, 1)
            for m in range(2):
                v.tensor_scalar(BQK[:, m:4:2], P[:, 7, 128 + m:132:2], 1.0 if m else ISQ, None, ALU.mult).then_inc(gs_norm, 1)
            v.tensor_copy(GRT[:, :, :], P[:, 5, 0:384].rearrange("p (m d) -> p m d", m=3)).then_inc(gs_norm, 1)
            dve.wait_ge(gs_norm, R + 6)
            link(v.tensor_scalar(COL[:, V_BADA:V_BADA + 1], COL[:, V_BADA:V_BADA + 1], 1.0, None, ALU.add))
            dve.wait_ge(su_pe, 4)
            v.tensor_copy(BST, P[:, 4, 0:128]).then_inc(su_dve, 1)
            dve.wait_ge(su_pe, 5)
            v.tensor_copy(BBm, P[:, 4, 128:128 + R]).then_inc(su_dve, 1)
            dve.wait_ge(su_pe, 6)
            v.tensor_copy(BBTt[:, :], P[0:R, 4, 256:384]).then_inc(su_dve, 1)
            dve.wait_ge(su_pe, 7)
            v.tensor_copy(RM[:, :], P[:, 4, 384:512]).then_inc(su_dve, 1)
            dve.wait_ge(ld_vec, N_VEC)
            dve.wait_ge(ld_row, N_ROW)
            link(v.tensor_copy(EMB[:, 0, :], TI))
            link(v.tensor_scalar(EMB[:, 1, :], EMB[:, 0, :], 40.0, None, ALU.mult))
            link(v.tensor_scalar(EMB[:, 2, :], EMB[:, 1, :], CST[:, C_FREQ:C_FREQ + 1], None, ALU.mult))
            link(v.tensor_scalar(EMB[:, 3, :], EMB[:, 2, :], float(1 / (2 * np.pi)), CST[:, C_QUART:C_QUART + 1], ALU.mult, ALU.add))
            link(v.tensor_scalar(EMB[:, 3, :], EMB[:, 3, :], 12582912.0, None, ALU.add))
            link(v.tensor_scalar(EMB[:, 3, :], EMB[:, 3, :], -12582912.0, None, ALU.add))
            c1 = 6.28125
            c2 = float(np.float32(2 * np.pi - c1))
            c3 = float(np.float32(2 * np.pi - c1 - float(np.float32(2 * np.pi - c1))))
            link(v.scalar_tensor_tensor(EMB[:, 4, :], EMB[:, 3, :], -c1, EMB[:, 2, :], ALU.mult, ALU.add))
            link(v.scalar_tensor_tensor(EMB[:, 4, :], EMB[:, 3, :], -c2, EMB[:, 4, :], ALU.mult, ALU.add))
            link(v.scalar_tensor_tensor(EMB[:, 4, :], EMB[:, 3, :], -c3, EMB[:, 4, :], ALU.mult, ALU.add))
            link(v.tensor_scalar(EMB[:, 4, :], EMB[:, 4, :], CST[:, C_PHASE:C_PHASE + 1], None, ALU.add))
            v.tensor_scalar(EMB[:, 5, :], EMB[:, 4, :], float(np.float32(3.1415925)), float(np.float32(-3.1415925)), ALU.min, ALU.max).then_inc(su_dve, 1)
            link(v.tensor_tensor(CB[:, 0, :], CB[:, 0, :], CB[:, 1, :], ALU.add))

            with dve.Fori(0, NG // 2) as i:
                for par in range(2):
                    n = 2 * i + par + 1
                    f4 = fS[:, par, :].rearrange("p (b y) -> p b y", b=GB)

                    def four(t):
                        return t.rearrange("p (b y) -> p b y", b=GB)

                    dve.wait_ge(f_landed[par], 16 * (i + 1))
                    v.tensor_tensor(four(AF[:, par, :]), f4, GRID[:, 0:1, :].to_broadcast([128, GB, D]), ALU.mult).then_inc(s_prod, 1)
                    v.tensor_tensor(four(BFv[:, par, :]), f4, GRID[:, 2:3, :].to_broadcast([128, GB, D]), ALU.mult).then_inc(s_prod, 1)
                    dve.wait_ge(s_fT, n)
                    for m in (2, 0, 1):
                        v.tensor_tensor(four(fT[:, par, m, :]), four(P[:, par, :]), GRT[:, m:m + 1, :].to_broadcast([128, GB, D]), ALU.mult).then_inc(s_fTp, 1)
                    dve.wait_ge(s_H, n)
                    dve.wait_ge(s_prod, 2 * n)
                    v.tensor_tensor(AF[:, par, :], AF[:, par, :], P[:, 2 + par, :], ALU.subtract).then_inc(s_U, 1)
                    dve.wait_ge(s_df, n)
                    dve.wait_ge(s_x0, 2 * i)
                    for j in range(GB):
                        ins = v.scalar_tensor_tensor(STG[:, par, D * j:D * j + D], P[:, 4 + par, D * j:D * j + D],
                                                     DTB[:, ds(GB * (2 * i + par) + j, 1)], fS[:, par, D * j:D * j + D], ALU.mult, ALU.add)
                    ins.then_inc(s_stage, 1)

            newton_at = [0]

            def rstd(k):
                def nl(ins):
                    newton_at[0] += 1
                    ins.then_inc(newton, 1)
                    dve.wait_ge(newton, newton_at[0])

                dve.wait_ge(stats_done, B * k)
                me, mo, se, so = ST6[:, :, 1], ST6[:, :, 4], ST6[:, :, 2], ST6[:, :, 5]
                nl(v.tensor_tensor(MV[:, :, 0], me, mo, ALU.add))
                nl(v.tensor_tensor(MV[:, :, 1], me, mo, ALU.subtract))
                nl(v.tensor_tensor(RS[:, :], se, so, ALU.add))
                nl(v.scalar_tensor_tensor(MV[:, :, 1], MV[:, :, 1], 0.25, MV[:, :, 1], ALU.mult, ALU.mult))
                nl(v.tensor_scalar(RS[:, :], RS[:, :], 1.0 / D, LN_EPS, ALU.mult, ALU.add))
                nl(v.tensor_tensor(NT[:, :], RS[:, :], MV[:, :, 1], ALU.add))
                nl(v.tensor_scalar(NI[:, :], NT[:, :].bitcast(I32), 1, None, ALU.arith_shift_right))
                nl(v.tensor_scalar(NY[:, :].bitcast(I32), NI[:, :], -1.0, float(MAGIC), ALU.mult, ALU.add))
                for _ in range(4):
                    nl(v.tensor_tensor(RS[:, :], NY[:, :], NY[:, :], ALU.mult))
                    nl(v.tensor_tensor(RS[:, :], RS[:, :], NT[:, :], ALU.mult))
                    nl(v.tensor_scalar(RS[:, :], RS[:, :], -0.5, 1.5, ALU.mult, ALU.add))
                    nl(v.tensor_tensor(NY[:, :], NY[:, :], RS[:, :], ALU.mult))
                nl(v.scalar_tensor_tensor(NMR[:, :], MV[:, :, 0], -0.5, NY[:, :], ALU.mult, ALU.mult))

            def stats(k, src):
                with dve.Fori(0, B) as b:
                    v.bn_stats(ST6[:, ds(b, 1), :].rearrange("p o s -> p (o s)"), src[:, ds(b, 1), :].rearrange("p o d -> p (o d)")).then_inc(stats_done, 1)

            def normed(dst, src, b, done):
                v.tensor_scalar(dst, src[:, ds(b, 1), :].rearrange("p o d -> p (o d)"), NY[:, ds(b, 1)], NMR[:, ds(b, 1)], ALU.mult, ALU.add).then_inc(done, 1)

            def project(l):
                with dve.Fori(0, NG // 2) as i:
                    for par in range(2):
                        g = 2 * i + par
                        n = NG * l + g + 1
                        for j in range(GB):
                            normed(xn[:, par, j, :], X, GB * g + j, p_norm)
                        if l == 0:
                            dve.wait_ge(p_back, n)
                            v.tensor_tensor(X[:, ds(GB * g, GB), :], P[:, 1, :].rearrange("p (b y) -> p b y", b=GB),
                                            BOB[:, 0:1, :].to_broadcast([128, GB, D]), ALU.add).then_inc(p_nat, 1)
                        for m in range(2):
                            dve.wait_ge(p_qf, 4 * (n - 1) + 2 * m + 2)
                            v.tensor_tensor(qr[:, m, :], qf[:, par, m, :], qp[:, par, m, 0, :], ALU.subtract).then_inc(p_r, 1)
                        dve.wait_ge(p_q, 3 * n)
                        v.tensor_tensor(V[:, ds(GB * g, GB), :], P[:, 6 + par, :].rearrange("p (b y) -> p b y", b=GB),
                                        BVB[:, l:l + 1, :].to_broadcast([128, GB, D]), ALU.add).then_inc(p_v, 1)
                        for m in range(2):
                            dve.wait_ge(p_q2, 2 * (n - 1) + m + 1)
                            v.tensor_tensor(qp[:, par, m, 2, :], qr[:, m, :], qp[:, par, m, 1, :], ALU.subtract).then_inc(p_q3, 1)

            def attention(l):
                def unit(u, c, i):
                    q = c % 2
                    ps = P[:, 2 * q:2 * q + 2, :].rearrange("p a (h k) -> p (a h) k", k=S)
                    dve.wait_ge(a_qk, u + 1)
                    if l == 0:
                        dve.wait_ge(fs_landed[c // 2], 32 * (i + 1))
                        v.tensor_tensor(Sc[:, q, :, :], ps, FS[:, c // 2, HU * q:HU * q + HU, :], ALU.add).then_inc(a_add, 1)
                        dve.wait_ge(a_add, u + 1)
                        v.tensor_reduce(MX[:, q, :], Sc[:, q, :, :], AX.X, ALU.max).then_inc(a_max, 1)
                    else:
                        v.tensor_reduce(MX[:, q, :], ps, AX.X, ALU.max).then_inc(a_max, 1)
                        dve.wait_ge(a_max, u + 1)
                        v.tensor_tensor(Sc[:, q, :, :], ps, MX[:, q, :, None].to_broadcast([128, HU, S]), ALU.subtract).then_inc(a_add, 1)

                def context(b):
                    n = B * l + b
                    ct = P[:, 7, 0:2 * S].rearrange("p (h e) -> p h e", h=H)
                    dve.wait_ge(a_ct, n + 1)
                    v.reciprocal(RSUM[:, :], ct[:, :, DH]).then_inc(a_rs, 1)
                    dve.wait_ge(a_rs, n + 1)
                    dst = CTX[:, b, :] if isinstance(b, int) else CTX[:, ds(b, 1), :].rearrange("p o d -> p (o d)")
                    v.tensor_tensor(dst.rearrange("p (h d) -> p h d", h=H), ct[:, :, 0:DH],
                                    RSUM[:, :, None].to_broadcast([128, H, DH]), ALU.mult).then_inc(a_ctx, 1)

                base = NU * l
                for c in range(4):
                    if c >= 2 or l:
                        dve.wait_ge(a_exp, base + c - 1)
                    unit(base + c, c, 0)
                with dve.Fori(1, B // 2) as i:
                    for c in range(4):
                        u = base + 4 * i + c
                        dve.wait_ge(a_exp, u - 1)
                        unit(u, c, i)
                        if c % 2:
                            context(2 * i + (c - 5) // 2)
                context(B - 2)
                context(B - 1)

            def out_projection(l):
                dst = V if l else X
                with dve.Fori(0, NG // 2) as i:
                    for par in range(2):
                        g = 2 * i + par
                        n = NG * l + g + 1
                        v.tensor_copy(cS[:, par, :, :], CTX[:, ds(GB * g, GB), :]).then_inc(o_cp, 1)
                        dve.wait_ge(o_wo, n)
                        ps = P[:, 2 + par, :].rearrange("p (b y) -> p b y", b=GB)
                        if l == 0:
                            v.tensor_tensor(X[:, ds(GB * g, GB), :], ps, X[:, ds(GB * g, GB), :], ALU.add).then_inc(o_res, 1)
                        else:
                            v.tensor_tensor(V[:, ds(GB * g, GB), :], ps, BOB[:, 1:2, :].to_broadcast([128, GB, D]), ALU.add).then_inc(o_bo, 1)
                            dve.wait_ge(o_bo, g + 1)
                            v.tensor_tensor(V[:, ds(GB * g, GB), :], V[:, ds(GB * g, GB), :], X[:, ds(GB * g, GB), :], ALU.add).then_inc(o_res, 1)

            def feed_forward(l):
                x1 = V if l else X
                with dve.Fori(0, NG // 2) as i:
                    for par in range(2):
                        g = 2 * i + par
                        n = NG * l + g + 1
                        grp = ds(GB * g, GB)
                        for j in range(GB):
                            normed(cS[:, par, j, :], x1, GB * g + j, m_n)
                        dve.wait_ge(m_y, n)
                        v.tensor_tensor(yS[:, par, :, :], P[:, 6 + par, :].rearrange("p (b y) -> p b y", b=GB),
                                        B2B[:, l:l + 1, :].to_broadcast([128, GB, D]), ALU.add).then_inc(m_t, 1)
                        dve.wait_ge(m_t, n)
                        if l == 0:
                            v.tensor_tensor(X[:, grp, :], yS[:, par, :, :], X[:, grp, :], ALU.add).then_inc(m_x, 1)
                        else:
                            v.tensor_tensor(zS[:, par, :, :], yS[:, par, :, :], V[:, grp, :], ALU.add).then_inc(m_u, 1)
                            dve.wait_ge(m_u, g + 1)
                            v.tensor_tensor(yS[:, par, :, :], zS[:, par, :, :], X[:, grp, :], ALU.subtract).then_inc(m_d, 1)
                            dve.wait_ge(m_d, g + 1)
                            for j in range(GB):
                                xb = X[:, ds(GB * g + j, 1), :].rearrange("p o d -> p (o d)")
                                ins = v.scalar_tensor_tensor(xb, yS[:, par, j, :], GATE[:, ds(GB * g + j, 1)], xb, ALU.mult, ALU.add)
                            ins.then_inc(m_x, 1)

            for l in range(2):
                dve.wait_ge(*((s_x0, NG) if l == 0 else (m_x, NG)))
                stats(2 * l, X)
                rstd(2 * l + 1)
                project(l)
                dve.wait_ge(p_q3, 2 * NG * (l + 1))
                dve.wait_ge(parts_out[0], 256 * (l + 1))
                dve.wait_ge(parts_out[1], 256 * (l + 1))
                attention(l)
                dve.wait_ge(a_ctx, B * (l + 1))
                out_projection(l)
                dve.wait_ge(o_res, NG * (l + 1))
                stats(2 * l + 1, V if l else X)
                rstd(2 * l + 2)
                feed_forward(l)

            dve.wait_ge(m_x, 2 * NG)
            dve.wait_ge(su_act, 9)
            with dve.Fori(0, NG // 2) as i:
                for par in range(2):
                    g = 2 * i + par
                    v.tensor_copy(cS[:, par, :, :], X[:, ds(GB * g, GB), :]).then_inc(r_cp, 1)
                    dve.wait_ge(r_hT, g + 1)
                    v.tensor_reduce(pl[:, par, 0:GB], cT[:, par, :].rearrange("p (b y) -> p b y", b=GB), AX.X, ALU.add).then_inc(r_pl, 1)
                    dve.wait_ge(r_m, g + 1)
                    v.tensor_tensor(yS[:, par, :, :], P[:, 2 + par, :].rearrange("p (b y) -> p b y", b=GB),
                                    CB[:, 0:1, :].to_broadcast([128, GB, D]), ALU.add).then_inc(r_t, 1)
                    dve.wait_ge(r_ba, g + 1)
                    v.tensor_tensor(pl[:, par, 12:12 + GB], pl[:, par, 8:8 + GB], MOD[:, ds(GB * g, GB)], ALU.mult).then_inc(r_st, 1)
                    dve.wait_ge(r_t, g + 1)
                    dve.wait_ge(r_st, g + 1)
                    dve.wait_ge(r_out, 32 * i)
                    for j in range(GB):
                        ins = v.scalar_tensor_tensor(zS[:, par, j, :], yS[:, par, j, :], pl[:, par, 12 + j:13 + j], cS[:, par, j, :], ALU.mult, ALU.add)
                    ins.then_inc(r_o, 1)


_INS = ['x', 'condB_dt', 'itok_B_34_63', 'fside_Bx16xSxS_0', 'condB_gatescore', 'condB_safetyscore', 'mask_Bx1xSxS_bk0',
        'L0_cond_A_grid', 'L0_cond_B_grid'] + \
       ['L1_cond_' + n for n in ('W_ada', 'b_ada', 'Wq', 'bq', 'Wk', 'bk', 'Wv', 'bv', 'Wo', 'bo', 'W1', 'b1', 'W2', 'b2', 'g2', 'beta2')] + \
       ['L2_cond_' + n for n in ('Wq', 'bq', 'Wk', 'bk', 'Wv', 'bv', 'Wo', 'bo', 'W1', 'b1', 'W2', 'b2', 'gamma1', 'beta1', 'gamma2', 'beta2')] + \
       ['L3_cond_' + n for n in ('U', 'V', 'safety_bias', 'gate_w1', 'gate_b1', 'gate_w2', 'gate_b2', 'resp_w', 'resp_b')]


def kernel(**inputs):
    import numpy as _np
    import concourse.bacc as _bacc
    from concourse import mybir as _mybir
    from concourse.bass_utils import run_bass_kernel_spmd as _run

    nc = _bacc.Bacc("TRN2", target_bir_lowering=False, num_devices=1)
    arrays, args = {}, {}
    host = {name: _np.ascontiguousarray(inputs[name]) for name in _INS}
    host["mask_Bx1xSxS_bk0"] = host["mask_Bx1xSxS_bk0"].view(_np.int32)
    host["consts"] = constants()
    for name, arr in host.items():
        arrays[f"in_{name}"] = arr
        args[name] = nc.dram_tensor(f"in_{name}", arr.shape, _mybir.dt.from_np(arr.dtype), kind="ExternalInput").ap()
    out = nc.dram_tensor("out_0", (B, S, D), F32, kind="ExternalOutput").ap()
    build(nc, args, out)
    r = _run(nc, [arrays], core_ids=[0])
    return r.results[0]["out_0"]
```

```python
from contextlib import ExitStack

import numpy as np
import concourse.bass as bass
from concourse import mybir

F32 = mybir.dt.float32
BF16 = mybir.dt.bfloat16
I32 = mybir.dt.int32
U32 = mybir.dt.uint32
U8 = mybir.dt.uint8
ALU = mybir.AluOpType
ACT = mybir.ActivationFunctionType
AX = mybir.AxisListType
ds = bass.ds

B, S, D, H, DH, FF = 16, 128, 128, 16, 8, 512
GB = 4
NG = B // GB
GW = GB * D
PR = H // 2
HU = H // 2
UW = HU * S
NU = 2 * B
R = 32
NF = FF // 128
SLOTS = 8
HROWS = SLOTS * DH
TOK = B * S
LN_EPS = 1e-5
GS_EPS = 1e-8
NEG = -1e30
ISQ = float(DH) ** -0.5
MAGIC = 0x5F3759DF

C_ID, C_PD1, C_ND1, C_HD2, C_CAUS, C_FREQ, C_PHASE, C_QUART, C_GSM = 0, 128, 256, 384, 512, 640, 641, 642, 643
C_ALL = C_GSM + 2 * R

V_BADA, V_G2, V_BETA2, V_B1, V_GA1, V_BE1, V_GA2, V_BE2, V_B1B = 0, 2, 3, 4, 8, 9, 10, 11, 12
V_ALL = 16


def constants():
    c = np.zeros((128, C_ALL), np.float32)
    n = S
    d1 = np.zeros((n, n), np.float32)
    d2 = np.zeros((n, n), np.float32)
    for i in range(1, n - 1):
        d1[i, i - 1], d1[i, i + 1] = -0.5, 0.5
        d2[i, i - 1], d2[i, i], d2[i, i + 1] = 1.0, -2.0, 1.0
    d1[0, :3] = [-1.5, 2.0, -0.5]
    d1[-1, -3:] = [0.5, -2.0, 1.5]
    d2[0, :4] = [2.0, -5.0, 4.0, -1.0]
    d2[-1, -4:] = [-1.0, 4.0, -5.0, 2.0]
    c[:, C_ID:C_ID + 128] = np.eye(128)
    c[:, C_PD1:C_PD1 + 128] = d1.T
    c[:, C_ND1:C_ND1 + 128] = -d1.T
    c[:, C_HD2:C_HD2 + 128] = 0.5 * d2.T
    c[:, C_CAUS:C_CAUS + 128] = np.where(np.tril(np.ones((n, n), bool)), 0.0, NEG)
    half = D // 2
    freq = np.exp(np.arange(half, dtype=np.float32) * np.float32(-np.log(10000.0) / (half - 1)))
    c[:, C_FREQ] = np.concatenate([freq, freq])
    c[half:, C_PHASE] = np.pi / 2
    c[half:, C_QUART] = 0.25
    c[:, C_GSM:C_GSM + R] = 1.0
    return c


def build(nc, a, out):
    ctx = ExitStack()
    with ctx:
        def sb(name, shape, dt=F32):
            return ctx.enter_context(nc.sbuf_tensor(name, shape, dt))

        def sem(name):
            return ctx.enter_context(nc.semaphore(name))

        X = sb("X", [128, B, D])
        V = sb("V", [128, B, D])
        CTX = sb("CTX", [128, B, D])
        QS = sb("QS", [128, PR, TOK], BF16)
        KS = sb("KS", [128, PR, 2, TOK], BF16)
        FS = sb("FS", [128, 2, H, S])
        VP = sb("VP", [128, 2, H, 32])
        MSK = sb("MSK", [128, B, S], BF16)
        CST = sb("CST", [128, C_ALL])
        IDB = sb("IDB", [128, 128], BF16)
        CAUS = sb("CAUS", [128, 128], BF16)
        WQK = sb("WQK", [128, 2, 2, D])
        WV = sb("WV", [128, 2, D])
        WO = sb("WO", [128, 2, D])
        W1 = sb("W1", [128, 2, FF])
        W2 = sb("W2", [128, 2, NF, D])
        VR = sb("VR", [32, 128])
        VRP = sb("VRP", [4, 128])
        VRT = sb("VRT", [4, 128])
        COL = sb("COL", [128, V_ALL])
        BQK = sb("BQK", [128, 4])
        BVB = sb("BVB", [128, 2, D])
        BOB = sb("BOB", [128, 2, D])
        B2B = sb("B2B", [128, 2, D])
        CB = sb("CB", [128, 2, D])
        DTB = sb("DTB", [128, B])
        GATE = sb("GATE", [128, B])
        SAFE = sb("SAFE", [128, B])
        MOD = sb("MOD", [128, B])
        GB2 = sb("GB2", [128, 1])
        ADA = sb("ADA", [128, 2, B])
        MV = sb("MV", [128, B, 2])
        ST6 = sb("ST6", [128, B, 6])
        RS = sb("RS", [128, B])
        NMR = sb("NMR", [128, B])
        NT = sb("NT", [128, B])
        NI = sb("NI", [128, B], I32)
        NY = sb("NY", [128, B])
        MX = sb("MX", [128, 4, HU])
        RSUM = sb("RSUM", [128, H])
        RM = sb("RM", [128, D])
        W1T = sb("W1T", [128, R])
        W2G = sb("W2G", [R, 1])
        GB1 = sb("GB1", [R, 1])
        DUM = sb("DUM", [128, 8])
        SM = sb("SM", [128, 64])
        WORK = sb("WORK", [128, 8320])

        P = ctx.enter_context(nc.psum_tensor("P", [128, 8, 512], F32))
        QKD = nc.dram_tensor("qk_parts", (2, 2, 3, 128, TOK), BF16, kind="Internal").ap()

        ident = CST[:, C_ID:C_ID + 128]
        pD1T = CST[:, C_PD1:C_PD1 + 128]
        nD1T = CST[:, C_ND1:C_ND1 + 128]
        hD2T = CST[:, C_HD2:C_HD2 + 128]

        def work(at, *shape, dt=F32):
            n = int(np.prod(shape))
            if dt == BF16:
                n //= 2
            v = WORK[:, at:at + n]
            if dt != F32:
                v = v.bitcast(dt)
            names = " ".join(f"d{i}" for i in range(len(shape)))
            if len(shape) == 1:
                return v
            return v.rearrange(f"p ({names}) -> p {names}", **{f"d{i}": s for i, s in enumerate(shape)})

        def early(at, *shape, buf=V[:, :, :].rearrange("p b d -> p (b d)")):
            v = buf[:, at:at + int(np.prod(shape))]
            if len(shape) == 1:
                return v
            names = " ".join(f"d{i}" for i in range(len(shape)))
            return v.rearrange(f"p ({names}) -> p {names}", **{f"d{i}": n for i, n in enumerate(shape)})

        EMB = early(0, 8, B)
        TI = early(128, B).bitcast(I32)
        WADA = early(144, 2 * D)
        LW = early(400, D)
        WQ0 = early(528, 2, 2, D)
        MU8 = early(1040, B * S // 4).bitcast(U8).rearrange("q (b k) -> q b k", b=B)
        GRID = sb("GRID", [128, 5, D])
        GRT = sb("GRT", [128, 3, D])
        gsb = sb("gsb", [128, 2, 2, R])
        gcm = sb("gcm", [128, 2, R])
        gws = sb("gws", [128, 16])
        gpr = sb("gpr", [128, 2, R - 1])
        LR = sb("LR", [128, R])
        late = FS[:, :, :, :].rearrange("p a h k -> p (a h k)")
        UT = early(0, 2, D, buf=late)
        BST = early(256, D, buf=late)
        BBm = early(384, R, buf=late)
        FS2 = CTX[:, :, :].rearrange("p b d -> p (b d)").rearrange("p (h k) -> p h k", h=H)
        BBTt = sb("BBTt", [R, D])
        RWT = sb("RWT", [R, D])
        fS = work(0, NG, GW)
        fT = work(2048, 2, 3, GW)
        AF = work(5120, 2, GW)
        BFv = work(6144, 2, GW)
        xn = work(0, 2, GB, D)
        xT = work(1024, 2, GW)
        qf = work(2048, 2, 2, GW)
        qr = work(4096, 2, GW)
        qp = work(5120, 2, 2, 3, GW, dt=BF16)
        SE = work(0, 4, HU, S)
        pT = work(4096, 2, HU, S)
        cs = work(6144, 2, 2 * S)
        cS = work(0, 2, GB, D)
        cT = work(1024, 2, GW)
        gT = work(2048, 2, NF, GW)
        yS = work(6144, 2, GB, D)
        zS = work(7168, 2, GB, D)
        pl = work(8192, 2, 16)

        ld_const, ld_vec, ld_w, ld_gs, ld_mask, ld_row = (sem(f"ld_{n}") for n in ("const", "vec", "w", "gs", "mask", "row"))
        f_landed = [sem(f"f_landed{g}") for g in range(NG)]
        fs_landed = [sem("fs_landed0"), sem("fs_landed1"), sem("fs_landed_third")]
        gs_dot, gs_norm, gs_step, gs_chain = sem("gs_dot"), sem("gs_norm"), sem("gs_step"), sem("gs_chain")
        su_pe, su_dve, su_act = sem("setup_pe"), sem("setup_dve"), sem("setup_act")
        zeros_set, mask_set, vrp_turned = sem("zeros_set"), sem("mask_set"), sem("biases_turned")
        s_prod, s_fT, s_fTp, s_H, s_U, s_df, s_stage, s_x0 = (sem(n) for n in (
            "stencil_products", "f_transposed", "fT_products", "H_ready", "U_ready", "df_ready", "stage_ready", "x_ready"))
        stats_st, stats_done, newton = sem("stats_st"), sem("stats_done"), sem("newton")
        p_norm, p_T, p_xT, p_back, p_nat, p_q, p_qf, p_r, p_q2, p_q3, p_v = (sem(n) for n in (
            "normed", "transposed", "xT_ready", "x_back", "x_natural", "qkv_ready", "qk_evacuated", "qk_rest", "qk_second",
            "qk_third", "v_ready"))
        parts_out = [sem("parts_out0"), sem("parts_out1")]
        stacks_in = sem("stacks_in")
        rm_pe, rm_dve, su_chain, gs_mask, gs_inv, gs_pool = sem("resp_matrix_pe"), sem("resp_matrix_dve"), sem("setup_chain"), sem("gs_masked"), sem("gs_inverse"), sem("gs_pool")
        gs_log, ada_in, grt_ready = sem("gs_log"), sem("ada_weights_used"), sem("grt_ready")
        a_qk, a_add, a_max, a_sub, a_exp, a_T, a_pT, a_pv, a_cs, a_ct, a_rs, a_ctx, a_vp = (sem(n) for n in (
            "scores_ready", "biased", "max_ready", "shifted", "exp_done", "probs_transposed", "probsT_ready", "pv_done",
            "ctxT_copied", "ctx_back", "rowsum_inv", "ctx_ready", "v_padded"))
        o_cp, o_T, o_cT, o_wo, o_res, o_bo = (sem(n) for n in (
            "ctx_staged", "ctx_T", "ctxT_ready", "wo_done", "x1_ready", "x1_bias"))
        m_n, m_T, m_hT, m_f, m_g, m_y, m_t, m_u, m_d, m_x = (sem(n) for n in (
            "ff_normed", "ff_T", "ff_hT", "ff_up", "ff_gelu", "ff_down", "ff_biased", "ff_sum", "ff_diff", "ff_x"))
        r_cp, r_T, r_hT, r_pl, r_m, r_g1, r_h1, r_g2, r_ba, r_st, r_t, r_o, r_out = (sem(n) for n in (
            "l3_staged", "l3_T", "l3_hT", "l3_pooled", "l3_resp", "l3_gate1", "l3_h1", "l3_gate2", "l3_base", "l3_strength",
            "l3_biased", "l3_out", "out_written"))

        GS = R // 2
        N_CONST = 5 * 16
        N_VEC = 16 * 16
        N_STACK = 12 * 16
        N_GS = 3 * 16
        N_W = 14 * 16
        N_ROW = 11 * 16
        block = ctx.enter_context(nc.Block())

        @block.sync
        def _(sp):
            sp.dma_start(CST[:, :], a["consts"]).then_inc(ld_const, 16)
            sp.dma_start(GRID[:, 0:2, :], a["L0_cond_A_grid"].rearrange("c x y -> x c y")).then_inc(ld_const, 16)
            sp.dma_start(GRID[:, 2:5, :], a["L0_cond_B_grid"].rearrange("c x y -> x c y")).then_inc(ld_const, 16)
            sp.dma_start(DTB[:, :], a["condB_dt"][None, :].to_broadcast([128, B])).then_inc(ld_const, 16)
            sp.dma_start(TI, a["itok_B_34_63"][None, :].to_broadcast([128, B])).then_inc(ld_const, 16)
            for g in range(NG):
                sp.dma_start(fS[:, g, :].rearrange("p (b y) -> p b y", b=GB),
                             a["x"][GB * g:GB * g + GB].rearrange("b x y -> x b y")).then_inc(f_landed[g], 16)
            vecs = [("L1_cond_b_ada", V_BADA, 2), ("L1_cond_g2", V_G2, 1), ("L1_cond_beta2", V_BETA2, 1), ("L1_cond_b1", V_B1, 4),
                    ("L2_cond_gamma1", V_GA1, 1), ("L2_cond_beta1", V_BE1, 1), ("L2_cond_gamma2", V_GA2, 1),
                    ("L2_cond_beta2", V_BE2, 1), ("L2_cond_b1", V_B1B, 4)]
            for name, at, n in vecs:
                sp.dma_start(VR[at:at + n, :], a[name].rearrange("(n d) -> n d", n=n)).then_inc(ld_vec, 16)
            sp.dma_start(GB1[:, :], a["L3_cond_gate_b1"][:, None], allow_slow_non_contiguous=True).then_inc(ld_vec, 16)
            for i, name in enumerate(("L1_cond_bq", "L1_cond_bk", "L2_cond_bq", "L2_cond_bk")):
                sp.dma_start(VRP[i:i + 1, :], a[name][None, :]).then_inc(ld_vec, 16)
            sp.dma_start(WADA, a["L1_cond_W_ada"]).then_inc(ld_vec, 16)
            sp.dma_start(LW[0:R, :], a["L3_cond_gate_w1"]).then_inc(ld_vec, 16)
            for l in range(2):
                n = f"L{l + 1}_cond_"
                sp.dma_start(WQ0[:, l, 0, :], a[n + "Wq"]).then_inc(ld_w, 16)
                sp.dma_start(WQ0[:, l, 1, :], a[n + "Wk"]).then_inc(ld_w, 16)
                sp.dma_start(WV[:, l, :], a[n + "Wv"]).then_inc(ld_w, 16)
                sp.dma_start(WO[:, l, :], a[n + "Wo"]).then_inc(ld_w, 16)
                sp.dma_start(W1[:, l, :], a[n + "W1"]).then_inc(ld_w, 16)
                sp.dma_start(W2[:, l, :, :], a[n + "W2"].rearrange("(c f) d -> f c d", c=NF)).then_inc(ld_w, 16)
            sp.dma_start(W2G[:, :], a["L3_cond_gate_w2"].rearrange("a b -> b a"), allow_slow_non_contiguous=True).then_inc(ld_w, 16)
            sp.dma_start(GB2[:, :], a["L3_cond_gate_b2"][None, :].to_broadcast([128, 1])).then_inc(ld_w, 16)
            for l in range(2):
                n = f"L{l + 1}_cond_"
                sp.dma_start(BVB[:, l, :], a[n + "bv"][None, :].to_broadcast([128, D])).then_inc(ld_row, 16)
                sp.dma_start(BOB[:, l, :], a[n + "bo"][None, :].to_broadcast([128, D])).then_inc(ld_row, 16)
                sp.dma_start(B2B[:, l, :], a[n + "b2"][None, :].to_broadcast([128, D])).then_inc(ld_row, 16)
            sp.dma_start(CB[:, 0, :], a["L3_cond_resp_b"][None, :].to_broadcast([128, D])).then_inc(ld_row, 16)
            sp.dma_start(CB[:, 1, :], a["L3_cond_safety_bias"][None, :].to_broadcast([128, D])).then_inc(ld_row, 16)
            sp.dma_start(GATE[:, :], a["condB_gatescore"][None, :].to_broadcast([128, B])).then_inc(ld_row, 16)
            sp.dma_start(SAFE[:, :], a["condB_safetyscore"][None, :].to_broadcast([128, B])).then_inc(ld_row, 16)
            sp.dma_start(MU8.bitcast(I32), a["mask_Bx1xSxS_bk0"].rearrange("b o q k -> q b (o k)")).then_inc(ld_row, 16)
            for b, dst in enumerate((FS[:, 0, :, :], FS[:, 1, :, :], FS2)):
                for rows in (slice(0, 64), slice(64, 128)):
                    sp.dma_start(dst[rows], a["fside_Bx16xSxS_0"][b, :, rows, :].rearrange("h q k -> q h k")).then_inc(fs_landed[b], 16)
            sp.dma_start(gsb[:, 0, 0, :], a["L3_cond_U"]).then_inc(ld_gs, 16)
            sp.dma_start(gsb[:, 0, 1, :], a["L3_cond_V"]).then_inc(ld_gs, 16)
            sp.dma_start(LR[:, :], a["L3_cond_resp_w"]).then_inc(ld_gs, 16)
            def stacks(l):
                for g in range(NG):
                    par, cols = g % 2, slice(g * GW, (g + 1) * GW)
                    sp.wait_ge(p_q3, 2 * (NG * l + g + 1))
                    for m in range(2):
                        sp.dma_start(QKD[l, m, :, :, cols].rearrange("s r t -> r s t"), qp[:, par, m, :, :]).then_inc(parts_out[par], 16)
                    if l == 0:
                        sp.wait_ge(zeros_set, 3)
                    else:
                        sp.wait_ge(a_qk, NU)
                    sp.wait_ge(parts_out[par], 32 * ((NG // 2) * l + g // 2 + 1))
                    if l or g:
                        sp.wait_ge(stacks_in, N_STACK * (NG * l + g))
                    for h2 in range(2):
                        for part, (s0, n) in enumerate(((0, 3), (3, 3), (6, 2))):
                            rows = slice(64 * h2 + DH * s0, 64 * h2 + DH * (s0 + n))
                            sp.dma_start(QS[rows, :, cols],
                                         QKD[l, 0, part:part + 1, 64 * h2:64 * h2 + 64, cols].rearrange("s (d r) t -> s d r t", r=PR)
                                         .to_broadcast([n, DH, PR, GW])).then_inc(stacks_in, 16)
                            sp.dma_start(KS[rows, :, h2, cols],
                                         QKD[l, 1, 0:n, 64 * h2:64 * h2 + 64, cols].rearrange("s (d r) t -> s d r t", r=PR)).then_inc(stacks_in, 16)

            stacks(0)
            stacks(1)
            for g in range(NG):
                sp.wait_ge(r_o, g + 1)
                if g >= 1:
                    sp.wait_ge(r_out, 16 * g)
                sp.dma_start(out[GB * g:GB * g + GB].rearrange("b s d -> s b d"), zS[:, g % 2, :, :]).then_inc(r_out, 16)
            sp.wait_ge(r_out, 16 * NG)

        @block.gpsimd
        def _(pool):
            def products():
                for g in range(NG):
                    par = g % 2
                    f4 = fS[:, g, :].rearrange("p (b y) -> p b y", b=GB)
                    pool.wait_ge(f_landed[g], 16)
                    if g >= 2:
                        pool.wait_ge(s_df, g - 1)
                    for dst, m in ((AF, 0), (BFv, 2)):
                        pool.tensor_tensor(dst[:, par, :].rearrange("p (b y) -> p b y", b=GB), f4,
                                           GRID[:, m:m + 1, :].to_broadcast([128, GB, D]), ALU.mult).then_inc(s_prod, 1)

            def pad_v(l, b, par):
                u = NU * l
                pool.wait_ge(a_pv, u + 2 * b - 2)
                src = V[:, ds(b, 1), :].rearrange("k o (r e) -> k (o r) e", r=PR)
                for h2 in range(2):
                    pool.tensor_copy(vp5[:, PR * par:PR * par + PR, h2, h2, 0:DH], src[:, :, DH * h2:DH * h2 + DH]).then_inc(a_vp, 1)

            def pad_first(l, b):
                src = V[:, b, :].rearrange("k (r e) -> k r e", r=PR)
                for h2 in range(2):
                    pool.tensor_copy(vp5[:, PR * b:PR * b + PR, h2, h2, 0:DH], src[:, :, DH * h2:DH * h2 + DH]).then_inc(a_vp, 1)

            def shift(u, c):
                pool.wait_ge(a_max, u + 1)
                pool.tensor_tensor(SE[:, c, :, :], SE[:, c, :, :],
                                   MX[:, c, :, None].to_broadcast([128, HU, S]), ALU.subtract).then_inc(a_sub, 1)

            pool.wait_ge(ld_const, N_CONST)
            products()
            pool.memset(VP[:, :, :, :], 0.0).then_inc(zeros_set, 1)
            pool.wait_ge(zeros_set, 1)
            pool.memset(KS[0:64, :, 1, :].bitcast(U32), 0).then_inc(zeros_set, 1)
            pool.wait_ge(zeros_set, 2)
            pool.memset(KS[64:128, :, 0, :].bitcast(U32), 0).then_inc(zeros_set, 1)
            pool.wait_ge(zeros_set, 3)
            vp5 = VP[:, :, :, :].rearrange("k p (r h2) (w e) -> k (p r) h2 w e", h2=2, w=2)
            for h2 in range(2):
                pool.memset(vp5[:, :, h2, h2, DH:DH + 1], 1.0).then_inc(mask_set, 1)
                pool.wait_ge(mask_set, h2 + 1)
            pool.tensor_scalar(CAUS[:, :], CST[:, C_CAUS:C_CAUS + 128], 1.0, 0.0, ALU.mult, ALU.add).then_inc(zeros_set, 1)
            pool.wait_ge(zeros_set, 4)
            pool.wait_ge(ld_row, N_ROW)
            pool.tensor_scalar(MSK[:, :, :], MU8,
                               NEG, 0.0, ALU.mult, ALU.add).then_inc(mask_set, 1)

            pool.wait_ge(p_v, NG)
            pad_first(0, 0)
            pad_first(0, 1)

            def gs_turn(k, par):
                s, d = gsb[:, par, :, :], gsb[:, 1 - par, :, :]
                pool.wait_ge(gs_mask, k + 1)
                pool.tensor_tensor(gpr[:, :, :], gcm[:, :, 1:R], s[:, :, 0:1].to_broadcast([128, 2, R - 1]), ALU.mult).then_inc(gs_pool, 1)
                pool.wait_ge(gs_inv, 2 * k + 1)
                pool.tensor_tensor(d[:, :, R - 1], s[:, :, 0], gws[:, 6:8], ALU.mult).then_inc(gs_pool, 1)
                pool.wait_ge(gs_inv, 2 * k + 2)
                pool.wait_ge(gs_pool, 3 * k + 1)
                pool.tensor_tensor(gpr[:, :, :], gpr[:, :, :], gws[:, 8:10, None].to_broadcast([128, 2, R - 1]), ALU.mult).then_inc(gs_pool, 1)
                pool.wait_ge(gs_pool, 3 * k + 3)
                pool.tensor_tensor(d[:, :, 0:R - 1], s[:, :, 1:R], gpr[:, :, :], ALU.subtract).then_inc(gs_step, 1)

            def slot(i, c):
                if c % 2 == 0 and (not isinstance(i, int) or 2 <= 2 * i + (c - 2) // 2 < B):
                    pad_v(0, 2 * i + (c - 2) // 2, ((c - 2) // 2) % 2)
                if c % 2 == 0 and (not isinstance(i, int) or 0 < 4 * i + c <= NU):
                    gs_turn(2 * i + c // 2 - 1, (c // 2 + 1) % 2)
                if not isinstance(i, int) or 4 * i + c < NU:
                    shift(4 * i + c, c)

            for k in range(8):
                slot(k // 4, k % 4)
            with pool.Fori(2, B // 2) as i:
                for c in range(4):
                    slot(i, c)
            slot(NU // 4, 0)
            pool.wait_ge(a_pv, NU)
            pool.wait_ge(p_v, 2 * NG)
            pad_first(1, 0)
            pad_first(1, 1)

            def slot1(i, c):
                b = 2 * i + (c - 2) // 2
                if c % 2 == 0 and (not isinstance(i, int) or 0 < 4 * i + c <= NU):
                    gs_turn(GS + 2 * i + c // 2 - 1, (c // 2 + 1) % 2)
                if c % 2 == 0 and (not isinstance(i, int) or 2 <= b < B):
                    pad_v(1, b, ((c - 2) // 2) % 2)

            for k in range(8):
                slot1(k // 4, k % 4)
            with pool.Fori(2, B // 2) as i:
                for c in range(4):
                    slot1(i, c)
            slot1(NU // 4, 0)

        @block.tensor
        def _(pe):
            mm, tr = nc.tensor.matmul, nc.tensor.transpose

            pe.wait_ge(ld_const, N_CONST)
            for m in range(3):
                ins = tr(P[:, 5, 128 * m:128 * m + 128], GRID[:, (1, 3, 4)[m], :], ident)
            ins.then_inc(su_pe, 1)

            def turn_f(g):
                par = g % 2
                pe.wait_ge(f_landed[g], 16)
                if g >= 2:
                    pe.wait_ge(s_fTp, 3 * (g - 1))
                for j in range(GB):
                    ins = tr(P[:, par, D * j:D * j + D], fS[:, g, D * j:D * j + D], ident)
                ins.then_inc(s_fT, 1)

            turn_f(0)
            for g in range(NG):
                par = g % 2
                if g + 1 < NG:
                    turn_f(g + 1)
                if g >= 2:
                    pe.wait_ge(s_U, g - 1)
                    pe.wait_ge(s_stage, g - 1)
                pe.wait_ge(s_fTp, 3 * g + 1)
                for j in range(GB):
                    ins = mm(P[:, 2 + par, D * j:D * j + D], fT[:, par, 2, D * j:D * j + D], pD1T, start=True, stop=True)
                ins.then_inc(s_H, 1)
                pe.wait_ge(s_prod, 2 * g + 2)
                mm(P[:, 4 + par, :], hD2T, BFv[:, par, :], start=True, stop=False, skip_group_check=True)
                pe.wait_ge(s_fTp, 3 * g + 3)
                for j in range(GB):
                    mm(P[:, 4 + par, D * j:D * j + D], fT[:, par, 0, D * j:D * j + D], nD1T, start=False, stop=False, skip_group_check=True)
                    mm(P[:, 4 + par, D * j:D * j + D], fT[:, par, 1, D * j:D * j + D], hD2T, start=False, stop=False, skip_group_check=True)
                pe.wait_ge(s_U, g + 1)
                mm(P[:, 4 + par, :], nD1T, AF[:, par, :], start=False, stop=True, skip_group_check=True).then_inc(s_df, 1)

            pe.wait_ge(ld_vec, N_VEC)
            tr(P[:, 7, 0:R], LW[0:R, :], ident[0:R, 0:R])
            tr(P[:, 7, 64:64 + V_ALL], VR[0:V_ALL, :], ident[0:V_ALL, 0:V_ALL])
            pe.wait_ge(vrp_turned, 1)
            tr(P[:, 7, 128:132], VRT[0:4, :], ident[0:4, 0:4]).then_inc(su_pe, 1)
            pe.wait_ge(su_dve, 2)
            for m in range(2):
                ins = mm(P[:, 6, B * m:B * m + B], WADA[:, 128 * m:128 * m + 128], EMB[:, 7, :], start=True, stop=True)
            ins.then_inc(su_pe, 1)

            def project(l):
                pe.wait_ge(ld_w, N_W)
                pe.wait_ge(su_act, 8)

                def turn(g):
                    n, par = NG * l + g + 1, g % 2
                    pe.wait_ge(p_norm, n)
                    if g >= 2:
                        pe.wait_ge(p_xT, n - 2)
                        if l == 0:
                            pe.wait_ge(p_nat, g - 1)
                    for j in range(GB):
                        ins = tr(P[:, par, D * j:D * j + D], xn[:, par, j, :], ident)
                    ins.then_inc(p_T, 1)

                turn(0)
                for g in range(NG):
                    n, par = NG * l + g + 1, g % 2
                    if g + 1 < NG:
                        turn(g + 1)
                    pe.wait_ge(p_xT, n)
                    if l == 0:
                        for j in range(GB):
                            ins = tr(P[:, par, D * j:D * j + D], xT[:, par, D * j:D * j + D], ident)
                        ins.then_inc(p_back, 1)
                    if g >= 2:
                        pe.wait_ge(p_qf, 4 * (n - 2))
                        pe.wait_ge(p_v, n - 2)
                    for m in range(2):
                        mm(P[:, 2 + 2 * par + m, :], WQK[:, l, m, :], xT[:, par, :], start=True, stop=True).then_inc(p_q, 1)
                    for j in range(GB):
                        ins = mm(P[:, 6 + par, D * j:D * j + D], xT[:, par, D * j:D * j + D], WV[:, l, :], start=True, stop=True)
                    ins.then_inc(p_q, 1)

            def attention(l):
                base = NU * l

                def scores(u, i, c):
                    if l or not isinstance(u, int) or u >= 2:
                        pe.wait_ge(a_add, u - 1)
                    b = 2 * i + c // 2
                    if c == 0:
                        pe.wait_ge(stacks_in, N_STACK * (NG * l + 1 + i // 2))
                    for k in range(2):
                        bank = P[:, 2 * (c % 2) + k, :]
                        mask = CAUS[:, None, :] if l else MSK[:, ds(b, 1), :]
                        mm(bank, IDB[:, :], mask.to_broadcast([128, 4, S]), start=True, stop=False, skip_group_check=True)
                        for r in range(2):
                            pr = 4 * (c % 2) + 2 * k + r
                            ins = mm(bank[:, 256 * r:256 * r + 256], QS[:, pr, ds(b * S, S)], KS[:, pr, :, ds(b * S, S)],
                                     start=False, stop=(r == 1), skip_group_check=True)
                    ins.then_inc(a_qk, 1)

                def gs_dots(k, i, c):
                    if isinstance(k, int) and k == 0:
                        pe.wait_ge(ld_gs, N_GS)
                    else:
                        pe.wait_ge(gs_step, k)
                    backs = 2 * i + (c - 5) // 2
                    if l or not isinstance(i, int) or backs > 0:
                        pe.wait_ge(a_ctx, B * l + (max(backs, 0) if isinstance(i, int) else backs))
                    for m in range(2):
                        ins = mm(P[:, 7, 256 + R * m:256 + R * m + R], gsb[:, c // 2, m, 0:1].to_broadcast([128, 128]),
                                 gsb[:, c // 2, m, :], start=True, stop=True)
                    ins.then_inc(gs_dot, 1)

                def transposes(u, c):
                    pe.wait_ge(a_exp, u + 1)
                    if l or not isinstance(u, int) or u:
                        pe.wait_ge(a_pT, u)
                    for hh in range(HU):
                        ins = tr(P[:, 4 + hh // 4, S * (hh % 4):S * (hh % 4) + S], SE[:, c, hh, :], ident)
                    ins.then_inc(a_T, 1)

                def back(b, par):
                    n = B * l + b
                    pe.wait_ge(a_cs, n + 1)
                    if l or not isinstance(b, int) or b:
                        pe.wait_ge(a_ctx, n)
                    pe.wait_ge(gs_mask, GS * l + (min(b + 3, GS) if isinstance(b, int) else b + 3))
                    for m in range(2):
                        ins = tr(P[:, 7, S * m:S * m + S], cs[:, par, S * m:S * m + S], ident)
                    ins.then_inc(a_ct, 1)

                def pv(u, c, b):
                    pe.wait_ge(a_pT, u + 1)
                    if c % 2 == 0:
                        pe.wait_ge(a_vp, 2 * (B * l + b + 1))
                        if l or not isinstance(b, int) or b:
                            pe.wait_ge(a_cs, B * l + b)
                    for h2 in range(2):
                        for r in range(4):
                            hh = 2 * r + h2
                            ins = mm(P[32 * r:32 * r + 32, 6, S * (c % 2):S * (c % 2) + S],
                                     VP[:, (c // 2) % 2, HU * (c % 2) + hh, :], pT[:, c % 2, hh, :],
                                     start=(h2 == 0), stop=(h2 == 1), skip_group_check=True)
                    ins.then_inc(a_pv, 1)

                def slot(i, c):
                    def live(lag):
                        return not isinstance(i, int) or 0 <= 4 * i + c - lag < NU

                    u = base + 4 * i + c
                    if live(0):
                        scores(u, i, c)
                    if live(3):
                        transposes(u - 3, (c + 1) % 4)
                    if c % 2 == 0 and live(6):
                        back(2 * i + c // 2 - 3, (c // 2 + 1) % 2)
                    if c % 2 and live(0):
                        gs_dots(GS * l + 2 * i + c // 2, i, c)
                    if live(4):
                        pv(u - 4, c, 2 * i + c // 2 - 2)

                for k in range(8):
                    slot(k // 4, k % 4)
                with pe.Fori(2, B // 2) as i:
                    for c in range(4):
                        slot(i, c)
                for k in range(NU, NU + 5):
                    slot(k // 4, k % 4)

            def out_projection(l):
                def turn(g):
                    pe.wait_ge(a_ctx, B * l + GB * (g + 1))
                    if g >= 2:
                        pe.wait_ge(o_cT, NG * l + g - 1)
                    for j in range(GB):
                        ins = tr(P[:, g % 2, D * j:D * j + D], CTX[:, GB * g + j, :], ident)
                    ins.then_inc(o_T, 1)

                turn(0)
                for g in range(NG):
                    if g + 1 < NG:
                        turn(g + 1)
                    par, n = g % 2, NG * l + g + 1
                    pe.wait_ge(o_cT, n)
                    if g >= 2:
                        pe.wait_ge(o_res, n - 2)
                    for j in range(GB):
                        ins = mm(P[:, 2 + par, D * j:D * j + D], cT[:, par, D * j:D * j + D], WO[:, l, :], start=True, stop=True)
                    ins.then_inc(o_wo, 1)

            def feed_forward(l):
                def turn(g):
                    n = NG * l + g + 1
                    pe.wait_ge(m_n, n)
                    if g >= 2:
                        pe.wait_ge(m_hT, n - 2)
                    for j in range(GB):
                        ins = tr(P[:, g % 2, D * j:D * j + D], cS[:, g % 2, j, :], ident)
                    ins.then_inc(m_T, 1)

                def up(g):
                    n = NG * l + g + 1
                    pe.wait_ge(m_hT, n)
                    for f in range(NF):
                        if g:
                            pe.wait_ge(m_g, NF * (n - 2) + f + 1)
                        mm(P[:, 2 + f, :], W1[:, l, 128 * f:128 * f + 128], cT[:, g % 2, :], start=True, stop=True).then_inc(m_f, 1)

                def down(g):
                    n = NG * l + g + 1
                    pe.wait_ge(m_g, NF * n)
                    if g >= 2:
                        pe.wait_ge(m_t, n - 2)
                    for j in range(GB):
                        for f in range(NF):
                            ins = mm(P[:, 6 + g % 2, D * j:D * j + D], gT[:, g % 2, f, D * j:D * j + D], W2[:, l, f, :],
                                     start=(f == 0), stop=(f == NF - 1))
                    ins.then_inc(m_y, 1)

                turn(0)
                turn(1)
                up(0)
                for g in range(1, NG):
                    if g + 1 < NG:
                        turn(g + 1)
                    up(g)
                    down(g - 1)
                down(NG - 1)

            def response_matrix():
                pe.wait_ge(gs_step, R)
                pe.wait_ge(m_t, 2 * NG)
                for m in range(2):
                    tr(P[0:R, 6, 128 * m:128 * m + 128], gsb[:, 0, m, :], ident)
                tr(P[0:R, 6, 256:384], LR[:, :], ident).then_inc(rm_pe, 1)
                pe.wait_ge(rm_dve, 1)
                mm(P[:, 5, 0:128], UT[0:R, 1, :], UT[0:R, 0, :], start=True, stop=True).then_inc(rm_pe, 1)
                pe.wait_ge(rm_dve, 2)
                mm(P[:, 5, 128:128 + R], BST, BST[:, 0:R], start=True, stop=True).then_inc(rm_pe, 1)
                pe.wait_ge(rm_dve, 3)
                tr(P[0:R, 5, 256:384], BBm, ident).then_inc(rm_pe, 1)
                pe.wait_ge(rm_dve, 4)
                mm(P[:, 5, 384:512], BBTt[:, :], RWT[:, :], start=True, stop=True).then_inc(rm_pe, 1)

            for l in range(2):
                project(l)
                if l == 0:
                    pe.wait_ge(mask_set, 3)
                    pe.wait_ge(zeros_set, 4)
                pe.wait_ge(p_v, NG * (l + 1))
                pe.wait_ge(p_qf, 4 * NG * (l + 1))
                attention(l)
                out_projection(l)
                feed_forward(l)

            response_matrix()

            def turn(g):
                pe.wait_ge(m_x, NG + g + 1)
                if g >= 2:
                    pe.wait_ge(r_hT, g - 1)
                for j in range(GB):
                    ins = tr(P[:, g % 2, D * j:D * j + D], X[:, GB * g + j, :], ident)
                ins.then_inc(r_T, 1)

            def gate(g):
                pe.wait_ge(r_h1, g + 1)
                mm(P[:, 6 + g % 2, 0:GB], W2G[:, :].to_broadcast([R, 128]), pl[0:R, g % 2, 4:4 + GB], start=True, stop=True).then_inc(r_g2, 1)

            turn(0)
            for g in range(NG):
                par = g % 2
                if g + 1 < NG:
                    turn(g + 1)
                if g:
                    gate(g - 1)
                pe.wait_ge(r_hT, g + 1)
                if g == 0:
                    pe.wait_ge(rm_dve, 5)
                if g >= 2:
                    pe.wait_ge(r_t, g - 1)
                for j in range(GB):
                    ins = mm(P[:, 2 + par, D * j:D * j + D], cT[:, par, D * j:D * j + D], RM[:, :], start=True, stop=True)
                ins.then_inc(r_m, 1)
                pe.wait_ge(r_pl, g + 1)
                mm(P[0:R, 4 + par, 0:GB], W1T[:, :], pl[:, par, 0:GB], start=True, stop=True).then_inc(r_g1, 1)
            gate(NG - 1)

        @block.scalar
        def _(act):
            af = nc.scalar.activation
            act.wait_ge(ld_const, N_CONST)
            af(IDB[:, :], ident, ACT.Copy).then_inc(su_act, 1)
            act.wait_ge(su_dve, 1)
            af(EMB[:, 6, :], EMB[:, 5, :], ACT.Sin).then_inc(su_act, 1)
            act.wait_ge(su_act, 2)
            af(EMB[:, 7, :], EMB[:, 6, :], ACT.Silu).then_inc(su_dve, 1)
            act.wait_ge(ld_vec, N_VEC)
            af(VRT[:, :].rearrange("n (h d r) -> n h d r", h=2, d=DH),
               VRP[:, :].rearrange("n (r h d) -> n h d r", h=2, d=DH), ACT.Copy).then_inc(vrp_turned, 1)
            act.wait_ge(ld_w, N_W)
            for l in range(2):
                for m in range(2):
                    af(WQK[:, l, m, :].rearrange("k (h d r) -> k h d r", h=2, d=DH),
                       WQ0[:, l, m, :].rearrange("k (r h d) -> k h d r", h=2, d=DH), ACT.Copy).then_inc(su_act, 1)
            act.wait_ge(su_pe, 3)
            act.wait_ge(su_dve, 3)
            for m in range(2):
                af(ADA[:, m, :], P[:, 6, B * m:B * m + B], ACT.Identity, bias=COL[:, V_BADA + m:V_BADA + m + 1]).then_inc(su_act, 1)
            act.wait_ge(su_act, 8)

            def project(l):
                def evac(g):
                    n, par = NG * l + g + 1, g % 2
                    act.wait_ge(p_T, n)
                    if g >= 2:
                        act.wait_ge(p_q, 3 * (n - 2))
                    if l == 0:
                        for j in range(GB):
                            b = GB * g + j
                            ins = af(xT[:, par, D * j:D * j + D], P[:, par, D * j:D * j + D], ACT.Identity,
                                     bias=ADA[:, 1, b:b + 1], scale=ADA[:, 0, b:b + 1])
                    else:
                        ins = af(xT[:, par, :], P[:, par, :], ACT.Identity, bias=COL[:, V_BE1:V_BE1 + 1],
                                 scale=COL[:, V_GA1:V_GA1 + 1])
                    ins.then_inc(p_xT, 1)

                evac(0)
                for g in range(NG):
                    n, par = NG * l + g + 1, g % 2
                    if g + 1 < NG:
                        evac(g + 1)
                    for m in range(2):
                        act.wait_ge(p_q, 3 * (n - 1) + m + 1)
                        if m == 0 and g >= 2:
                            act.wait_ge(p_q3, 2 * (n - 2))
                            act.wait_ge(parts_out[par], 32 * (2 * l + g // 2))
                        for dst in (qf[:, par, m, :], qp[:, par, m, 0, :]):
                            af(dst, P[:, 2 + 2 * par + m, :], ACT.Identity, bias=BQK[:, 2 * l + m:2 * l + m + 1],
                               scale=ISQ if m == 0 else 1.0).then_inc(p_qf, 1)
                    for m in range(2):
                        act.wait_ge(p_r, 2 * (n - 1) + m + 1)
                        af(qp[:, par, m, 1, :], qr[:, m, :], ACT.Copy).then_inc(p_q2, 1)

            def attention(l):
                base = NU * l

                def gs_norm_of(u):
                    act.wait_ge(gs_mask, u + 1)
                    af(gws[:, 2:4], gcm[:, :, 0], ACT.Ln).then_inc(gs_log, 1)
                    act.wait_ge(gs_log, u + 1)
                    af(gws[:, 0:2], gws[:, 2:4], ACT.Exp, scale=0.5).then_inc(gs_norm, 1)

                def exps(u, c):
                    act.wait_ge(a_add if l else a_sub, u + 1)
                    af(SE[:, c, :, :], SE[:, c, :, :], ACT.Exp).then_inc(a_exp, 1)

                def evac(u, c):
                    act.wait_ge(a_T, u + 1)
                    if isinstance(u, int) and u == base:
                        act.wait_ge(parts_out[0], 32 * (NG // 2) * (l + 1))
                    if l or not isinstance(u, int) or u >= 2:
                        act.wait_ge(a_pv, u - 1)
                    af(pT[:, c % 2, :, :].rearrange("p h k -> p (h k)"), P[:, 4:6, :].rearrange("p a k -> p (a k)"), ACT.Copy).then_inc(a_pT, 1)

                def context(b, par):
                    act.wait_ge(a_pv, base + 2 * b + 2)
                    af(cs[:, par, :], P[:, 6, 0:2 * S], ACT.Copy).then_inc(a_cs, 1)

                def slot(i, c):
                    def live(lag):
                        return not isinstance(i, int) or 0 <= 4 * i + c - lag < NU

                    u = base + 4 * i + c
                    if c % 2 == 0 and live(1):
                        gs_norm_of(GS * l + 2 * i + c // 2 - 1)
                    if live(1):
                        exps(u - 1, (c - 1) % 4)
                    if live(3):
                        evac(u - 3, (c - 3) % 4)
                    if l == 0 and c % 2 == 0:
                        bias_in(u, 2 * i + c // 2 + 1, (c // 2 + 1) % 2)
                    if c % 2 and live(5):
                        context(2 * i + (c - 5) // 2, ((c - 5) // 2) % 2)

                def bias_in(u, b, par):
                    if isinstance(b, int) and not 3 <= b < B:
                        return
                    act.wait_ge(a_add, u)
                    for rows in (slice(0, 64), slice(64, 128)):
                        act.dma_start(FS[rows, par, :, :], a["fside_Bx16xSxS_0"][ds(b, 1), :, rows, :].rearrange("b h q k -> q (b h) k"))\
                          .then_inc(fs_landed[par], 16)

                act.preload_act_table_set("natural_log_exp_and_others")
                for k in range(8):
                    slot(k // 4, k % 4)
                with act.Fori(2, B // 2 - 1) as i:
                    for c in range(4):
                        slot(i, c)
                for k in range(NU - 4, NU + 6):
                    slot(k // 4, k % 4)

            def out_projection(l):
                for g in range(NG):
                    act.wait_ge(o_T, NG * l + g + 1)
                    if g >= 2:
                        act.wait_ge(o_wo, NG * l + g - 1)
                    af(cT[:, g % 2, :], P[:, g % 2, :], ACT.Copy).then_inc(o_cT, 1)

            def feed_forward(l):
                sc, bi, b1 = ((V_G2, V_BETA2, V_B1), (V_GA2, V_BE2, V_B1B))[l]

                def evac(g):
                    n = NG * l + g + 1
                    act.wait_ge(m_T, n)
                    if g >= 2:
                        act.wait_ge(m_f, NF * (n - 2))
                    af(cT[:, g % 2, :], P[:, g % 2, :], ACT.Identity, bias=COL[:, bi:bi + 1], scale=COL[:, sc:sc + 1]).then_inc(m_hT, 1)

                evac(0)
                evac(1)
                for g in range(NG):
                    n = NG * l + g + 1
                    if 0 < g < NG - 1:
                        evac(g + 1)
                    for f in range(NF):
                        act.wait_ge(m_f, NF * (n - 1) + f + 1)
                        if g >= 2 and f == 0:
                            act.wait_ge(m_y, n - 2)
                        af(gT[:, g % 2, f, :], P[:, 2 + f, :], ACT.Gelu if l else ACT.Gelu_apprx_sigmoid,
                           bias=COL[:, b1 + f:b1 + f + 1]).then_inc(m_g, 1)

            for l in range(2):
                project(l)
                attention(l)
                act.wait_ge(a_ctx, B * (l + 1))
                out_projection(l)
                feed_forward(l)
            af(MOD[:, :], SAFE[:, :], ACT.Sigmoid).then_inc(su_act, 1)
            def evac(g):
                act.wait_ge(r_T, g + 1)
                if g >= 2:
                    act.wait_ge(r_m, g - 1)
                    act.wait_ge(r_pl, g - 1)
                af(cT[:, g % 2, :], P[:, g % 2, :], ACT.Copy).then_inc(r_hT, 1)

            evac(0)
            for g in range(NG):
                par, n = g % 2, g + 1
                if g + 1 < NG:
                    evac(g + 1)
                act.wait_ge(r_g1, n)
                if g >= 2:
                    act.wait_ge(r_g2, n - 2)
                af(pl[0:R, par, 4:4 + GB], P[0:R, 4 + par, 0:GB], ACT.Relu, bias=GB1[:, 0:1], scale=1.0 / S).then_inc(r_h1, 1)
                act.wait_ge(r_g2, n)
                if g >= 2:
                    act.wait_ge(r_st, n - 2)
                af(pl[:, par, 8:8 + GB], P[:, 6 + par, 0:GB], ACT.Sigmoid, bias=GB2[:, 0:1]).then_inc(r_ba, 1)

        @block.vector
        def _(dve):
            v = nc.vector
            chain = [0]

            def link(ins):
                chain[0] += 1
                ins.then_inc(su_chain, 1)
                dve.wait_ge(su_chain, chain[0])

            dve.wait_ge(ld_const, N_CONST)
            link(v.tensor_copy(EMB[:, 0, :], TI))
            link(v.tensor_scalar(EMB[:, 1, :], EMB[:, 0, :], 40.0, None, ALU.mult))
            link(v.tensor_scalar(EMB[:, 2, :], EMB[:, 1, :], CST[:, C_FREQ:C_FREQ + 1], None, ALU.mult))
            link(v.tensor_scalar(EMB[:, 3, :], EMB[:, 2, :], float(1 / (2 * np.pi)), CST[:, C_QUART:C_QUART + 1], ALU.mult, ALU.add))
            link(v.tensor_scalar(EMB[:, 3, :], EMB[:, 3, :], 12582912.0, None, ALU.add))
            link(v.tensor_scalar(EMB[:, 3, :], EMB[:, 3, :], -12582912.0, None, ALU.add))
            c1 = 6.28125
            c2 = float(np.float32(2 * np.pi - c1))
            c3 = float(np.float32(2 * np.pi - c1 - float(np.float32(2 * np.pi - c1))))
            link(v.scalar_tensor_tensor(EMB[:, 4, :], EMB[:, 3, :], -c1, EMB[:, 2, :], ALU.mult, ALU.add))
            link(v.scalar_tensor_tensor(EMB[:, 4, :], EMB[:, 3, :], -c2, EMB[:, 4, :], ALU.mult, ALU.add))
            link(v.scalar_tensor_tensor(EMB[:, 4, :], EMB[:, 3, :], -c3, EMB[:, 4, :], ALU.mult, ALU.add))
            link(v.tensor_scalar(EMB[:, 4, :], EMB[:, 4, :], CST[:, C_PHASE:C_PHASE + 1], None, ALU.add))
            v.tensor_scalar(EMB[:, 5, :], EMB[:, 4, :], float(np.float32(3.1415925)), float(np.float32(-3.1415925)), ALU.min, ALU.max).then_inc(su_dve, 1)
            dve.wait_ge(su_pe, 1)
            link(v.tensor_copy(GRT[:, :, :], P[:, 5, 0:384].rearrange("p (m d) -> p m d", m=3)))

            def four(t):
                return t.rearrange("p (b y) -> p b y", b=GB)

            def stats(src, b):
                v.bn_stats(ST6[:, b, :], src[:, b, :]).then_inc(stats_done, 1)

            def stencil_products(g):
                par = g % 2
                dve.wait_ge(s_fT, g + 1)
                if g >= 2:
                    dve.wait_ge(s_df, g - 1)
                for m in (2, 0, 1):
                    v.tensor_tensor(four(fT[:, par, m, :]), four(P[:, par, :]), GRT[:, m:m + 1, :].to_broadcast([128, GB, D]), ALU.mult).then_inc(s_fTp, 1)

            stencil_products(0)
            for g in range(NG):
                par = g % 2
                if g + 1 < NG:
                    stencil_products(g + 1)
                dve.wait_ge(s_H, g + 1)
                dve.wait_ge(s_prod, 2 * g + 2)
                v.tensor_tensor(AF[:, par, :], AF[:, par, :], P[:, 2 + par, :], ALU.subtract).then_inc(s_U, 1)
                dve.wait_ge(s_df, g + 1)
                for j in range(GB):
                    b = GB * g + j
                    ins = v.scalar_tensor_tensor(X[:, b, :], P[:, 4 + par, D * j:D * j + D],
                                                 DTB[:, b:b + 1], fS[:, g, D * j:D * j + D], ALU.mult, ALU.add)
                ins.then_inc(s_stage, 1)
                dve.wait_ge(s_stage, g + 1)
                v.tensor_scalar(X[:, GB * g:GB * g + GB, :], X[:, GB * g:GB * g + GB, :], 0.0, None, ALU.max).then_inc(s_x0, 1)
                dve.wait_ge(s_x0, g + 1)
                for j in range(GB):
                    stats(X, GB * g + j)

            dve.wait_ge(su_pe, 2)
            v.tensor_copy(W1T[:, :], P[:, 7, 0:R])
            v.tensor_copy(COL[:, :], P[:, 7, 64:64 + V_ALL]).then_inc(su_chain, 1)
            chain[0] += 1
            for m in range(2):
                v.tensor_scalar(BQK[:, m:4:2], P[:, 7, 128 + m:132:2], 1.0 if m else ISQ, None, ALU.mult)
            dve.wait_ge(su_chain, chain[0])
            v.tensor_scalar(COL[:, V_BADA:V_BADA + 1], COL[:, V_BADA:V_BADA + 1], 1.0, None, ALU.add).then_inc(su_dve, 1)

            newton_at = [0]

            def rstd(k):
                def nl(ins):
                    newton_at[0] += 1
                    ins.then_inc(newton, 1)
                    dve.wait_ge(newton, newton_at[0])

                dve.wait_ge(stats_done, B * k)
                me, mo, se, so = ST6[:, :, 1], ST6[:, :, 4], ST6[:, :, 2], ST6[:, :, 5]
                nl(v.tensor_tensor(MV[:, :, 1], me, mo, ALU.subtract))
                nl(v.tensor_tensor(RS[:, :], se, so, ALU.add))
                nl(v.scalar_tensor_tensor(MV[:, :, 1], MV[:, :, 1], 0.25, MV[:, :, 1], ALU.mult, ALU.mult))
                nl(v.tensor_scalar(RS[:, :], RS[:, :], 1.0 / D, LN_EPS, ALU.mult, ALU.add))
                nl(v.tensor_tensor(NT[:, :], RS[:, :], MV[:, :, 1], ALU.add))
                nl(v.tensor_scalar(NI[:, :], NT[:, :].bitcast(I32), 1, None, ALU.arith_shift_right))
                nl(v.tensor_scalar(NY[:, :].bitcast(I32), NI[:, :], -1.0, float(MAGIC), ALU.mult, ALU.add))
                nl(v.tensor_tensor(MV[:, :, 0], me, mo, ALU.add))
                for _ in range(3):
                    nl(v.tensor_tensor(RS[:, :], NY[:, :], NY[:, :], ALU.mult))
                    nl(v.scalar_tensor_tensor(RS[:, :], RS[:, :], -0.5, NT[:, :], ALU.mult, ALU.mult))
                    nl(v.scalar_tensor_tensor(NY[:, :], RS[:, :], 1.5, NY[:, :], ALU.add, ALU.mult))
                nl(v.scalar_tensor_tensor(NMR[:, :], MV[:, :, 0], -0.5, NY[:, :], ALU.mult, ALU.mult))

            def normed(dst, src, g, done):
                for j in range(GB):
                    b = GB * g + j
                    ins = v.tensor_scalar(dst[:, g % 2, j, :], src[:, b, :], NY[:, b:b + 1], NMR[:, b:b + 1], ALU.mult, ALU.add)
                ins.then_inc(done, 1)

            def project(l):
                normed(xn, X, 0, p_norm)
                normed(xn, X, 1, p_norm)
                for g in range(NG):
                    par, n = g % 2, NG * l + g + 1
                    grp = slice(GB * g, GB * g + GB)
                    if l == 0:
                        dve.wait_ge(p_back, n)
                        v.tensor_tensor(X[:, grp, :], four(P[:, par, :]), BOB[:, 0:1, :].to_broadcast([128, GB, D]), ALU.add).then_inc(p_nat, 1)
                    if g + 2 < NG:
                        dve.wait_ge(p_T, n)
                        normed(xn, X, g + 2, p_norm)
                    for m in range(2):
                        dve.wait_ge(p_qf, 4 * (n - 1) + 2 * m + 2)
                        if n > 1:
                            dve.wait_ge(p_q3, 2 * (n - 2) + m + 1)
                        v.tensor_tensor(qr[:, m, :], qf[:, par, m, :], qp[:, par, m, 0, :], ALU.subtract).then_inc(p_r, 1)
                    dve.wait_ge(p_q, 3 * n)
                    v.tensor_tensor(V[:, grp, :], four(P[:, 6 + par, :]), BVB[:, l:l + 1, :].to_broadcast([128, GB, D]), ALU.add).then_inc(p_v, 1)
                    for m in range(2):
                        dve.wait_ge(p_q2, 2 * (n - 1) + m + 1)
                        v.tensor_tensor(qp[:, par, m, 2, :], qr[:, m, :], qp[:, par, m, 1, :], ALU.subtract).then_inc(p_q3, 1)

            def attention(l):
                base = NU * l

                def gs_copy(k, i, c):
                    dve.wait_ge(gs_dot, k + 1)
                    v.tensor_tensor(gcm[:, :, :], P[:, 7, 256:256 + 2 * R].rearrange("p (m c) -> p m c", m=2),
                                    CST[:, None, ds(C_GSM + k, R)].to_broadcast([128, 2, R]), ALU.mult).then_inc(gs_mask, 1)

                def gs_scale(k):
                    dve.wait_ge(gs_norm, k + 1)
                    v.tensor_scalar(gws[:, 4:6], gws[:, 0:2], GS_EPS, None, ALU.add).then_inc(gs_chain, 1)
                    dve.wait_ge(gs_chain, k + 1)
                    v.reciprocal(gws[:, 6:8], gws[:, 4:6]).then_inc(gs_inv, 1)
                    dve.wait_ge(gs_inv, 2 * k + 1)
                    v.tensor_tensor(gws[:, 8:10], gws[:, 6:8], gws[:, 6:8], ALU.mult).then_inc(gs_inv, 1)

                def slot(i, c):
                    def live(lag):
                        return not isinstance(i, int) or 0 <= 4 * i + c - lag < NU

                    u = base + 4 * i + c
                    k = GS * l + 2 * i + c // 2
                    ps = P[:, 2 * (c % 2):2 * (c % 2) + 2, :].rearrange("p a (h k) -> p (a h) k", k=S)
                    if live(0):
                        dve.wait_ge(a_qk, u + 1)
                        if l or not isinstance(u, int) or u >= 4:
                            dve.wait_ge(a_T, u - 3)
                        if l == 0:
                            third = isinstance(i, int) and 2 * i + c // 2 == 2
                            if c % 2 == 0:
                                dve.wait_ge(*((fs_landed[2], 32) if third else (fs_landed[1], 32 * (i + 1)) if c
                                              else (fs_landed[0], 32 * (1 if isinstance(i, int) and i == 0 else i))))
                            bias = FS2 if third else FS[:, c // 2, :, :]
                            v.tensor_tensor(SE[:, c, :, :], ps, bias[:, HU * (c % 2):HU * (c % 2) + HU, :], ALU.add).then_inc(a_add, 1)
                        else:
                            v.tensor_reduce(MX[:, c, :], ps, AX.X, ALU.max).then_inc(a_max, 1)
                    if c % 2 == 0 and live(1):
                        gs_scale(k - 1)
                    if live(0):
                        if l == 0:
                            dve.wait_ge(a_add, u + 1)
                            v.tensor_reduce(MX[:, c, :], SE[:, c, :, :], AX.X, ALU.max).then_inc(a_max, 1)
                        else:
                            dve.wait_ge(a_max, u + 1)
                            v.tensor_tensor(SE[:, c, :, :], ps, MX[:, c, :, None].to_broadcast([128, HU, S]), ALU.subtract).then_inc(a_add, 1)
                    if c % 2 == 0 and live(6):
                        context(2 * i + c // 2 - 3)
                    if c % 2 and live(0):
                        gs_copy(k, i, c)

                def context(b):
                    n = B * l + b
                    ct = P[:, 7, 0:2 * S].rearrange("p (h e) -> p h e", h=H)
                    dve.wait_ge(a_ct, n + 1)
                    v.reciprocal(RSUM[:, :], ct[:, :, DH]).then_inc(a_rs, 1)
                    dve.wait_ge(a_rs, n + 1)
                    dst = CTX[:, b, :] if isinstance(b, int) else CTX[:, ds(b, 1), :].rearrange("p o d -> p (o d)")
                    v.tensor_tensor(dst.rearrange("p (h d) -> p h d", h=H), ct[:, :, 0:DH],
                                    RSUM[:, :, None].to_broadcast([128, H, DH]), ALU.mult).then_inc(a_ctx, 1)

                for k in range(8):
                    slot(k // 4, k % 4)
                with dve.Fori(2, B // 2) as i:
                    for c in range(4):
                        slot(i, c)
                for k in range(NU, NU + 5):
                    slot(k // 4, k % 4)

            def out_projection(l):
                for g in range(NG):
                    par, n = g % 2, NG * l + g + 1
                    grp = slice(GB * g, GB * g + GB)
                    dve.wait_ge(o_wo, n)
                    ps = four(P[:, 2 + par, :])
                    if l == 0:
                        v.tensor_tensor(X[:, grp, :], ps, X[:, grp, :], ALU.add).then_inc(o_res, 1)
                    else:
                        v.tensor_tensor(V[:, grp, :], ps, BOB[:, 1:2, :].to_broadcast([128, GB, D]), ALU.add).then_inc(o_bo, 1)
                        dve.wait_ge(o_bo, g + 1)
                        v.tensor_tensor(V[:, grp, :], V[:, grp, :], X[:, grp, :], ALU.add).then_inc(o_res, 1)
                    dve.wait_ge(o_res, n)
                    for j in range(GB):
                        stats(V if l else X, GB * g + j)

            def feed_forward(l):
                x1 = V if l else X
                normed(cS, x1, 0, m_n)
                normed(cS, x1, 1, m_n)
                for g in range(NG):
                    par, n = g % 2, NG * l + g + 1
                    grp = slice(GB * g, GB * g + GB)
                    if g + 2 < NG:
                        dve.wait_ge(m_T, n)
                        normed(cS, x1, g + 2, m_n)
                    dve.wait_ge(m_y, n)
                    v.tensor_tensor(yS[:, par, :, :], four(P[:, 6 + par, :]), B2B[:, l:l + 1, :].to_broadcast([128, GB, D]), ALU.add).then_inc(m_t, 1)
                    dve.wait_ge(m_t, n)
                    if l == 0:
                        v.tensor_tensor(X[:, grp, :], yS[:, par, :, :], X[:, grp, :], ALU.add).then_inc(m_x, 1)
                        dve.wait_ge(m_x, n)
                        for j in range(GB):
                            stats(X, GB * g + j)
                    else:
                        v.tensor_tensor(zS[:, par, :, :], yS[:, par, :, :], V[:, grp, :], ALU.add).then_inc(m_u, 1)
                        dve.wait_ge(m_u, g + 1)
                        v.tensor_tensor(yS[:, par, :, :], zS[:, par, :, :], X[:, grp, :], ALU.subtract).then_inc(m_d, 1)
                        dve.wait_ge(m_d, g + 1)
                        for j in range(GB):
                            b = GB * g + j
                            ins = v.scalar_tensor_tensor(X[:, b, :], yS[:, par, j, :], GATE[:, b:b + 1], X[:, b, :], ALU.mult, ALU.add)
                        ins.then_inc(m_x, 1)

            def response_matrix():
                dve.wait_ge(rm_pe, 1)
                v.tensor_copy(RWT[:, :], P[0:R, 6, 256:384])
                v.tensor_copy(UT[0:R, :, :], P[0:R, 6, 0:256].rearrange("p (m d) -> p m d", m=2)).then_inc(rm_dve, 1)
                for k, (dst, ps) in enumerate(((BST, P[:, 5, 0:128]), (BBm, P[:, 5, 128:128 + R]),
                                               (BBTt[:, :], P[0:R, 5, 256:384]), (RM[:, :], P[:, 5, 384:512]))):
                    dve.wait_ge(rm_pe, k + 2)
                    v.tensor_copy(dst, ps).then_inc(rm_dve, 1)
                link(v.tensor_tensor(CB[:, 0, :], CB[:, 0, :], CB[:, 1, :], ALU.add))

            for l in range(2):
                rstd(2 * l + 1)
                if l == 0:
                    dve.wait_ge(ld_row, N_ROW)
                    dve.wait_ge(mask_set, 3)
                    dve.wait_ge(su_act, 8)
                project(l)
                dve.wait_ge(p_q3, 2 * NG * (l + 1))
                attention(l)
                dve.wait_ge(a_ctx, B * (l + 1))
                out_projection(l)
                rstd(2 * l + 2)
                feed_forward(l)

            response_matrix()
            dve.wait_ge(su_act, 9)
            for g in range(NG):
                par, n = g % 2, g + 1
                dve.wait_ge(r_hT, n)
                if g >= 2:
                    dve.wait_ge(r_g1, n - 2)
                v.tensor_reduce(pl[:, par, 0:GB], four(cT[:, par, :]), AX.X, ALU.add).then_inc(r_pl, 1)
                dve.wait_ge(r_m, n)
                v.tensor_tensor(yS[:, par, :, :], four(P[:, 2 + par, :]), CB[:, 0:1, :].to_broadcast([128, GB, D]), ALU.add).then_inc(r_t, 1)
                dve.wait_ge(r_ba, n)
                v.tensor_tensor(pl[:, par, 12:12 + GB], pl[:, par, 8:8 + GB], MOD[:, GB * g:GB * g + GB], ALU.mult).then_inc(r_st, 1)
                dve.wait_ge(r_t, n)
                dve.wait_ge(r_st, n)
                if g >= 2:
                    dve.wait_ge(r_out, 16 * (g - 1))
                for j in range(GB):
                    ins = v.scalar_tensor_tensor(zS[:, par, j, :], yS[:, par, j, :], pl[:, par, 12 + j:13 + j], X[:, GB * g + j, :], ALU.mult, ALU.add)
                ins.then_inc(r_o, 1)


_INS = ['x', 'condB_dt', 'itok_B_34_63', 'fside_Bx16xSxS_0', 'condB_gatescore', 'condB_safetyscore', 'mask_Bx1xSxS_bk0',
        'L0_cond_A_grid', 'L0_cond_B_grid'] + \
       ['L1_cond_' + n for n in ('W_ada', 'b_ada', 'Wq', 'bq', 'Wk', 'bk', 'Wv', 'bv', 'Wo', 'bo', 'W1', 'b1', 'W2', 'b2', 'g2', 'beta2')] + \
       ['L2_cond_' + n for n in ('Wq', 'bq', 'Wk', 'bk', 'Wv', 'bv', 'Wo', 'bo', 'W1', 'b1', 'W2', 'b2', 'gamma1', 'beta1', 'gamma2', 'beta2')] + \
       ['L3_cond_' + n for n in ('U', 'V', 'safety_bias', 'gate_w1', 'gate_b1', 'gate_w2', 'gate_b2', 'resp_w', 'resp_b')]


def kernel(**inputs):
    import numpy as _np
    import concourse.bacc as _bacc
    from concourse import mybir as _mybir
    from concourse.bass_utils import run_bass_kernel_spmd as _run

    nc = _bacc.Bacc("TRN2", target_bir_lowering=False, num_devices=1)
    arrays, args = {}, {}
    host = {name: _np.ascontiguousarray(inputs[name]) for name in _INS}
    host["mask_Bx1xSxS_bk0"] = host["mask_Bx1xSxS_bk0"].view(_np.int32)
    host["consts"] = constants()
    for name, arr in host.items():
        arrays[f"in_{name}"] = arr
        args[name] = nc.dram_tensor(f"in_{name}", arr.shape, _mybir.dt.from_np(arr.dtype), kind="ExternalInput").ap()
    out = nc.dram_tensor("out_0", (B, S, D), F32, kind="ExternalOutput").ap()
    build(nc, args, out)
    r = _run(nc, [arrays], core_ids=[0])
    return r.results[0]["out_0"]
```

```python
from contextlib import ExitStack

import numpy as np
import concourse.bass as bass
from concourse import mybir

F32 = mybir.dt.float32
BF16 = mybir.dt.bfloat16
I32 = mybir.dt.int32
U32 = mybir.dt.uint32
U8 = mybir.dt.uint8
ALU = mybir.AluOpType
ACT = mybir.ActivationFunctionType
AX = mybir.AxisListType
ds = bass.ds

B, S, D, H, DH, FF = 16, 128, 128, 16, 8, 512
GB = 4
NG = B // GB
GW = GB * D
PR = H // 2
HU = H // 2
HA = 2
NU = 2 * B
R = 32
NF = FF // 128
SLOTS = 8
TOK = B * S
LN_EPS = 1e-5
GS_EPS = 1e-8
NEG = -1e30
ISQ = float(DH) ** -0.5
MAGIC = 0x5F3759DF

C_ID, C_PD1, C_ND1, C_HD2, C_CAUS, C_FREQ, C_PHASE, C_QUART, C_GSM = 0, 128, 256, 384, 512, 640, 641, 642, 643
C_ALL = C_GSM + 2 * R

V_BADA, V_G2, V_BETA2, V_B1, V_GA1, V_BE1, V_GA2, V_BE2, V_B1B = 0, 2, 3, 4, 8, 9, 10, 11, 12
V_ALL = 16


def constants():
    c = np.zeros((128, C_ALL), np.float32)
    n = S
    d1 = np.zeros((n, n), np.float32)
    d2 = np.zeros((n, n), np.float32)
    for i in range(1, n - 1):
        d1[i, i - 1], d1[i, i + 1] = -0.5, 0.5
        d2[i, i - 1], d2[i, i], d2[i, i + 1] = 1.0, -2.0, 1.0
    d1[0, :3] = [-1.5, 2.0, -0.5]
    d1[-1, -3:] = [0.5, -2.0, 1.5]
    d2[0, :4] = [2.0, -5.0, 4.0, -1.0]
    d2[-1, -4:] = [-1.0, 4.0, -5.0, 2.0]
    c[:, C_ID:C_ID + 128] = np.eye(128)
    c[:, C_PD1:C_PD1 + 128] = d1.T
    c[:, C_ND1:C_ND1 + 128] = -d1.T
    c[:, C_HD2:C_HD2 + 128] = 0.5 * d2.T
    c[:, C_CAUS:C_CAUS + 128] = np.where(np.tril(np.ones((n, n), bool)), 0.0, NEG)
    half = D // 2
    freq = np.exp(np.arange(half, dtype=np.float32) * np.float32(-np.log(10000.0) / (half - 1)))
    c[:, C_FREQ] = np.concatenate([freq, freq])
    c[half:, C_PHASE] = np.pi / 2
    c[half:, C_QUART] = 0.25
    c[:, C_GSM:C_GSM + R] = 1.0
    return c


def build(nc, a, out):
    ctx = ExitStack()
    with ctx:
        def sb(name, shape, dt=F32):
            return ctx.enter_context(nc.sbuf_tensor(name, shape, dt))

        def sem(name):
            return ctx.enter_context(nc.semaphore(name))

        X = sb("X", [128, B, D])
        V = sb("V", [128, B, D])
        CTX = sb("CTX", [128, B, D])
        QS = sb("QS", [128, NG, PR, GW], BF16)
        KS = sb("KS", [128, NG, 2, PR, GW], BF16)
        FS = sb("FS", [128, 4, HU, S])
        VP = sb("VP", [128, 2, H, 32])
        MSK = sb("MSK", [128, B, S], BF16)
        CST = sb("CST", [128, C_ALL])
        IDB = sb("IDB", [128, 128], BF16)
        CAUS = sb("CAUS", [128, 128], BF16)
        WQK = sb("WQK", [128, 2, 2, D])
        WV = sb("WV", [128, 2, D])
        WO = sb("WO", [128, 2, D])
        W1 = sb("W1", [128, 2, FF])
        W2 = sb("W2", [128, 2, NF, D])
        VR = sb("VR", [32, 128])
        VRP = sb("VRP", [4, 128])
        VRT = sb("VRT", [4, 128])
        COL = sb("COL", [128, V_ALL])
        BQK = sb("BQK", [128, 4])
        BVB = sb("BVB", [128, 2, D])
        BOB = sb("BOB", [128, 2, D])
        B2B = sb("B2B", [128, 2, D])
        CB = sb("CB", [128, 2, D])
        DTB = sb("DTB", [128, B])
        GATE = sb("GATE", [128, B])
        SAFE = sb("SAFE", [128, B])
        MOD = sb("MOD", [128, B])
        GB2 = sb("GB2", [128, 1])
        ADA = sb("ADA", [128, 2, B])
        MV = sb("MV", [128, B, 2])
        ST6 = sb("ST6", [128, B, 6])
        RS = sb("RS", [128, B])
        NMR = sb("NMR", [128, B])
        NT = sb("NT", [128, B])
        NI = sb("NI", [128, B], I32)
        NY = sb("NY", [128, B])
        MX = sb("MX", [128, 4, HU])
        RSUM = sb("RSUM", [128, H])
        RM = sb("RM", [128, D])
        W1T = sb("W1T", [128, R])
        W2G = sb("W2G", [R, 1])
        GB1 = sb("GB1", [R, 1])
        WORK = sb("WORK", [128, 8320])

        P = ctx.enter_context(nc.psum_tensor("P", [128, 8, 512], F32))
        QKD = nc.dram_tensor("qk_parts", (2, NG, 2, 3, 128, GW), BF16, kind="Internal").ap()

        ident = CST[:, C_ID:C_ID + 128]
        pD1T = CST[:, C_PD1:C_PD1 + 128]
        nD1T = CST[:, C_ND1:C_ND1 + 128]
        hD2T = CST[:, C_HD2:C_HD2 + 128]

        def work(at, *shape, dt=F32):
            n = int(np.prod(shape))
            if dt == BF16:
                n //= 2
            v = WORK[:, at:at + n]
            if dt != F32:
                v = v.bitcast(dt)
            names = " ".join(f"d{i}" for i in range(len(shape)))
            if len(shape) == 1:
                return v
            return v.rearrange(f"p ({names}) -> p {names}", **{f"d{i}": s for i, s in enumerate(shape)})

        bias_flat = FS[:, :, :, :].rearrange("p a h k -> p (a h k)")
        v_flat = V[:, :, :].rearrange("p b d -> p (b d)")
        ctx_flat = CTX[:, :, :].rearrange("p b d -> p (b d)")

        def within(buf, at, *shape):
            v = buf[:, at:at + int(np.prod(shape))]
            if len(shape) == 1:
                return v
            names = " ".join(f"d{i}" for i in range(len(shape)))
            return v.rearrange(f"p ({names}) -> p {names}", **{f"d{i}": n for i, n in enumerate(shape)})

        EMB = within(v_flat, 0, 8, B)
        TI = within(v_flat, 128, B).bitcast(I32)
        WADA = within(v_flat, 144, 2 * D)
        LW = within(v_flat, 400, D)
        WQ0 = within(v_flat, 528, 2, 2, D)
        MU8 = within(v_flat, 1040, B * S // 4).bitcast(U8).rearrange("q (b k) -> q b k", b=B)
        GRID = sb("GRID", [128, 5, D])
        GRT = sb("GRT", [128, 3, D])
        gsb = sb("gsb", [128, 2, 2, R])
        gcm = sb("gcm", [128, 2, R])
        gws = sb("gws", [128, 16])
        gpr = sb("gpr", [128, 2, R - 1])
        LR = sb("LR", [128, R])
        UT = within(bias_flat, 0, 2, D)
        BST = within(bias_flat, 256, D)
        BBm = within(bias_flat, 384, R)
        XBO = within(bias_flat, 2048, B, D)
        FS2 = ctx_flat.rearrange("p (a h k) -> p a h k", a=2, h=HU)
        BBTt = sb("BBTt", [R, D])
        RWT = sb("RWT", [R, D])
        AF = work(0, 2, GW)
        BFv = work(1024, 2, GW)
        fT = work(2048, 2, 3, GW)
        fS = work(5120, NG, GW)
        xn = work(0, 2, GB, D)
        xT = work(1024, 2, GW)
        qf = work(2048, 2, 2, GW)
        qr = work(4096, 2, GW)
        qp = work(6656, 2, 3, GW, dt=BF16)

        def parts_of(g):
            if g != 1:
                return QS[:, max(g, 1), :, :].rearrange("p r t -> p (r t)")[:, 0:2 * 3 * GW].rearrange("p (m s t) -> p m s t", m=2, s=3)
            return qp[:, :, :, :]

        SE = work(0, 4, HU, S)
        pT = work(4096, 2, HU, S)
        cs = work(6144, 2, 2 * S)
        cS = work(0, 2, GB, D)
        cT = work(1024, 2, GW)
        gT = work(2048, 2, NF, GW)
        yS = work(6144, 2, GB, D)
        zS = work(7168, 2, GB, D)
        pl = work(8192, 2, 16)

        ld_const, ld_vec, ld_w, ld_gs, ld_mask, ld_row = (sem(f"ld_{n}") for n in ("const", "vec", "w", "gs", "mask", "row"))
        f_landed = [sem(f"f_landed{g}") for g in range(NG)]
        fs_landed = [sem(f"fs_landed{k}") for k in range(5)]
        gs_dot, gs_mask, gs_log, gs_norm, gs_chain, gs_inv, gs_pool, gs_step = (sem(n) for n in (
            "gs_dot", "gs_masked", "gs_log", "gs_norm", "gs_norm_eps", "gs_inverse", "gs_pool", "gs_step"))
        su_pe, su_dve, su_act, su_chain = sem("setup_pe"), sem("setup_dve"), sem("setup_act"), sem("setup_chain")
        rm_pe, rm_dve = sem("resp_matrix_pe"), sem("resp_matrix_dve")
        zeros_set, mask_set, vrp_turned = sem("zeros_set"), sem("mask_set"), sem("biases_turned")
        s_prod, s_fT, s_fTp, s_H, s_U, s_df, s_stage, s_x0 = (sem(n) for n in (
            "stencil_products", "f_transposed", "fT_products", "H_ready", "U_ready", "df_ready", "stage_ready", "x_ready"))
        stats_done, newton = sem("stats_done"), sem("newton")
        p_norm, p_T, p_xT, p_back, p_nat, p_q, p_qf, p_r, p_q2, p_q3, p_v = (sem(n) for n in (
            "normed", "transposed", "xT_ready", "x_back", "x_natural", "qkv_ready", "qk_evacuated", "qk_rest", "qk_second",
            "qk_third", "v_ready"))
        parts_out = [sem(f"parts_out{g}") for g in range(NG)]
        stacks_in = sem("stacks_in")
        a_qk, a_half, a_heads, a_add, a_max, a_sub, a_exp, a_T, a_pT, a_pv, a_cs, a_ct, a_rs, a_ctx, a_vp = (sem(n) for n in (
            "scores_ready", "shifted_half", "act_heads", "biased", "max_ready", "shifted", "exp_done", "probs_transposed", "probsT_ready", "pv_done",
            "ctxT_copied", "ctx_back", "rowsum_inv", "ctx_ready", "v_padded"))
        o_T, o_cT, o_wo, o_res, x_bo, x_b2, pool_b2 = (sem(n) for n in (
            "ctx_T", "ctxT_ready", "wo_done", "x1_ready", "x_plus_bo", "x_plus_b2", "x_plus_b2_half"))
        m_n, m_T, m_hT, m_f, m_g, m_y, m_t, m_x = (sem(n) for n in (
            "ff_normed", "ff_T", "ff_hT", "ff_up", "ff_gelu", "ff_down", "ff_sum", "ff_x"))
        r_T, r_hT, r_m, r_g1, r_h1, r_g2, r_ba, r_st, r_t, r_o, r_out = (sem(n) for n in (
            "l3_T", "l3_hT", "l3_resp", "l3_gate1", "l3_h1", "l3_gate2", "l3_base", "l3_strength",
            "l3_biased", "l3_out", "out_written"))

        GS = R // 2
        N_CONST = 5 * 16
        N_VEC = 16 * 16
        N_STACK = 8 * 16
        N_GS = 3 * 16
        N_W = 14 * 16
        N_ROW = 10 * 16
        block = ctx.enter_context(nc.Block())

        @block.sync
        def _(sp):
            sp.dma_start(CST[:, :], a["consts"]).then_inc(ld_const, 16)
            sp.dma_start(GRID[:, 0:2, :], a["L0_cond_A_grid"].rearrange("c x y -> x c y")).then_inc(ld_const, 16)
            sp.dma_start(GRID[:, 2:5, :], a["L0_cond_B_grid"].rearrange("c x y -> x c y")).then_inc(ld_const, 16)
            sp.dma_start(DTB[:, :], a["condB_dt"][None, :].to_broadcast([128, B])).then_inc(ld_const, 16)
            sp.dma_start(TI, a["itok_B_34_63"][None, :].to_broadcast([128, B])).then_inc(ld_const, 16)
            for g in range(NG):
                sp.dma_start(fS[:, g, :].rearrange("p (b y) -> p b y", b=GB),
                             a["x"][GB * g:GB * g + GB].rearrange("b x y -> x b y")).then_inc(f_landed[g], 16)
            sp.dma_start(MU8.bitcast(I32), a["mask_Bx1xSxS_bk0"].rearrange("b o q k -> q b (o k)")).then_inc(ld_mask, 16)
            vecs = [("L1_cond_b_ada", V_BADA, 2), ("L1_cond_g2", V_G2, 1), ("L1_cond_beta2", V_BETA2, 1), ("L1_cond_b1", V_B1, 4),
                    ("L2_cond_gamma1", V_GA1, 1), ("L2_cond_beta1", V_BE1, 1), ("L2_cond_gamma2", V_GA2, 1),
                    ("L2_cond_beta2", V_BE2, 1), ("L2_cond_b1", V_B1B, 4)]
            for name, at, n in vecs:
                sp.dma_start(VR[at:at + n, :], a[name].rearrange("(n d) -> n d", n=n)).then_inc(ld_vec, 16)
            sp.dma_start(GB1[:, :], a["L3_cond_gate_b1"][:, None], allow_slow_non_contiguous=True).then_inc(ld_vec, 16)
            for i, name in enumerate(("L1_cond_bq", "L1_cond_bk", "L2_cond_bq", "L2_cond_bk")):
                sp.dma_start(VRP[i:i + 1, :], a[name][None, :]).then_inc(ld_vec, 16)
            sp.dma_start(WADA, a["L1_cond_W_ada"]).then_inc(ld_vec, 16)
            sp.dma_start(LW[0:R, :], a["L3_cond_gate_w1"]).then_inc(ld_vec, 16)
            for l in range(2):
                n = f"L{l + 1}_cond_"
                sp.dma_start(WQ0[:, l, 0, :], a[n + "Wq"]).then_inc(ld_w, 16)
                sp.dma_start(WQ0[:, l, 1, :], a[n + "Wk"]).then_inc(ld_w, 16)
                sp.dma_start(WV[:, l, :], a[n + "Wv"]).then_inc(ld_w, 16)
                sp.dma_start(WO[:, l, :], a[n + "Wo"]).then_inc(ld_w, 16)
                sp.dma_start(W1[:, l, :], a[n + "W1"]).then_inc(ld_w, 16)
                sp.dma_start(W2[:, l, :, :], a[n + "W2"].rearrange("(c f) d -> f c d", c=NF)).then_inc(ld_w, 16)
            sp.dma_start(W2G[:, :], a["L3_cond_gate_w2"].rearrange("a b -> b a"), allow_slow_non_contiguous=True).then_inc(ld_w, 16)
            sp.dma_start(GB2[:, :], a["L3_cond_gate_b2"][None, :].to_broadcast([128, 1])).then_inc(ld_w, 16)
            for l in range(2):
                n = f"L{l + 1}_cond_"
                sp.dma_start(BVB[:, l, :], a[n + "bv"][None, :].to_broadcast([128, D])).then_inc(ld_row, 16)
                sp.dma_start(BOB[:, l, :], a[n + "bo"][None, :].to_broadcast([128, D])).then_inc(ld_row, 16)
                sp.dma_start(B2B[:, l, :], a[n + "b2"][None, :].to_broadcast([128, D])).then_inc(ld_row, 16)
            sp.dma_start(CB[:, 0, :], a["L3_cond_resp_b"][None, :].to_broadcast([128, D])).then_inc(ld_row, 16)
            sp.dma_start(CB[:, 1, :], a["L3_cond_safety_bias"][None, :].to_broadcast([128, D])).then_inc(ld_row, 16)
            sp.dma_start(GATE[:, :], a["condB_gatescore"][None, :].to_broadcast([128, B])).then_inc(ld_row, 16)
            sp.dma_start(SAFE[:, :], a["condB_safetyscore"][None, :].to_broadcast([128, B])).then_inc(ld_row, 16)
            for u in range(6):
                for rows in (slice(0, 64), slice(64, 128)):
                    dst = FS[rows, u, :, :] if u < 4 else FS2[rows, u - 4, :, :]
                    sp.dma_start(dst, a["fside_Bx16xSxS_0"][u // 2, HU * (u % 2):HU * (u % 2) + HU, rows, :].rearrange("h q k -> q h k"))\
                      .then_inc(fs_landed[min(u, 4)], 16)
            sp.dma_start(gsb[:, 0, 0, :], a["L3_cond_U"]).then_inc(ld_gs, 16)
            sp.dma_start(gsb[:, 0, 1, :], a["L3_cond_V"]).then_inc(ld_gs, 16)
            sp.dma_start(LR[:, :], a["L3_cond_resp_w"]).then_inc(ld_gs, 16)

            def stacks(l):
                def parts(g):
                    sp.wait_ge(p_q3, 2 * (NG * l + g + 1))
                    sp.dma_start(QKD[l, g].rearrange("m s r t -> r (m s) t"), parts_of(g).rearrange("r m s t -> r (m s) t"))\
                      .then_inc(parts_out[g], 16)

                def gather(g, some=range(8)):
                    if g == 0:
                        if l == 0:
                            sp.wait_ge(zeros_set, 4)
                        else:
                            sp.wait_ge(a_qk, NU)
                    sp.wait_ge(parts_out[g], 16 * (l + 1))
                    if (l or g) and 0 in some:
                        sp.wait_ge(stacks_in, N_STACK * (NG * l + g))
                    for k in some:
                        if k < 2:
                            rows, n = ((slice(0, 96), 3), (slice(96, 128), 2))[k]
                            src = QKD[l, g, 0, 0:n, :, :].rearrange("s r t -> (s r t)")
                            if k == 0:
                                src = src[None, :].to_broadcast([2, n * 128 * GW])
                            sp.dma_start(QS[rows, g, :, :], src).then_inc(stacks_in, 16)
                        else:
                            part, h2 = (k - 2) // 2, k % 2
                            n = (3, 3, 2)[part]
                            rows = slice(48 * part + h2, 48 * part + 16 * n, 2)
                            src = QKD[l, g, 1, part].rearrange("(d h r) t -> d h (r t)", d=DH, h=2)[None, :, h2, :]
                            sp.dma_start(KS[rows, g, h2, :, :], src.to_broadcast([n, DH, PR * GW])).then_inc(stacks_in, 16)

                parts(0)
                gather(0)
                parts(1)
                parts(2)
                parts(3)
                gather(1)
                if l:
                    gather(2)
                    gather(3)
                else:
                    for k in range(6):
                        bias_in((k + 6) // 4, (k + 6) % 4)
                        gather(2 + k // 3, ((0, 1, 2), (3, 4, 5), (6, 7))[k % 3])
                    with sp.Fori(3, B // 2) as i:
                        for c in range(4):
                            bias_in(i, c)

            def bias_in(i, c):
                sp.wait_ge(a_add, 4 * i + c - 3)
                for rows in (slice(0, 64), slice(64, 128)):
                    src = a["fside_Bx16xSxS_0"][ds(2 * i + c // 2, 1), HU * (c % 2):HU * (c % 2) + HU, rows, :]
                    sp.dma_start(FS[rows, c, :, :], src.rearrange("b h q k -> q (b h) k")).then_inc(fs_landed[c], 16)

            stacks(0)
            stacks(1)
            for g in range(NG):
                sp.wait_ge(r_o, g + 1)
                if g >= 1:
                    sp.wait_ge(r_out, 16 * g)
                sp.dma_start(out[GB * g:GB * g + GB].rearrange("b s d -> s b d"), zS[:, g % 2, :, :]).then_inc(r_out, 16)
            sp.wait_ge(r_out, 16 * NG)

        @block.gpsimd
        def _(pool):
            def products():
                for g in range(NG):
                    par = g % 2
                    f4 = fS[:, g, :].rearrange("p (b y) -> p b y", b=GB)
                    pool.wait_ge(f_landed[g], 16)
                    if g >= 2:
                        pool.wait_ge(s_df, g - 1)
                    for dst, m in ((AF, 0), (BFv, 2)):
                        pool.tensor_tensor(dst[:, par, :].rearrange("p (b y) -> p b y", b=GB), f4,
                                           GRID[:, m:m + 1, :].to_broadcast([128, GB, D]), ALU.mult).then_inc(s_prod, 1)

            pool.wait_ge(ld_const, N_CONST)
            products()
            vp5 = VP[:, :, :, :].rearrange("k p (r h2) (w e) -> k (p r) h2 w e", h2=2, w=2)
            pool.memset(VP[:, :, :, :], 0.0).then_inc(zeros_set, 1)
            pool.wait_ge(zeros_set, 1)
            for h2 in range(2):
                pool.memset(vp5[:, :, h2, h2, DH:DH + 1], 1.0).then_inc(mask_set, 1)
                pool.wait_ge(mask_set, h2 + 1)
            pool.tensor_scalar(CAUS[:, :], CST[:, C_CAUS:C_CAUS + 128], 1.0, 0.0, ALU.mult, ALU.add).then_inc(zeros_set, 1)
            pool.wait_ge(zeros_set, 2)
            pool.wait_ge(ld_mask, 16)
            pool.tensor_scalar(MSK[:, :, :], MU8, NEG, 0.0, ALU.mult, ALU.add).then_inc(mask_set, 1)
            pool.wait_ge(mask_set, 3)
            for h2 in range(2):
                pool.memset(KS[:, :, h2, :, :].bitcast(U32), 0).then_inc(zeros_set, 1)

            def pad_v(l, b, par):
                u = NU * l
                pool.wait_ge(a_pv, u + 2 * b - 2)
                src = V[:, ds(b, 1), :].rearrange("k o (r e) -> k (o r) e", r=PR)
                for h2 in range(2):
                    pool.tensor_copy(vp5[:, PR * par:PR * par + PR, h2, h2, 0:DH], src[:, :, DH * h2:DH * h2 + DH]).then_inc(a_vp, 1)

            def pad_first(l, b):
                src = V[:, b, :].rearrange("k (r e) -> k r e", r=PR)
                for h2 in range(2):
                    pool.tensor_copy(vp5[:, PR * b:PR * b + PR, h2, h2, 0:DH], src[:, :, DH * h2:DH * h2 + DH]).then_inc(a_vp, 1)

            def shift(u, c):
                pool.wait_ge(a_max, u + 1)
                pool.tensor_tensor(SE[:, c, :, :], SE[:, c, :, :],
                                   MX[:, c, :, None].to_broadcast([128, HU, S]), ALU.subtract).then_inc(a_sub, 1)

            pool.wait_ge(zeros_set, 4)
            pool.wait_ge(p_v, NG)
            pad_first(0, 0)
            pad_first(0, 1)

            def gs_turn(k, par):
                s, d = gsb[:, par, :, :], gsb[:, 1 - par, :, :]
                pool.wait_ge(gs_mask, k + 1)
                pool.tensor_tensor(gpr[:, :, :], gcm[:, :, 1:R], s[:, :, 0:1].to_broadcast([128, 2, R - 1]), ALU.mult).then_inc(gs_pool, 1)
                pool.wait_ge(gs_inv, 2 * k + 1)
                pool.tensor_tensor(d[:, :, R - 1], s[:, :, 0], gws[:, 6:8], ALU.mult).then_inc(gs_pool, 1)
                pool.wait_ge(gs_inv, 2 * k + 2)
                pool.wait_ge(gs_pool, 3 * k + 1)
                pool.tensor_tensor(gpr[:, :, :], gpr[:, :, :], gws[:, 8:10, None].to_broadcast([128, 2, R - 1]), ALU.mult).then_inc(gs_pool, 1)
                pool.wait_ge(gs_pool, 3 * k + 3)
                pool.tensor_tensor(d[:, :, 0:R - 1], s[:, :, 1:R], gpr[:, :, :], ALU.subtract).then_inc(gs_step, 1)

            def slot(i, c):
                if c % 2 == 0 and (not isinstance(i, int) or 2 <= 2 * i + (c - 2) // 2 < B):
                    pad_v(0, 2 * i + (c - 2) // 2, ((c - 2) // 2) % 2)
                if c % 2 == 0 and (not isinstance(i, int) or 0 < 4 * i + c <= NU):
                    gs_turn(2 * i + c // 2 - 1, (c // 2 + 1) % 2)
                if not isinstance(i, int) or 4 * i + c < NU:
                    shift(4 * i + c, c)

            for k in range(8):
                slot(k // 4, k % 4)
            with pool.Fori(2, B // 2) as i:
                for c in range(4):
                    slot(i, c)
            slot(NU // 4, 0)

            def residual(l, g):
                grp = slice(GB * g, GB * g + GB)
                pool.wait_ge(m_n, NG * l + g + 1)
                x1 = V if l else X
                bias = B2B[:, l:l + 1, :].to_broadcast([128, GB, D])
                if l == 0:
                    pool.tensor_tensor(X[:, grp, :], X[:, grp, :], bias, ALU.add).then_inc(x_b2, 1)
                else:
                    pool.tensor_tensor(V[:, grp, :], V[:, grp, :], bias, ALU.add).then_inc(pool_b2, 1)
                    pool.wait_ge(pool_b2, g + 1)
                    pool.tensor_tensor(V[:, grp, :], V[:, grp, :], X[:, grp, :], ALU.subtract).then_inc(x_b2, 1)

            for g in range(NG):
                residual(0, g)
            pool.wait_ge(a_pv, NU)
            pool.wait_ge(p_v, 2 * NG)
            pad_first(1, 0)
            pad_first(1, 1)

            def slot1(i, c):
                b = 2 * i + (c - 2) // 2
                if c % 2 == 0 and (not isinstance(i, int) or 0 < 4 * i + c <= NU):
                    gs_turn(GS + 2 * i + c // 2 - 1, (c // 2 + 1) % 2)
                if c % 2 == 0 and (not isinstance(i, int) or 2 <= b < B):
                    pad_v(1, b, ((c - 2) // 2) % 2)

            for k in range(8):
                slot1(k // 4, k % 4)
                if k % 2:
                    g = k // 2
                    pool.tensor_tensor(XBO[:, GB * g:GB * g + GB, :], X[:, GB * g:GB * g + GB, :],
                                       BOB[:, 1:2, :].to_broadcast([128, GB, D]), ALU.add).then_inc(x_bo, 1)
            with pool.Fori(2, B // 2) as i:
                for c in range(4):
                    slot1(i, c)
            slot1(NU // 4, 0)
            for g in range(NG):
                residual(1, g)

        @block.tensor
        def _(pe):
            mm, tr = nc.tensor.matmul, nc.tensor.transpose

            pe.wait_ge(ld_const, N_CONST)
            for m in range(3):
                ins = tr(P[:, 5, 128 * m:128 * m + 128], GRID[:, (1, 3, 4)[m], :], ident)
            ins.then_inc(su_pe, 1)

            def turn_f(g):
                par = g % 2
                pe.wait_ge(f_landed[g], 16)
                if g >= 2:
                    pe.wait_ge(s_fTp, 3 * (g - 1))
                for j in range(GB):
                    ins = tr(P[:, par, D * j:D * j + D], fS[:, g, D * j:D * j + D], ident)
                ins.then_inc(s_fT, 1)

            def vectors():
                pe.wait_ge(ld_vec, N_VEC)
                tr(P[:, 7, 0:R], LW[0:R, :], ident[0:R, 0:R])
                tr(P[:, 7, 64:64 + V_ALL], VR[0:V_ALL, :], ident[0:V_ALL, 0:V_ALL])
                pe.wait_ge(vrp_turned, 1)
                tr(P[:, 7, 128:132], VRT[0:4, :], ident[0:4, 0:4]).then_inc(su_pe, 1)
                pe.wait_ge(su_dve, 2)
                for m in range(2):
                    ins = mm(P[:, 6, B * m:B * m + B], WADA[:, 128 * m:128 * m + 128], EMB[:, 7, :], start=True, stop=True)
                ins.then_inc(su_pe, 1)

            turn_f(0)
            for g in range(NG):
                par = g % 2
                if g + 1 < NG:
                    turn_f(g + 1)
                if g >= 2:
                    pe.wait_ge(s_U, g - 1)
                    pe.wait_ge(s_stage, g - 1)
                pe.wait_ge(s_fTp, 3 * g + 1)
                for j in range(GB):
                    ins = mm(P[:, 2 + par, D * j:D * j + D], fT[:, par, 2, D * j:D * j + D], pD1T, start=True, stop=True)
                ins.then_inc(s_H, 1)
                pe.wait_ge(s_prod, 2 * g + 2)
                mm(P[:, 4 + par, :], hD2T, BFv[:, par, :], start=True, stop=False, skip_group_check=True)
                pe.wait_ge(s_fTp, 3 * g + 3)
                for j in range(GB):
                    mm(P[:, 4 + par, D * j:D * j + D], fT[:, par, 0, D * j:D * j + D], nD1T, start=False, stop=False, skip_group_check=True)
                    mm(P[:, 4 + par, D * j:D * j + D], fT[:, par, 1, D * j:D * j + D], hD2T, start=False, stop=False, skip_group_check=True)
                pe.wait_ge(s_U, g + 1)
                mm(P[:, 4 + par, :], nD1T, AF[:, par, :], start=False, stop=True, skip_group_check=True).then_inc(s_df, 1)
                if g == NG - 2:
                    vectors()

            def turn_normed(l, g):
                n, par = NG * l + g + 1, g % 2
                pe.wait_ge(p_norm, n)
                if g >= 2:
                    pe.wait_ge(p_xT, n - 2)
                    if l == 0:
                        pe.wait_ge(p_nat, g - 1)
                elif l:
                    pe.wait_ge(m_hT, NG)
                for j in range(GB):
                    ins = tr(P[:, par, D * j:D * j + D], xn[:, par, j, :], ident)
                ins.then_inc(p_T, 1)

            def q_and_k(l, g):
                n, par = NG * l + g + 1, g % 2
                pe.wait_ge(p_xT, n)
                if g >= 2:
                    pe.wait_ge(p_qf, 4 * (n - 2))
                elif l:
                    pe.wait_ge(m_g, NF * NG)
                elif g == 1:
                    pe.wait_ge(s_stage, NG)
                for m in range(2):
                    mm(P[:, 2 + 2 * par + m, :], WQK[:, l, m, :], xT[:, par, :], start=True, stop=True).then_inc(p_q, 1)

            def project(l):
                if l == 0:
                    pe.wait_ge(ld_w, N_W)
                    pe.wait_ge(s_fTp, 3 * NG)
                    pe.wait_ge(s_U, NG)
                    turn_normed(0, 0)
                for g in range(NG):
                    n, par = NG * l + g + 1, g % 2
                    q_and_k(l, g)
                    if g + 1 < NG and (l == 0 or g):
                        turn_normed(l, g + 1)
                    if l == 0:
                        for j in range(GB):
                            ins = tr(P[:, par, D * j:D * j + D], xT[:, par, D * j:D * j + D], ident)
                        ins.then_inc(p_back, 1)
                    if g >= 2:
                        pe.wait_ge(p_v, n - 2)
                    elif l:
                        pe.wait_ge(m_t, NG - 1 + g)
                    elif g == 0:
                        pe.wait_ge(su_act, 8)
                    for j in range(GB):
                        ins = mm(P[:, 6 + par, D * j:D * j + D], xT[:, par, D * j:D * j + D], WV[:, l, :], start=True, stop=True)
                    ins.then_inc(p_q, 1)

            def attention(l):
                base = NU * l

                def scores(u, i, c, g, tokens):
                    if l or not isinstance(u, int) or u >= 2:
                        pe.wait_ge(a_add, u - 1)
                        if l and (not isinstance(i, int) or 4 * i + c >= 2):
                            pe.wait_ge(a_heads, u - 1 - NU)
                    b = 2 * i + c // 2
                    if c == 0:
                        pe.wait_ge(stacks_in, N_STACK * (NG * l + 1 + g))
                    for k in range(2):
                        bank = P[:, 2 * (c % 2) + k, :]
                        mask = CAUS[:, None, :] if l else MSK[:, ds(b, 1), :]
                        mm(bank, IDB[:, :], mask.to_broadcast([128, 4, S]), start=True, stop=False, skip_group_check=True)
                        for r in range(2):
                            pr = 4 * (c % 2) + 2 * k + r
                            ins = mm(bank[:, 256 * r:256 * r + 256],
                                     QS[:, ds(g, 1), pr, tokens].rearrange("p o t -> p (o t)"),
                                     KS[:, ds(g, 1), :, pr, tokens].rearrange("p o h t -> p (o h) t"),
                                     start=False, stop=(r == 1), skip_group_check=True)
                    ins.then_inc(a_qk, 1)

                def gs_dots(k, i, c):
                    if isinstance(k, int) and k == 0:
                        pe.wait_ge(ld_gs, N_GS)
                    else:
                        pe.wait_ge(gs_step, k)
                    backs = 2 * i + (c - 5) // 2
                    if l or not isinstance(i, int) or backs > 0:
                        pe.wait_ge(a_ctx, B * l + (max(backs, 0) if isinstance(i, int) else backs))
                    for m in range(2):
                        ins = mm(P[:, 7, 256 + R * m:256 + R * m + R], gsb[:, c // 2, m, 0:1].to_broadcast([128, 128]),
                                 gsb[:, c // 2, m, :], start=True, stop=True)
                    ins.then_inc(gs_dot, 1)

                def transposes(u, c):
                    pe.wait_ge(a_exp, u + 1)
                    if l or not isinstance(u, int) or u:
                        pe.wait_ge(a_pT, u)
                    for hh in range(HU):
                        ins = tr(P[:, 4 + hh // 4, S * (hh % 4):S * (hh % 4) + S], SE[:, c, hh, :], ident)
                    ins.then_inc(a_T, 1)

                def back(b, par):
                    n = B * l + b
                    pe.wait_ge(a_cs, n + 1)
                    if l or not isinstance(b, int) or b:
                        pe.wait_ge(a_ctx, n)
                    pe.wait_ge(gs_mask, GS * l + (min(b + 3, GS) if isinstance(b, int) else b + 3))
                    for m in range(2):
                        ins = tr(P[:, 7, S * m:S * m + S], cs[:, par, S * m:S * m + S], ident)
                    ins.then_inc(a_ct, 1)

                def pv(u, c, b):
                    pe.wait_ge(a_pT, u + 1)
                    if c % 2 == 0:
                        pe.wait_ge(a_vp, 2 * (B * l + b + 1))
                        if l or not isinstance(b, int) or b:
                            pe.wait_ge(a_cs, B * l + b)
                    for h2 in range(2):
                        for r in range(4):
                            hh = 2 * r + h2
                            ins = mm(P[32 * r:32 * r + 32, 6, S * (c % 2):S * (c % 2) + S],
                                     VP[:, (c // 2) % 2, HU * (c % 2) + hh, :], pT[:, c % 2, hh, :],
                                     start=(h2 == 0), stop=(h2 == 1), skip_group_check=True)
                    ins.then_inc(a_pv, 1)

                def slot(g, c8):
                    i, c = 2 * g + c8 // 4, c8 % 4
                    def live(lag):
                        return not isinstance(i, int) or 0 <= 4 * i + c - lag < NU

                    u = base + 4 * i + c
                    if live(0):
                        scores(u, i, c, g, slice(S * (c8 // 2), S * (c8 // 2) + S))
                    if live(3):
                        transposes(u - 3, (c + 1) % 4)
                    if c % 2 == 0 and live(6):
                        back(2 * i + c // 2 - 3, (c // 2 + 1) % 2)
                    if live(4):
                        pv(u - 4, c, 2 * i + c // 2 - 2)
                    if c % 2 and live(0):
                        gs_dots(GS * l + 2 * i + c // 2, i, c)

                for c8 in range(8):
                    slot(0, c8)
                with pe.Fori(1, NG) as g:
                    for c8 in range(8):
                        slot(g, c8)
                slot(NG, 0)
                pe.wait_ge(a_add, NU * (l + 1))
                if l:
                    pe.wait_ge(a_heads, NU)
                turn_context(l, 0)
                slot(NG, 1)
                turn_context(l, 1)
                out_projection(l, 0)
                slot(NG, 2)
                turn_context(l, 2)
                out_projection(l, 1)
                slot(NG, 3)
                out_projection(l, 2)
                slot(NG, 4)
                turn_context(l, 3)
                out_projection(l, 3)

            def turn_context(l, g):
                pe.wait_ge(a_ctx, B * l + GB * (g + 1))
                if g >= 2:
                    pe.wait_ge(o_cT, NG * l + g - 1)
                for j in range(GB):
                    ins = tr(P[:, g % 2, D * j:D * j + D], CTX[:, GB * g + j, :], ident)
                ins.then_inc(o_T, 1)

            def out_projection(l, g):
                par, n = g % 2, NG * l + g + 1
                pe.wait_ge(o_cT, n)
                if g >= 2:
                    pe.wait_ge(o_res, n - 2)
                for j in range(GB):
                    ins = mm(P[:, 2 + par, D * j:D * j + D], cT[:, par, D * j:D * j + D], WO[:, l, :], start=True, stop=True)
                ins.then_inc(o_wo, 1)

            def feed_forward(l):
                def turn(g):
                    n = NG * l + g + 1
                    pe.wait_ge(m_n, n)
                    if g >= 2:
                        pe.wait_ge(m_hT, n - 2)
                    if l and g == 3:
                        pe.wait_ge(rm_dve, 5)
                    for j in range(GB):
                        ins = tr(P[:, g % 2, D * j:D * j + D], cS[:, g % 2, j, :], ident)
                    ins.then_inc(m_T, 1)

                def up(g):
                    n = NG * l + g + 1
                    pe.wait_ge(m_hT, n)
                    for f in range(NF):
                        if g:
                            pe.wait_ge(m_g, NF * (n - 2) + f + 1)
                        elif f < 2:
                            pe.wait_ge(o_res, NG * l + 3 + f)
                        mm(P[:, 2 + f, :], W1[:, l, 128 * f:128 * f + 128], cT[:, g % 2, :], start=True, stop=True).then_inc(m_f, 1)

                def down(g, between=None):
                    n = NG * l + g + 1
                    pe.wait_ge(m_g, NF * n)
                    if g >= 2:
                        pe.wait_ge(m_t, n - 2)
                    for j in range(GB):
                        for f in range(NF):
                            ins = mm(P[:, 6 + g % 2, D * j:D * j + D], gT[:, g % 2, f, D * j:D * j + D], W2[:, l, f, :],
                                     start=(f == 0), stop=(f == NF - 1))
                        if between and j < GB - 1:
                            between(j)
                    ins.then_inc(m_y, 1)

                turn(0)
                turn(1)
                if l:
                    response_matrix(0)
                up(0)
                if l:
                    response_matrix(1)
                for g in range(1, NG):
                    up(g)
                    if l and g == 2:
                        response_matrix(4)

                    def between(j, g=g):
                        if j == 1:
                            if l and g == 1:
                                response_matrix(2)
                            if g + 1 < NG:
                                turn(g + 1)
                        if l and g == NG - 1 and j == 0:
                            turn_out(1)

                    if l and g == NG - 1:
                        turn_out(0)
                    down(g - 1, between)
                    if l and g == 1:
                        response_matrix(3)

                def last_between(j):
                    if j == 0:
                        gate2(0)
                    elif j == 1:
                        gate1(1)
                        response(1)
                    else:
                        gate2(1)
                        turn_out(2)

                if l:
                    gate1(0)
                    response(0)
                    down(NG - 1, last_between)
                    gate1(2)
                    response(2)
                    gate2(2)
                    turn_out(3)
                    gate1(3)
                    response(3)
                    gate2(3)
                else:
                    down(NG - 1, lambda j: turn_normed(1, j) if j < 2 else None)

            def response_matrix(k):
                if k == 0:
                    pe.wait_ge(gs_step, R)
                    pe.wait_ge(a_ctx, 2 * B)
                    for m in range(2):
                        tr(P[0:R, 7, 128 * m:128 * m + 128], gsb[:, 0, m, :], ident)
                    ins = tr(P[0:R, 7, 256:384], LR[:, :], ident)
                else:
                    pe.wait_ge(rm_dve, k)
                    if k == 1:
                        ins = mm(P[:, 7, 0:128], UT[0:R, 1, :], UT[0:R, 0, :], start=True, stop=True)
                    elif k == 2:
                        ins = mm(P[:, 7, 128:128 + R], BST, BST[:, 0:R], start=True, stop=True)
                    elif k == 3:
                        ins = tr(P[0:R, 7, 256:384], BBm, ident)
                    else:
                        pe.wait_ge(m_hT, NG + 2)
                        ins = mm(P[:, 1, 384:512], BBTt[:, :], RWT[:, :], start=True, stop=True)
                ins.then_inc(rm_pe, 1)

            def turn_out(g):
                pe.wait_ge(m_x, g + 1)
                pe.wait_ge(*((r_hT, g - 1) if g >= 2 else (m_hT, 2 * NG)))
                for j in range(GB):
                    ins = tr(P[:, g % 2, D * j:D * j + D], X[:, GB * g + j, :], ident)
                ins.then_inc(r_T, 1)

            def gate1(g):
                pe.wait_ge(r_hT, g + 1)
                pe.wait_ge(*((r_ba, g - 1) if g >= 2 else (m_g, 2 * NF * NG)))
                mm(P[0:R, 4 + g % 2, 8:8 + GB], W1T[:, :], pl[:, g % 2, 0:GB], start=True, stop=True).then_inc(r_g1, 1)

            def gate2(g):
                pe.wait_ge(r_h1, g + 1)
                mm(P[:, 4 + g % 2, 16:16 + GB], W2G[:, :].to_broadcast([R, 128]), pl[0:R, g % 2, 4:4 + GB], start=True, stop=True).then_inc(r_g2, 1)

            def response(g):
                par = g % 2
                pe.wait_ge(r_hT, g + 1)
                pe.wait_ge(rm_dve, 5)
                pe.wait_ge(*((r_t, g - 1) if g >= 2 else (m_g, 2 * NF * NG)))
                for j in range(GB):
                    ins = mm(P[:, 2 + par, D * j:D * j + D], cT[:, par, D * j:D * j + D], RM[:, :], start=True, stop=True)
                ins.then_inc(r_m, 1)

            for l in range(2):
                project(l)
                if l == 0:
                    pe.wait_ge(mask_set, 3)
                    pe.wait_ge(zeros_set, 4)
                pe.wait_ge(p_v, NG * (l + 1))
                pe.wait_ge(p_qf, 4 * NG * (l + 1))
                attention(l)
                feed_forward(l)

        @block.scalar
        def _(act):
            af = nc.scalar.activation
            act.wait_ge(ld_const, N_CONST)
            af(IDB[:, :], ident, ACT.Copy).then_inc(su_act, 1)
            act.wait_ge(su_dve, 1)
            af(EMB[:, 6, :], EMB[:, 5, :], ACT.Sin).then_inc(su_act, 1)
            act.wait_ge(su_act, 2)
            af(EMB[:, 7, :], EMB[:, 6, :], ACT.Silu).then_inc(su_dve, 1)
            act.wait_ge(ld_vec, N_VEC)
            af(VRT[:, :].rearrange("n (d h r) -> n h d r", h=2, d=DH),
               VRP[:, :].rearrange("n (r h d) -> n h d r", h=2, d=DH), ACT.Copy).then_inc(vrp_turned, 1)
            act.wait_ge(ld_w, N_W)
            for l in range(2):
                for m in range(2):
                    af(WQK[:, l, m, :].rearrange("k (d h r) -> k h d r", h=2, d=DH),
                       WQ0[:, l, m, :].rearrange("k (r h d) -> k h d r", h=2, d=DH), ACT.Copy).then_inc(su_act, 1)
            act.wait_ge(su_pe, 3)
            act.wait_ge(su_dve, 3)
            for m in range(2):
                af(ADA[:, m, :], P[:, 6, B * m:B * m + B], ACT.Identity, bias=COL[:, V_BADA + m:V_BADA + m + 1]).then_inc(su_act, 1)
            act.wait_ge(su_act, 8)

            def project(l):
                def evac(g):
                    n, par = NG * l + g + 1, g % 2
                    act.wait_ge(p_T, n)
                    if g >= 2:
                        act.wait_ge(p_q, 3 * (n - 2))
                    if l == 0:
                        for j in range(GB):
                            b = GB * g + j
                            ins = af(xT[:, par, D * j:D * j + D], P[:, par, D * j:D * j + D], ACT.Identity,
                                     bias=ADA[:, 1, b:b + 1], scale=ADA[:, 0, b:b + 1])
                    else:
                        ins = af(xT[:, par, :], P[:, par, :], ACT.Identity, bias=COL[:, V_BE1:V_BE1 + 1],
                                 scale=COL[:, V_GA1:V_GA1 + 1])
                    ins.then_inc(p_xT, 1)

                evac(0)
                for g in range(NG):
                    n, par = NG * l + g + 1, g % 2
                    if l and g == 0:
                        evac(1)
                    if n == 1:
                        act.wait_ge(s_stage, NG)
                    for m in range(2):
                        act.wait_ge(p_q, 3 * (n - 1) + m + 1)
                        if m == 0 and g >= 2:
                            act.wait_ge(p_q3, 2 * (n - 2))
                        for dst in (qf[:, par, m, :], parts_of(g)[:, m, 0, :]):
                            af(dst, P[:, 2 + 2 * par + m, :], ACT.Identity, bias=BQK[:, 2 * l + m:2 * l + m + 1],
                               scale=ISQ if m == 0 else 1.0).then_inc(p_qf, 1)
                    if g + 1 < NG and (l == 0 or g):
                        evac(g + 1)
                    for m in range(2):
                        act.wait_ge(p_r, 2 * (n - 1) + m + 1)
                        af(parts_of(g)[:, m, 1, :], qr[:, m, :], ACT.Copy).then_inc(p_q2, 1)

            def attention(l):
                base = NU * l

                def gs_norm_of(u):
                    act.wait_ge(gs_mask, u + 1)
                    af(gws[:, 2:4], gcm[:, :, 0], ACT.Ln).then_inc(gs_log, 1)
                    act.wait_ge(gs_log, u + 1)
                    af(gws[:, 0:2], gws[:, 2:4], ACT.Exp, scale=0.5).then_inc(gs_norm, 1)

                def exps(u, c):
                    act.wait_ge(a_add if l else a_sub, u + 1)
                    n = HU - HA if l else HU
                    af(SE[:, c, 0:n, :], SE[:, c, 0:n, :], ACT.Exp).then_inc(a_exp, 1)

                def heads(u, c):
                    act.wait_ge(a_half, u + 1 - NU)
                    for hh in range(HU - HA, HU):
                        ins = af(SE[:, c, hh, :], P[:, 2 * (c % 2) + 1, S * (hh - HU // 2):S * (hh - HU // 2 + 1)], ACT.Exp, bias=MX[:, c, hh:hh + 1])
                    ins.then_inc(a_heads, 1)

                def evac(u, c):
                    act.wait_ge(a_T, u + 1)
                    if l or not isinstance(u, int) or u >= 2:
                        act.wait_ge(a_pv, u - 1)
                    af(pT[:, c % 2, :, :].rearrange("p h k -> p (h k)"), P[:, 4:6, :].rearrange("p a k -> p (a k)"), ACT.Copy).then_inc(a_pT, 1)

                def context(b, par):
                    act.wait_ge(a_pv, base + 2 * b + 2)
                    af(cs[:, par, :], P[:, 6, 0:2 * S], ACT.Copy).then_inc(a_cs, 1)

                def slot(i, c):
                    def live(lag):
                        return not isinstance(i, int) or 0 <= 4 * i + c - lag < NU

                    u = base + 4 * i + c
                    if c % 2 == 0 and live(1):
                        gs_norm_of(GS * l + 2 * i + c // 2 - 1)
                    if l and live(1):
                        heads(u - 1, (c - 1) % 4)
                    if live(3):
                        evac(u - 3, (c - 3) % 4)
                    if live(1):
                        exps(u - 1, (c - 1) % 4)
                    if c % 2 and live(5):
                        context(2 * i + (c - 5) // 2, ((c - 5) // 2) % 2)

                act.preload_act_table_set("natural_log_exp_and_others")
                for k in range(8):
                    slot(k // 4, k % 4)
                with act.Fori(2, B // 2) as i:
                    for c in range(4):
                        slot(i, c)
                for k in range(NU, NU + 6):
                    slot(k // 4, k % 4)
                    if k < NU + 3:
                        out_projection(l, k - NU)
                out_projection(l, NG - 1)

            def out_projection(l, g):
                act.wait_ge(o_T, NG * l + g + 1)
                if g >= 2:
                    act.wait_ge(o_wo, NG * l + g - 1)
                af(cT[:, g % 2, :], P[:, g % 2, :], ACT.Copy).then_inc(o_cT, 1)

            def feed_forward(l):
                sc, bi, b1 = ((V_G2, V_BETA2, V_B1), (V_GA2, V_BE2, V_B1B))[l]

                def evac(g):
                    n = NG * l + g + 1
                    act.wait_ge(m_T, n)
                    if g >= 2:
                        act.wait_ge(m_f, NF * (n - 2))
                    af(cT[:, g % 2, :], P[:, g % 2, :], ACT.Identity, bias=COL[:, bi:bi + 1], scale=COL[:, sc:sc + 1]).then_inc(m_hT, 1)

                evac(0)
                evac(1)
                for g in range(NG):
                    n = NG * l + g + 1
                    for f in range(NF):
                        act.wait_ge(m_f, NF * (n - 1) + f + 1)
                        if g >= 2 and f == 0:
                            act.wait_ge(m_y, n - 2)
                        af(gT[:, g % 2, f, :], P[:, 2 + f, :], ACT.Gelu if l else ACT.Gelu_apprx_sigmoid,
                           bias=COL[:, b1 + f:b1 + f + 1]).then_inc(m_g, 1)
                    if 0 < g < NG - 1:
                        evac(g + 1)

            for l in range(2):
                project(l)
                attention(l)
                feed_forward(l)
            af(MOD[:, :], SAFE[:, :], ACT.Sigmoid).then_inc(su_act, 1)
            def evac(g):
                act.wait_ge(r_T, g + 1)
                if g >= 2:
                    act.wait_ge(r_m, g - 1)
                    act.wait_ge(r_g1, g - 1)
                for j in range(GB):
                    ins = af(cT[:, g % 2, D * j:D * j + D], P[:, g % 2, D * j:D * j + D], ACT.Copy, accum_out=pl[:, g % 2, j:j + 1])
                ins.then_inc(r_hT, 1)

            def hidden(g):
                act.wait_ge(r_g1, g + 1)
                if g >= 2:
                    act.wait_ge(r_g2, g - 1)
                af(pl[0:R, g % 2, 4:4 + GB], P[0:R, 4 + g % 2, 8:8 + GB], ACT.Relu, bias=GB1[:, 0:1], scale=1.0 / S).then_inc(r_h1, 1)

            def gate(g):
                act.wait_ge(r_g2, g + 1)
                if g >= 2:
                    act.wait_ge(r_st, g - 1)
                af(pl[:, g % 2, 8:8 + GB], P[:, 4 + g % 2, 16:16 + GB], ACT.Sigmoid, bias=GB2[:, 0:1]).then_inc(r_ba, 1)

            evac(0)
            evac(1)
            hidden(0)
            gate(0)
            hidden(1)
            gate(1)
            evac(2)
            hidden(2)
            gate(2)
            evac(3)
            hidden(3)
            gate(3)

        @block.vector
        def _(dve):
            v = nc.vector
            chain = [0]

            def link(ins):
                chain[0] += 1
                ins.then_inc(su_chain, 1)
                dve.wait_ge(su_chain, chain[0])

            dve.wait_ge(ld_const, N_CONST)
            link(v.tensor_copy(EMB[:, 0, :], TI))
            link(v.tensor_scalar(EMB[:, 1, :], EMB[:, 0, :], 40.0, None, ALU.mult))
            link(v.tensor_scalar(EMB[:, 2, :], EMB[:, 1, :], CST[:, C_FREQ:C_FREQ + 1], None, ALU.mult))
            link(v.tensor_scalar(EMB[:, 3, :], EMB[:, 2, :], float(1 / (2 * np.pi)), CST[:, C_QUART:C_QUART + 1], ALU.mult, ALU.add))
            link(v.tensor_scalar(EMB[:, 3, :], EMB[:, 3, :], 12582912.0, None, ALU.add))
            link(v.tensor_scalar(EMB[:, 3, :], EMB[:, 3, :], -12582912.0, None, ALU.add))
            c1 = 6.28125
            c2 = float(np.float32(2 * np.pi - c1))
            c3 = float(np.float32(2 * np.pi - c1 - float(np.float32(2 * np.pi - c1))))
            link(v.scalar_tensor_tensor(EMB[:, 4, :], EMB[:, 3, :], -c1, EMB[:, 2, :], ALU.mult, ALU.add))
            link(v.scalar_tensor_tensor(EMB[:, 4, :], EMB[:, 3, :], -c2, EMB[:, 4, :], ALU.mult, ALU.add))
            link(v.scalar_tensor_tensor(EMB[:, 4, :], EMB[:, 3, :], -c3, EMB[:, 4, :], ALU.mult, ALU.add))
            link(v.tensor_scalar(EMB[:, 4, :], EMB[:, 4, :], CST[:, C_PHASE:C_PHASE + 1], None, ALU.add))
            v.tensor_scalar(EMB[:, 5, :], EMB[:, 4, :], float(np.float32(3.1415925)), float(np.float32(-3.1415925)), ALU.min, ALU.max).then_inc(su_dve, 1)
            dve.wait_ge(su_pe, 1)
            link(v.tensor_copy(GRT[:, :, :], P[:, 5, 0:384].rearrange("p (m d) -> p m d", m=3)))

            def four(t):
                return t.rearrange("p (b y) -> p b y", b=GB)

            def stats(src, b):
                v.bn_stats(ST6[:, b, :], src[:, b, :]).then_inc(stats_done, 1)

            newton_at = [0]

            def rstd(k, half):
                def nl(ins):
                    newton_at[0] += 1
                    ins.then_inc(newton, 1)
                    dve.wait_ge(newton, newton_at[0])

                h = slice(half * B // 2, (half + 1) * B // 2)
                dve.wait_ge(stats_done, B * (k - 1) + (half + 1) * B // 2)
                me, mo, se, so = ST6[:, h, 1], ST6[:, h, 4], ST6[:, h, 2], ST6[:, h, 5]
                mean2, dev, r, x, g0, y = MV[:, h, 0], MV[:, h, 1], RS[:, h], NT[:, h], NI[:, h], NY[:, h]
                nl(v.tensor_tensor(dev, me, mo, ALU.subtract))
                nl(v.tensor_tensor(r, se, so, ALU.add))
                nl(v.scalar_tensor_tensor(dev, dev, 0.25, dev, ALU.mult, ALU.mult))
                nl(v.tensor_scalar(r, r, 1.0 / D, LN_EPS, ALU.mult, ALU.add))
                nl(v.tensor_tensor(x, r, dev, ALU.add))
                nl(v.tensor_scalar(g0, x.bitcast(I32), 1, None, ALU.arith_shift_right))
                nl(v.tensor_scalar(y.bitcast(I32), g0, -1.0, float(MAGIC), ALU.mult, ALU.add))
                nl(v.tensor_tensor(mean2, me, mo, ALU.add))
                for _ in range(3):
                    nl(v.tensor_tensor(r, y, y, ALU.mult))
                    nl(v.scalar_tensor_tensor(r, r, -0.5, x, ALU.mult, ALU.mult))
                    nl(v.scalar_tensor_tensor(y, r, 1.5, y, ALU.add, ALU.mult))
                nl(v.scalar_tensor_tensor(NMR[:, h], mean2, -0.5, y, ALU.mult, ALU.mult))

            def normed(dst, src, g, done):
                for j in range(GB):
                    b = GB * g + j
                    ins = v.tensor_scalar(dst[:, g % 2, j, :], src[:, b, :], NY[:, b:b + 1], NMR[:, b:b + 1], ALU.mult, ALU.add)
                ins.then_inc(done, 1)

            def vectors():
                dve.wait_ge(su_pe, 2)
                v.tensor_copy(W1T[:, :], P[:, 7, 0:R])
                v.tensor_copy(COL[:, :], P[:, 7, 64:64 + V_ALL]).then_inc(su_chain, 1)
                chain[0] += 1
                for m in range(2):
                    v.tensor_scalar(BQK[:, m:4:2], P[:, 7, 128 + m:132:2], 1.0 if m else ISQ, None, ALU.mult)
                dve.wait_ge(su_chain, chain[0])
                v.tensor_scalar(COL[:, V_BADA:V_BADA + 1], COL[:, V_BADA:V_BADA + 1], 1.0, None, ALU.add).then_inc(su_dve, 1)

            def stencil_products(g):
                par = g % 2
                dve.wait_ge(s_fT, g + 1)
                if g >= 2:
                    dve.wait_ge(s_df, g - 1)
                for m in (2, 0, 1):
                    v.tensor_tensor(four(fT[:, par, m, :]), four(P[:, par, :]), GRT[:, m:m + 1, :].to_broadcast([128, GB, D]), ALU.mult).then_inc(s_fTp, 1)

            def subtract_flux(g):
                par = g % 2
                dve.wait_ge(s_H, g + 1)
                dve.wait_ge(s_prod, 2 * g + 2)
                v.tensor_tensor(AF[:, par, :], AF[:, par, :], P[:, 2 + par, :], ALU.subtract).then_inc(s_U, 1)

            stencil_products(0)
            stencil_products(1)
            subtract_flux(0)
            for g in range(NG):
                par = g % 2
                if g == NG - 1:
                    vectors()
                    rstd(1, 0)
                    dve.wait_ge(s_df, NG - 1)
                    normed(xn, X, 0, p_norm)
                dve.wait_ge(s_df, g + 1)
                for j in range(GB):
                    b = GB * g + j
                    ins = v.scalar_tensor_tensor(X[:, b, :], P[:, 4 + par, D * j:D * j + D],
                                                 DTB[:, b:b + 1], fS[:, g, D * j:D * j + D], ALU.mult, ALU.add)
                ins.then_inc(s_stage, 1)
                if g + 1 < NG:
                    subtract_flux(g + 1)
                dve.wait_ge(s_stage, g + 1)
                v.tensor_scalar(X[:, GB * g:GB * g + GB, :], X[:, GB * g:GB * g + GB, :], 0.0, None, ALU.max).then_inc(s_x0, 1)
                dve.wait_ge(s_x0, g + 1)
                if g + 2 < NG:
                    stencil_products(g + 2)
                for j in range(GB):
                    stats(X, GB * g + j)

            def project(l):
                def later_norm(g):
                    dve.wait_ge(p_T, NG * l + g - 1)
                    normed(xn, X, g, p_norm)

                def natural(g):
                    dve.wait_ge(p_back, g + 1)
                    v.tensor_tensor(X[:, GB * g:GB * g + GB, :], four(P[:, g % 2, :]), BOB[:, 0:1, :].to_broadcast([128, GB, D]), ALU.add).then_inc(p_nat, 1)

                def rest(g):
                    for m in range(2):
                        dve.wait_ge(p_qf, 4 * (NG * l + g) + 2 * m + 2)
                        if l or g:
                            dve.wait_ge(p_q3, 2 * (NG * l + g - 1) + m + 1)
                        v.tensor_tensor(qr[:, m, :], qf[:, g % 2, m, :], parts_of(g)[:, m, 0, :], ALU.subtract).then_inc(p_r, 1)

                def third(g):
                    for m in range(2):
                        dve.wait_ge(p_q2, 2 * (NG * l + g) + m + 1)
                        v.tensor_tensor(parts_of(g)[:, m, 2, :], qr[:, m, :], parts_of(g)[:, m, 1, :], ALU.subtract).then_inc(p_q3, 1)

                def values(g):
                    dve.wait_ge(p_q, 3 * (NG * l + g + 1))
                    v.tensor_tensor(V[:, GB * g:GB * g + GB, :], four(P[:, 6 + g % 2, :]), BVB[:, l:l + 1, :].to_broadcast([128, GB, D]), ALU.add).then_inc(p_v, 1)

                if l == 0:
                    normed(xn, X, 1, p_norm)
                    rstd(1, 1)
                    rest(0)
                    dve.wait_ge(ld_row, N_ROW)
                    natural(0)
                    third(0)
                    later_norm(2)
                else:
                    rstd(3, 1)
                    rest(0)
                    later_norm(2)
                    third(0)
                later_norm(3)
                if l == 0:
                    dve.wait_ge(mask_set, 3)
                    dve.wait_ge(su_act, 8)
                values(0)
                for g in range(1, NG):
                    if l == 0:
                        natural(g)
                    rest(g)
                    values(g)
                    third(g)

            def attention(l):
                base = NU * l

                def gs_copy(k, i, c):
                    dve.wait_ge(gs_dot, k + 1)
                    v.tensor_tensor(gcm[:, :, :], P[:, 7, 256:256 + 2 * R].rearrange("p (m c) -> p m c", m=2),
                                    CST[:, None, ds(C_GSM + k, R)].to_broadcast([128, 2, R]), ALU.mult).then_inc(gs_mask, 1)

                def gs_scale(k, step):
                    if step == 0:
                        dve.wait_ge(gs_norm, k + 1)
                        v.tensor_scalar(gws[:, 4:6], gws[:, 0:2], GS_EPS, None, ALU.add).then_inc(gs_chain, 1)
                    elif step == 1:
                        dve.wait_ge(gs_chain, k + 1)
                        v.reciprocal(gws[:, 6:8], gws[:, 4:6]).then_inc(gs_inv, 1)
                    else:
                        dve.wait_ge(gs_inv, 2 * k + 1)
                        v.tensor_tensor(gws[:, 8:10], gws[:, 6:8], gws[:, 6:8], ALU.mult).then_inc(gs_inv, 1)

                def slot(i, c):
                    def live(lag):
                        return not isinstance(i, int) or 0 <= 4 * i + c - lag < NU

                    u = base + 4 * i + c
                    k = GS * l + 2 * i + c // 2
                    ps = P[:, 2 * (c % 2):2 * (c % 2) + 2, :].rearrange("p a (h k) -> p (a h) k", k=S)
                    if live(0):
                        dve.wait_ge(a_qk, u + 1)
                        if l or not isinstance(u, int) or u >= 4:
                            dve.wait_ge(a_T, u - 3)
                        if l == 0:
                            if isinstance(i, int) and 4 * i + c in (4, 5):
                                dve.wait_ge(fs_landed[4], 64)
                                bias = FS2[:, c, :, :]
                            else:
                                dve.wait_ge(fs_landed[c], 32 * (i + 1 if c >= 2 or isinstance(i, int) and i == 0 else i))
                                bias = FS[:, c, :, :]
                            v.tensor_tensor(SE[:, c, :, :], ps, bias, ALU.add).then_inc(a_add, 1)
                        else:
                            v.tensor_reduce(MX[:, c, :], ps, AX.X, ALU.max, negate=True).then_inc(a_max, 1)
                    if c % 2 == 0 and live(1):
                        gs_scale(k - 1, 0)
                    if live(0):
                        if l == 0:
                            dve.wait_ge(a_add, u + 1)
                            v.tensor_reduce(MX[:, c, :], SE[:, c, :, :], AX.X, ALU.max).then_inc(a_max, 1)
                        else:
                            dve.wait_ge(a_max, u + 1)
                            for heads, done in ((slice(HU // 2, HU - HA), a_half), (slice(0, HU // 2), a_add)):
                                v.tensor_tensor(SE[:, c, heads, :], ps[:, heads, :],
                                                MX[:, c, heads, None].to_broadcast([128, heads.stop - heads.start, S]), ALU.add).then_inc(done, 1)
                    if c % 2 == 0 and live(1):
                        gs_scale(k - 1, 1)
                    if c % 2 == 0 and live(6):
                        row_sums(2 * i + c // 2 - 3)
                    if c % 2 == 0 and live(1):
                        gs_scale(k - 1, 2)
                    if c % 2 == 0 and live(6):
                        context(2 * i + c // 2 - 3)
                    if c % 2 and live(0):
                        gs_copy(k, i, c)

                ct = P[:, 7, 0:2 * S].rearrange("p (h e) -> p h e", h=H)

                def row_sums(b):
                    dve.wait_ge(a_ct, B * l + b + 1)
                    v.reciprocal(RSUM[:, :], ct[:, :, DH]).then_inc(a_rs, 1)

                def context(b):
                    dve.wait_ge(a_rs, B * l + b + 1)
                    dst = CTX[:, b, :] if isinstance(b, int) else CTX[:, ds(b, 1), :].rearrange("p o d -> p (o d)")
                    v.tensor_tensor(dst.rearrange("p (h d) -> p h d", h=H), ct[:, :, 0:DH],
                                    RSUM[:, :, None].to_broadcast([128, H, DH]), ALU.mult).then_inc(a_ctx, 1)

                for k in range(8):
                    slot(k // 4, k % 4)
                with dve.Fori(2, B // 2) as i:
                    for c in range(4):
                        slot(i, c)
                x1 = V if l else X
                slot(NU // 4, 0)
                if l:
                    dve.wait_ge(a_vp, 2 * B * 2)
                slot(NU // 4, 1)
                out_projection(l, 0)
                slot(NU // 4, 2)
                out_projection(l, 1)
                slot(NU // 4, 3)
                slot(NU // 4 + 1, 0)
                dve.wait_ge(p_norm, NG * (l + 1))
                rstd(2 * l + 2, 0)
                normed(cS, x1, 0, m_n)
                normed(cS, x1, 1, m_n)
                out_projection(l, 2)
                out_projection(l, 3)

            def out_projection(l, g):
                par, n = g % 2, NG * l + g + 1
                grp = slice(GB * g, GB * g + GB)
                dve.wait_ge(o_wo, n)
                ps = four(P[:, 2 + par, :])
                if l == 0:
                    v.tensor_tensor(X[:, grp, :], ps, X[:, grp, :], ALU.add).then_inc(o_res, 1)
                else:
                    dve.wait_ge(x_bo, g + 1)
                    v.tensor_tensor(V[:, grp, :], ps, XBO[:, grp, :], ALU.add).then_inc(o_res, 1)
                dve.wait_ge(o_res, n)
                for j in range(GB):
                    stats(V if l else X, GB * g + j)

            def feed_forward(l):
                x1 = V if l else X
                if l:
                    response_matrix(0)
                rstd(2 * l + 2, 1)
                if l:
                    response_matrix(1)
                for g in range(2, NG):
                    dve.wait_ge(m_T, NG * l + g - 1)
                    normed(cS, x1, g, m_n)
                if l:
                    response_matrix(2)
                for g in range(NG):
                    par, n = g % 2, NG * l + g + 1
                    grp = slice(GB * g, GB * g + GB)
                    dve.wait_ge(m_y, n)
                    dve.wait_ge(x_b2, n)
                    if l == 0:
                        v.tensor_tensor(X[:, grp, :], four(P[:, 6 + par, :]), X[:, grp, :], ALU.add).then_inc(m_t, 1)
                        dve.wait_ge(m_t, n)
                        for j in range(GB):
                            stats(X, GB * g + j)
                        if g == 1:
                            dve.wait_ge(m_n, NG)
                            rstd(3, 0)
                            dve.wait_ge(m_T, NG)
                            normed(xn, X, 0, p_norm)
                            normed(xn, X, 1, p_norm)
                    else:
                        v.tensor_tensor(yS[:, par, :, :], four(P[:, 6 + par, :]), V[:, grp, :], ALU.add).then_inc(m_t, 1)
                        dve.wait_ge(m_t, n)
                        for j in range(GB):
                            b = GB * g + j
                            ins = v.scalar_tensor_tensor(X[:, b, :], yS[:, par, j, :], GATE[:, b:b + 1], X[:, b, :], ALU.mult, ALU.add)
                        ins.then_inc(m_x, 1)
                        if g == 0:
                            response_matrix(3)
                            response_matrix(4)
                            link(v.tensor_tensor(CB[:, 0, :], CB[:, 0, :], CB[:, 1, :], ALU.add))
                        elif g == 2:
                            response(0)
                            response(1)
                        elif g == 3:
                            response(2)
                            response(3)

            def response_matrix(k):
                dve.wait_ge(rm_pe, k + 1)
                if k == 0:
                    v.tensor_copy(RWT[:, :], P[0:R, 7, 256:384])
                dst, ps = ((UT[0:R, :, :], P[0:R, 7, 0:256].rearrange("p (m d) -> p m d", m=2)), (BST, P[:, 7, 0:128]),
                           (BBm, P[:, 7, 128:128 + R]), (BBTt[:, :], P[0:R, 7, 256:384]), (RM[:, :], P[:, 1, 384:512]))[k]
                v.tensor_copy(dst, ps).then_inc(rm_dve, 1)

            def response(g):
                par, n = g % 2, g + 1
                if g >= 2:
                    dve.wait_ge(r_out, 16 * (g - 1))
                dve.wait_ge(r_m, n)
                v.tensor_tensor(zS[:, par, :, :], four(P[:, 2 + par, :]), CB[:, 0:1, :].to_broadcast([128, GB, D]), ALU.add).then_inc(r_t, 1)
                dve.wait_ge(r_ba, n)
                dve.wait_ge(su_act, 9)
                v.tensor_tensor(pl[:, par, 12:12 + GB], pl[:, par, 8:8 + GB], MOD[:, GB * g:GB * g + GB], ALU.mult).then_inc(r_st, 1)
                dve.wait_ge(r_t, n)
                dve.wait_ge(r_st, n)
                for j in range(GB):
                    ins = v.scalar_tensor_tensor(zS[:, par, j, :], zS[:, par, j, :], pl[:, par, 12 + j:13 + j], X[:, GB * g + j, :], ALU.mult, ALU.add)
                ins.then_inc(r_o, 1)

            for l in range(2):
                project(l)
                dve.wait_ge(p_q3, 2 * NG * (l + 1))
                attention(l)
                feed_forward(l)



_INS = ['x', 'condB_dt', 'itok_B_34_63', 'fside_Bx16xSxS_0', 'condB_gatescore', 'condB_safetyscore', 'mask_Bx1xSxS_bk0',
        'L0_cond_A_grid', 'L0_cond_B_grid'] + \
       ['L1_cond_' + n for n in ('W_ada', 'b_ada', 'Wq', 'bq', 'Wk', 'bk', 'Wv', 'bv', 'Wo', 'bo', 'W1', 'b1', 'W2', 'b2', 'g2', 'beta2')] + \
       ['L2_cond_' + n for n in ('Wq', 'bq', 'Wk', 'bk', 'Wv', 'bv', 'Wo', 'bo', 'W1', 'b1', 'W2', 'b2', 'gamma1', 'beta1', 'gamma2', 'beta2')] + \
       ['L3_cond_' + n for n in ('U', 'V', 'safety_bias', 'gate_w1', 'gate_b1', 'gate_w2', 'gate_b2', 'resp_w', 'resp_b')]


def kernel(**inputs):
    import numpy as _np
    import concourse.bacc as _bacc
    from concourse import mybir as _mybir
    from concourse.bass_utils import run_bass_kernel_spmd as _run

    nc = _bacc.Bacc("TRN2", target_bir_lowering=False, num_devices=1)
    arrays, args = {}, {}
    host = {name: _np.ascontiguousarray(inputs[name]) for name in _INS}
    host["mask_Bx1xSxS_bk0"] = host["mask_Bx1xSxS_bk0"].view(_np.int32)
    host["consts"] = constants()
    for name, arr in host.items():
        arrays[f"in_{name}"] = arr
        args[name] = nc.dram_tensor(f"in_{name}", arr.shape, _mybir.dt.from_np(arr.dtype), kind="ExternalInput").ap()
    out = nc.dram_tensor("out_0", (B, S, D), F32, kind="ExternalOutput").ap()
    build(nc, args, out)
    r = _run(nc, [arrays], core_ids=[0])
    return r.results[0]["out_0"]
```
